# Optimizing a Trainium2 kernel written in Bass

```python
import numpy as np
import jax
import jax.numpy as jnp

def _softmax(x, axis=-1):
    return jax.nn.softmax(x, axis=axis)

def _gelu(x):
    return jax.nn.gelu(x, approximate=True)

def _silu(x):
    return jax.nn.silu(x)

def _sigmoid(x):
    return jax.nn.sigmoid(x)

def _layernorm(x, axis=-1, eps=1e-05):
    m = jnp.mean(x, axis=axis, keepdims=True)
    v = jnp.var(x, axis=axis, keepdims=True)
    return (x - m) / jnp.sqrt(v + eps)

def _scatter_add(tgt, idx, src, axis=0):
    return tgt.at[idx].add(src)

def _segment_sum(src, seg, n):
    return jax.ops.segment_sum(src, seg, n)
kernel_name = 'mk_xattn_ffn_d2_seqx_r8_2cc354'

def setup_inputs(seed: int=0):
    np.random.seed(seed)
    _w = jnp.asarray

    def _rec_inputs():
        import jax
        import jax.numpy as jnp
        _rk = jax.random.key(seed)
        x = -0.0003929 + 0.9999 * jax.random.normal(jax.random.fold_in(_rk, 1), (2, 512, 128), jnp.float32)
        _lenS = 512 - jax.random.randint(jax.random.fold_in(_rk, 7), (2,), 0, max(1, 512 // 4) + 1, jnp.int32)
        _lenS2 = 77 - jax.random.randint(jax.random.fold_in(_rk, 8), (2,), 0, max(1, 77 // 4) + 1, jnp.int32)
        _ctx_1024P = jax.random.normal(jax.random.fold_in(_rk, 11), (2, 16, 128), jnp.float32)
        _ctx_1024c = jax.random.dirichlet(jax.random.fold_in(_rk, 511), 0.3 * jnp.ones((16,), jnp.float32), (2, 77))
        _ctx_1024t = jnp.einsum('bsk,bkd->bsd', _ctx_1024c, _ctx_1024P)
        _ctx_1024t = _ctx_1024t * jax.lax.rsqrt(jnp.mean(jnp.square(_ctx_1024t)) + 1e-12) * 0.953939
        ctx_1024 = 2.81802e-05 + 1.00001 * (_ctx_1024t + 0.3 * jax.random.normal(jax.random.fold_in(_rk, 611), (2, 77, 128), jnp.float32))
        return (x, ctx_1024)
    x, ctx_1024 = _rec_inputs()

    def _L0_xattn_setup():
        import jax, jax.numpy as jnp
        import numpy as np
        D_MODEL = 128
        NUM_HEADS = 16
        FOCUS = 3
        EPS = 1e-06

        def _focused_feature_map(x, scale):
            x = jax.nn.relu(x) + EPS
            x = x / scale
            x_norm = jnp.linalg.norm(x, axis=-1, keepdims=True)
            xp = x ** FOCUS
            return xp / jnp.linalg.norm(xp, axis=-1, keepdims=True) * x_norm
        key = jax.random.key(seed)
        ks = jax.random.split(key, 10)
        b, n, d = (4, 512, D_MODEL)
        s = 0.02
        return {'input_q': jax.random.normal(ks[0], (b, n, d), jnp.float32), 'input_k': jax.random.normal(ks[1], (b, n, d), jnp.float32), 'input_v': jax.random.normal(ks[2], (b, n, d), jnp.float32), 'Wq': jax.random.normal(ks[3], (d, d), jnp.float32) * s, 'bq': jnp.zeros((d,), jnp.float32), 'Wk': jax.random.normal(ks[4], (d, d), jnp.float32) * s, 'bk': jnp.zeros((d,), jnp.float32), 'Wv': jax.random.normal(ks[5], (d, d), jnp.float32) * s, 'bv': jnp.zeros((d,), jnp.float32), 'scale': jnp.zeros((1, 1, d), jnp.float32)}
    _L0_xattn_all = _L0_xattn_setup()
    _L0_xattn_in = {k: v for k, v in _L0_xattn_all.items() if k in ('Wq', 'bq', 'Wk', 'bk', 'Wv', 'bv', 'scale')}
    del _L0_xattn_all

    def _L0_ffn_setup():
        import jax, jax.numpy as jnp
        import numpy as np
        B, T, C = (4, 256, 128)
        E, F, K = (8, 256, 2)
        key = jax.random.key(seed)
        k0, k1, k2, k3 = jax.random.split(key, 4)
        s = lambda d: 1.0 / np.sqrt(d)
        x = jax.random.normal(k0, (B, T, C), dtype=jnp.float32)
        Wr = jax.random.normal(k1, (E, C), dtype=jnp.float32) * s(C)
        W1 = jax.random.normal(k2, (E, 2 * F, C), dtype=jnp.float32) * s(C)
        W2 = jax.random.normal(k3, (E, C, F), dtype=jnp.float32) * s(F)
        return {'x': x, 'Wr': Wr, 'W1': W1, 'W2': W2}
    _L0_ffn_all = _L0_ffn_setup()
    _L0_ffn_in = {k: v for k, v in _L0_ffn_all.items() if k in ('Wr', 'W1', 'W2')}
    del _L0_ffn_all

    def _L1_xattn_setup():
        import jax, jax.numpy as jnp
        import numpy as np
        EMBED_DIM = 128
        B, QL, KL = (4, 256, 256)
        key = jax.random.key(seed)
        k1, k2, k3, k4 = jax.random.split(key, 4)
        hidden_states = jax.random.normal(k1, (B, QL, EMBED_DIM), dtype=jnp.float32)
        decoder_hidden_states = jax.random.normal(k2, (B, KL, EMBED_DIM), dtype=jnp.float32)
        Wq = jax.random.normal(k3, (EMBED_DIM, EMBED_DIM), dtype=jnp.float32) * (1.0 / np.sqrt(EMBED_DIM))
        Wkv = jax.random.normal(k4, (EMBED_DIM, 2 * EMBED_DIM), dtype=jnp.float32) * (1.0 / np.sqrt(EMBED_DIM))
        return {'hidden_states': hidden_states, 'decoder_hidden_states': decoder_hidden_states, 'Wq': Wq, 'Wkv': Wkv}
    _L1_xattn_all = _L1_xattn_setup()
    _L1_xattn_in = {k: v for k, v in _L1_xattn_all.items() if k in ('Wq', 'Wkv')}
    del _L1_xattn_all

    def _L1_ffn_setup():
        import jax, jax.numpy as jnp
        import numpy as np
        EMB = 128
        FF = 4 * EMB

        def _ternary(w):
            scale = jnp.maximum(jnp.mean(jnp.abs(w)), 1e-08)
            w_t = jnp.clip(jnp.round(w / scale), -1.0, 1.0)
            return w + jax.lax.stop_gradient(w_t - w)
        key = jax.random.key(seed)
        kx, k1, k2, kb1, kb2 = jax.random.split(key, 5)
        x = jax.random.normal(kx, (4, 256, EMB), dtype=jnp.float32)
        lim1 = 1.0 / np.sqrt(EMB)
        lim2 = 1.0 / np.sqrt(FF)
        W1 = jax.random.uniform(k1, (FF, EMB), jnp.float32, -lim1, lim1)
        b1 = jax.random.uniform(kb1, (FF,), jnp.float32, -lim1, lim1)
        W2 = jax.random.uniform(k2, (EMB, FF), jnp.float32, -lim2, lim2)
        b2 = jax.random.uniform(kb2, (EMB,), jnp.float32, -lim2, lim2)
        return {'x': x, 'W1': W1, 'b1': b1, 'W2': W2, 'b2': b2}
    _L1_ffn_all = _L1_ffn_setup()
    _L1_ffn_in = {k: v for k, v in _L1_ffn_all.items() if k in ('W1', 'b1', 'W2', 'b2')}
    del _L1_ffn_all
    return {'x': x, 'ctx_1024': ctx_1024, 'L0_xattn_Wq': _L0_xattn_in['Wq'], 'L0_xattn_bq': _L0_xattn_in['bq'], 'L0_xattn_Wk': _L0_xattn_in['Wk'], 'L0_xattn_bk': _L0_xattn_in['bk'], 'L0_xattn_Wv': _L0_xattn_in['Wv'], 'L0_xattn_bv': _L0_xattn_in['bv'], 'L0_xattn_scale': _L0_xattn_in['scale'], 'L0_ffn_Wr': _L0_ffn_in['Wr'], 'L0_ffn_W1': _L0_ffn_in['W1'], 'L0_ffn_W2': _L0_ffn_in['W2'], 'L1_xattn_Wq': _L1_xattn_in['Wq'], 'L1_xattn_Wkv': _L1_xattn_in['Wkv'], 'L1_ffn_W1': _L1_ffn_in['W1'], 'L1_ffn_b1': _L1_ffn_in['b1'], 'L1_ffn_W2': _L1_ffn_in['W2'], 'L1_ffn_b2': _L1_ffn_in['b2']}

def reference(x, ctx_1024, L0_xattn_Wq, L0_xattn_bq, L0_xattn_Wk, L0_xattn_bk, L0_xattn_Wv, L0_xattn_bv, L0_xattn_scale, L0_ffn_Wr, L0_ffn_W1, L0_ffn_W2, L1_xattn_Wq, L1_xattn_Wkv, L1_ffn_W1, L1_ffn_b1, L1_ffn_W2, L1_ffn_b2):
    import jax
    import jax.numpy as jnp

    def _L0_xattn_ref(input_q, input_k, input_v, Wq, bq, Wk, bk, Wv, bv, scale):
        import jax, jax.numpy as jnp
        import numpy as np
        D_MODEL = 128
        NUM_HEADS = 16
        FOCUS = 3
        EPS = 1e-06

        def _focused_feature_map(x, scale):
            x = jax.nn.relu(x) + EPS
            x = x / scale
            x_norm = jnp.linalg.norm(x, axis=-1, keepdims=True)
            xp = x ** FOCUS
            return xp / jnp.linalg.norm(xp, axis=-1, keepdims=True) * x_norm
        b, n_q, d = input_q.shape
        h = NUM_HEADS
        c = d // h
        q = input_q @ Wq + bq
        k = input_k @ Wk + bk
        v = input_v @ Wv + bv
        sp = jax.nn.softplus(scale)
        q = _focused_feature_map(q, sp)
        k = _focused_feature_map(k, sp)
        q = q.reshape(b, n_q, h, c).transpose(0, 2, 1, 3)
        k = k.reshape(b, -1, h, c).transpose(0, 2, 1, 3)
        v = v.reshape(b, -1, h, c).transpose(0, 2, 1, 3)
        z = 1.0 / (jnp.einsum('bhic,bhc->bhi', q, k.sum(axis=2)) + EPS)
        kv = jnp.einsum('bhjc,bhjd->bhcd', k, v)
        x = jnp.einsum('bhic,bhcd->bhid', q, kv) * z[..., None]
        return x.transpose(0, 2, 1, 3).reshape(b, n_q, d)

    def _L0_ffn_ref(x, Wr, W1, W2):
        import jax, jax.numpy as jnp
        import numpy as np
        B, T, C = (4, 256, 128)
        E, F, K = (8, 256, 2)
        Bb, Tt, Cc = x.shape
        flat = x.reshape(-1, Cc)
        N = flat.shape[0]
        logits = flat @ Wr.T
        weights, ids = jax.lax.top_k(logits, K)
        weights = jax.nn.softmax(weights, axis=-1)
        rows = jnp.arange(N)[:, None]
        router_weights = jnp.zeros((N, E), dtype=flat.dtype).at[rows, ids].add(weights)
        h = jnp.einsum('nc,efc->nef', flat, W1)
        val, gate = (h[..., :F], h[..., F:])
        act = val * jax.nn.silu(gate)
        expert_outputs = jnp.einsum('nef,ecf->nec', act, W2)
        out = jnp.einsum('nec,ne->nc', expert_outputs, router_weights)
        return out.reshape(Bb, Tt, Cc)

    def _L1_xattn_ref(hidden_states, decoder_hidden_states, Wq, Wkv):
        import jax, jax.numpy as jnp
        import numpy as np
        EMBED_DIM = 128
        B, QL, KL = (4, 256, 256)
        d = Wq.shape[0]
        scale = 1.0 / np.sqrt(d)
        query = hidden_states @ Wq
        kv = decoder_hidden_states @ Wkv
        key, value = jnp.split(kv, 2, axis=-1)
        scores = jnp.einsum('bqd,bkd->bqk', query, key) * scale
        w = jax.nn.softmax(scores, axis=-1)
        return jnp.einsum('bqk,bkd->bqd', w, value)

    def _L1_ffn_ref(x, W1, b1, W2, b2):
        import jax, jax.numpy as jnp
        import numpy as np
        EMB = 128
        FF = 4 * EMB

        def _ternary(w):
            scale = jnp.maximum(jnp.mean(jnp.abs(w)), 1e-08)
            w_t = jnp.clip(jnp.round(w / scale), -1.0, 1.0)
            return w + jax.lax.stop_gradient(w_t - w)
        h = jnp.einsum('bsd,fd->bsf', x, _ternary(W1)) + b1
        h = jax.nn.gelu(h, approximate=False)
        out = jnp.einsum('bsf,df->bsd', h, _ternary(W2)) + b2
        return out
    x = x + _L0_xattn_ref(_layernorm(x, axis=-1), ctx_1024, ctx_1024, L0_xattn_Wq, L0_xattn_bq, L0_xattn_Wk, L0_xattn_bk, L0_xattn_Wv, L0_xattn_bv, L0_xattn_scale)
    x = x + _L0_ffn_ref(_layernorm(x, axis=-1), L0_ffn_Wr, L0_ffn_W1, L0_ffn_W2)
    x = x + _L1_xattn_ref(_layernorm(x, axis=-1), ctx_1024, L1_xattn_Wq, L1_xattn_Wkv)
    x = x + _L1_ffn_ref(_layernorm(x, axis=-1), L1_ffn_W1, L1_ffn_b1, L1_ffn_W2, L1_ffn_b2)
    return x

_drawn_inputs = setup_inputs


def setup_inputs(seed=0):
    import zlib

    import numpy as np

    out = dict(_drawn_inputs(seed))
    spreads = {'L0_xattn_bq': (0.0, 0.1),
     'L0_xattn_bk': (0.0, 0.1),
     'L0_xattn_bv': (0.0, 0.1),
     'L0_xattn_scale': (0.0, 0.1)}
    factors = {'L1_ffn_b1': 8.0, 'L1_ffn_b2': 200.0}
    for name, (base, spread) in spreads.items():
        noise = np.random.default_rng([zlib.crc32(name.encode()), seed]).standard_normal(out[name].shape)
        drawn = base * np.exp(spread * noise) if base else spread * noise
        out[name] = jnp.asarray(drawn.astype(out[name].dtype))
    for name, factor in factors.items():
        out[name] = (out[name] * factor).astype(out[name].dtype)
    return out
```

```python
import concourse.bass as bass
from concourse import mybir
from contextlib import ExitStack
import numpy as np

P = 128
B, N_TOK, C = 2, 512, 128
CTX = 77
HEADS = 16
HEAD_DIM = C // HEADS
EXPERTS, FFN = 8, 256
TILES = N_TOK // P
CHUNKS_PER_EXPERT = FFN // P
CHUNKS = EXPERTS * CHUNKS_PER_EXPERT
FF1 = 4 * C
FF1_CHUNKS = FF1 // P
KV_COLS = C + HEADS
W2_LAG = 3
RAW = 4
FOCUS_EPS = 1e-6
LN_EPS = 1e-5

PACK = {}
_at = 0
for _name, _width in (("ctxT", B * CTX), ("Wkv0", 2 * C), ("Wq0", C), ("scale_bq", 2), ("ident", C),
                      ("Wkv1", 2 * C), ("Wq1T", C), ("WrT", EXPERTS), ("b1", FF1_CHUNKS), ("b2", 1),
                      ("kv_mask", KV_COLS), ("iota", EXPERTS)):
    PACK[_name] = (_at, _at + _width)
    _at += _width
PACK_COLS = _at
ROW_COLS = 2 * 2 * C + C


def build(nc, x, pack, rows, w1, w2, ternary_w, out):
    f32, f32r, u32 = mybir.dt.float32, mybir.dt.float32r, mybir.dt.uint32
    ALU, ACT, AX = mybir.AluOpType, mybir.ActivationFunctionType, mybir.AxisListType
    ctx = ExitStack()
    with ctx:
        def sb(name, shape, dt=f32):
            return ctx.enter_context(nc.sbuf_tensor(name, shape, dt))

        def sem(name):
            return ctx.enter_context(nc.semaphore(name))

        def bank(name):
            return ctx.enter_context(nc.psum_tensor(name, [P, 512], f32))

        def per_half(name, shape, dt=f32):
            return [sb(f"{name}_{h}", shape, dt) for h in range(B)]

        small = sb("small", [P, PACK_COLS])
        row_sb = sb("row_sb", [1, ROW_COLS])
        w1_raw = sb("w1_raw", [P, RAW, 2 * FFN])
        w2_raw = sb("w2_raw", [P, RAW, CHUNKS_PER_EXPERT, C])
        tw_raw = sb("tw_raw", [P, 2, FF1])
        x_in = per_half("x_in", [P, TILES, C])

        def packed(name):
            a, b = PACK[name]
            return small[:, a:b]

        ctxT, ident = packed("ctxT"), packed("ident")

        w1_hi = sb("w1_hi", [P, EXPERTS, 2 * FFN], f32r)
        w1_lo = sb("w1_lo", [P, EXPERTS, 2 * FFN], f32r)
        w2_hi = sb("w2_hi", [P, EXPERTS, CHUNKS_PER_EXPERT, C], f32r)
        w2_lo = sb("w2_lo", [P, EXPERTS, CHUNKS_PER_EXPERT, C], f32r)
        below = sb("below", [P, FF1])
        tern = sb("tern", [P, 2, FF1], f32r)
        select = sb("select", [2 * EXPERTS, EXPERTS, P], f32r)
        ones = sb("ones", [P, P])
        half_power = sb("half_power", [P, 4])
        neg_half_power = sb("neg_half_power", [P, 4])
        abs_sum = sb("abs_sum", [P, 2])
        t_scale = sb("t_scale", [P, 2])
        t_hi = sb("t_hi", [P, 2])
        t_lo = sb("t_lo", [P, 2])

        sp_in = sb("sp_in", [P, C + 1])
        sp_abs = sb("sp_abs", [P, C + 1])
        sp_exp = sb("sp_exp", [P, C + 1])
        sp_ln = sb("sp_ln", [P, C + 1])
        sp = sb("sp", [P, C + 1])
        inv_sp = sb("inv_sp", [P, C + 1])
        eps_inv_sp = sb("eps_inv_sp", [P, 1])
        bq_inv_sp = sb("bq_inv_sp", [P, 1])
        k_act = sb("k_act", [CTX, B, C])
        k_div = sb("k_div", [CTX, B, C])
        k_sq = sb("k_sq", [CTX, B, C])
        k_cube = sb("k_cube", [CTX, B, C])
        k_six = sb("k_six", [CTX, B, C])
        k_sums = sb("k_sums", [CTX, 2, B])
        k_rec = sb("k_rec", [CTX, B])
        k_ratio = sb("k_ratio", [CTX, B])
        k_factor = sb("k_factor", [CTX, B])
        k_feat = sb("k_feat", [CTX, B, C])
        v_ones = sb("v_ones", [CTX, B, KV_COLS])
        kv_heads = sb("kv_heads", [P, B, KV_COLS])
        k1T = sb("k1T", [P, B * CTX])
        wq_k1T = sb("wq_k1T", [P, B * CTX])
        v1 = sb("v1", [CTX, B, C])

        LN = range(8)
        ln_stats = [sb(f"ln_stats_{i}", [P, TILES, 6]) for i in LN]
        ln_mv = [sb(f"ln_mv_{i}", [P, TILES, 2]) for i in LN]
        ln_var = [sb(f"ln_var_{i}", [P, TILES]) for i in LN]
        ln_rstd = [sb(f"ln_rstd_{i}", [P, TILES]) for i in LN]
        ln_out = [sb(f"ln_out_{i}", [P, TILES, C]) for i in range(2)] * 4
        xn1T = per_half("xn1T", [P, N_TOK])
        q_relu = [sb("q_relu", [P, N_TOK])] * B
        q_act = [sb("q_act", [P, N_TOK])] * B
        q_sq = [sb("q_sq", [P, N_TOK])] * B
        q_cube = [sb("q_cube", [P, N_TOK])] * B
        q_six = [sb("q_six", [P, N_TOK])] * B
        q_rec = per_half("q_rec", [P, TILES])
        q_ratio = per_half("q_ratio", [P, TILES])
        q_inv = per_half("q_inv", [P, TILES])
        q_inv_eps = per_half("q_inv_eps", [P, TILES])
        den = per_half("den", [P, TILES, HEADS])
        inv_den = per_half("inv_den", [P, TILES, HEADS])
        x1 = per_half("x1", [P, TILES, C])
        att0 = x1
        xn2T = [sb("xn2T", [P, N_TOK])] * B
        xn2_hi = per_half("xn2_hi", [P, N_TOK], f32r)
        xn2_lo = per_half("xn2_lo", [P, N_TOK], f32r)
        top8 = per_half("top8", [P, TILES, 8])
        top8_at = per_half("top8_at", [P, TILES, 8], u32)
        gap = per_half("gap", [P, TILES])
        gap_tanh = per_half("gap_tanh", [P, TILES])
        top_w = per_half("top_w", [P, 2, TILES])
        pick = per_half("pick", [P, 2, TILES, EXPERTS])
        pick_w = per_half("pick_w", [P, 2, TILES, EXPERTS])
        route = per_half("route", [P, TILES, EXPERTS])
        route_hl = per_half("route_hl", [P, TILES, 2 * EXPERTS], f32r)
        routeT = per_half("routeT", [2 * EXPERTS, N_TOK], f32r)
        moeT = [sb("moeT", [P, N_TOK])] * B
        x2 = per_half("x2", [P, TILES, C])
        xn3T = [sb("xn3T", [P, N_TOK])] * B
        s_max = per_half("s_max", [P, TILES])
        s_shift = [sb("s_shift", [P, TILES, CTX])] * B
        s_exp = [sb("s_exp", [P, TILES, CTX])] * B
        s_sum = per_half("s_sum", [P, TILES])
        s_inv = per_half("s_inv", [P, TILES])
        probs = [sb("probs", [P, TILES, CTX])] * B
        probsT = [sb("probsT", [CTX, N_TOK])] * B
        x3 = per_half("x3", [P, TILES, C])
        xn4_hi = per_half("xn4_hi", [P, N_TOK], f32r)
        xn4_lo = per_half("xn4_lo", [P, N_TOK], f32r)
        yT = [q_six[0], sb("yT", [P, N_TOK])]

        SG, SW, AB, HL = 3, 2, 2, 4
        silu_g = [sb(f"silu_g_{i}", [P, N_TOK]) for i in range(SG)]
        silu_w = [sb(f"silu_w_{i}", [P, N_TOK]) for i in range(SW)]
        hid = [sb(f"hid_{i}", [P, N_TOK]) for i in range(AB)]
        hid_hi = [sb(f"hid_hi_{i}", [P, N_TOK], f32r) for i in range(HL)]
        hid_lo = [sb(f"hid_lo_{i}", [P, N_TOK], f32r) for i in range(HL)]
        route_b = [sb(f"route_b_{i}", [P, N_TOK]) for i in range(2)]
        gelu = [q_relu[0], q_act[0], q_sq[0], q_cube[0]]
        gelu_hi, gelu_lo = hid_hi, hid_lo

        gate_ps = [bank("gate_ps_0"), bank("gate_ps_1")]
        val_ps = [bank("val_ps_0"), bank("val_ps_1")]
        acc_ps = bank("acc_ps")
        spread_ps = bank("spread_ps")
        side0 = bank("side0")
        side1 = bank("side1")
        ff_ps = [gate_ps[0], gate_ps[1], val_ps[0], val_ps[1]]

        small_in, rows_in, tw_in = sem("small_in"), sem("rows_in"), sem("tw_in")
        x_loaded = [sem(f"x_loaded_{h}") for h in range(B)]
        w1_in = [sem(f"w1_in_{e}") for e in range(EXPERTS)]
        w2_in = [sem(f"w2_in_{e}") for e in range(EXPERTS)]
        ones_set, powers_set, v_ones_set = sem("ones_set"), sem("powers_set"), sem("v_ones_set")
        scale_row_ps, scale_read = sem("scale_row_ps"), sem("scale_read")
        sp_ln_ready, sp_ready = sem("sp_ln_ready"), sem("sp_ready")
        kv_ps_ready, kv_read = sem("kv_ps_ready"), sem("kv_read")
        k_div_ready, k_sq_ready, k_cube_ready, k_six_ready = (
            sem("k_div_ready"), sem("k_sq_ready"), sem("k_cube_ready"), sem("k_six_ready"))
        k_ratio_ready, k_factor_ready, k_feat_ready = (
            sem("k_ratio_ready"), sem("k_factor_ready"), sem("k_feat_ready"))
        kvh_ps_ready, kvh_ready = sem("kvh_ps_ready"), sem("kvh_ready")
        k1T_ps_ready, k1T_ready = sem("k1T_ps_ready"), sem("k1T_ready")
        wqk_ps_ready, wqk_ready = sem("wqk_ps_ready"), sem("wqk_ready")
        v1_ps_ready, v1_ready = sem("v1_ps_ready"), sem("v1_ready")
        abs_ready, abs_ps_ready, tern_ready, select_ready = (
            sem("abs_ready"), sem("abs_ps_ready"), sem("tern_ready"), sem("select_ready"))
        w_hi_ready, w_lo_ready = sem("w_hi_ready"), sem("w_lo_ready")
        var_ready, rstd_ready, ln_ready = sem("var_ready"), sem("rstd_ready"), sem("ln_ready")
        lnT_ps_ready = sem("lnT_ps_ready")
        xn1T_ready, q_ps_ready, q_relu_ready, q_act_ready = (
            sem("xn1T_ready"), sem("q_ps_ready"), sem("q_relu_ready"), sem("q_act_ready"))
        q_sq_ready, q_cube_ready, q_six_ready = (
            sem("q_sq_ready"), sem("q_cube_ready"), sem("q_six_ready"))
        att0_ps_ready, q_ratio_ready, q_inv_ready, att0_read = (
            sem("att0_ps_ready"), sem("q_ratio_ready"), sem("q_inv_ready"), sem("att0_read"))
        xn2T_ready, xn2_hi_ready, xn2_lo_ready = (
            sem("xn2T_ready"), sem("xn2_hi_ready"), sem("xn2_lo_ready"))
        logits_ready, logits_read, gap_ready, gap_tanh_ready = (
            sem("logits_ready"), sem("logits_read"), sem("gap_ready"), sem("gap_tanh_ready"))
        route_ready, routeT_ps_ready, routeT_ready = (
            sem("route_ready"), sem("routeT_ps_ready"), sem("routeT_ready"))
        spread_ready, route_b_ready = sem("spread_ready"), sem("route_b_ready")
        gate_ready, val_ready = sem("gate_ready"), sem("val_ready")
        silu_ready, silu_w_ready, hid_ready = sem("silu_ready"), sem("silu_w_ready"), sem("hid_ready")
        hid_hi_ready, hid_lo_ready, w2_done = sem("hid_hi_ready"), sem("hid_lo_ready"), sem("w2_done")
        acc_ready, moeT_ready, moe_ps_ready, x2_ready = (
            sem("acc_ready"), sem("moeT_ready"), sem("moe_ps_ready"), sem("x2_ready"))
        xn3T_ready, score_ps_ready, s_shift_ready, s_exp_ready = (
            sem("xn3T_ready"), sem("score_ps_ready"), sem("s_shift_ready"), sem("s_exp_ready"))
        probs_ready, probsT_ps_ready, probsT_ready = (
            sem("probs_ready"), sem("probsT_ps_ready"), sem("probsT_ready"))
        att1_ps_ready, x3_ready = sem("att1_ps_ready"), sem("x3_ready")
        xn4_hi_ready, xn4_lo_ready = sem("xn4_hi_ready"), sem("xn4_lo_ready")
        ff_ps_ready, gelu_ready, gelu_hi_ready, gelu_lo_ready = (
            sem("ff_ps_ready"), sem("gelu_ready"), sem("gelu_hi_ready"), sem("gelu_lo_ready"))
        y_ps_ready, y_ready, y_stored = sem("y_ps_ready"), sem("y_ready"), sem("y_stored")
        dve_chain, act_chain, pool_chain = sem("dve_chain"), sem("act_chain"), sem("pool_chain")

        def ln_index(layer, h, which):
            return 4 * layer + 2 * h + which

        block = ctx.enter_context(nc.Block())

        @block.sync
        def _(sp_q):
            sp_q.dma_start(x_in[0][:, :, :], x[0].rearrange("(p t) c -> p t c", t=TILES)).then_inc(x_loaded[0], 16)
            sp_q.dma_start(row_sb[:, :], rows).then_inc(rows_in, 16)
            sp_q.dma_start(small[:, :], pack).then_inc(small_in, 16)
            for e in range(EXPERTS):
                if e >= RAW:
                    sp_q.wait_ge(w_lo_ready, 2 * (e - RAW) + 2)
                sp_q.dma_start(w1_raw[:, e % RAW, :], w1[:, e, :]).then_inc(w1_in[e], 16)
                sp_q.dma_start(w2_raw[:, e % RAW, :, :], w2[:, e, :, :]).then_inc(w2_in[e], 16)
                if e == 1:
                    sp_q.dma_start(x_in[1][:, :, :], x[1].rearrange("(p t) c -> p t c", t=TILES)).then_inc(x_loaded[1], 16)
                if e == RAW - 1:
                    sp_q.dma_start(tw_raw[:, :, :], ternary_w).then_inc(tw_in, 16)
            for h in range(B):
                sp_q.wait_ge(y_ready, h + 1)
                sp_q.dma_start(out[:, h, :], yT[h][:, :]).then_inc(y_stored, 16)
            sp_q.wait_ge(y_stored, 16 * B)

        @block.gpsimd
        def _(pool):
            nc.gpsimd.memset(ones[:, :], 1.0).then_inc(ones_set, 1)
            nc.gpsimd.memset(half_power[:, :], 0.5).then_inc(powers_set, 1)
            nc.gpsimd.memset(neg_half_power[:, :], -0.5).then_inc(powers_set, 1)
            nc.gpsimd.memset(v_ones[:, :, C:KV_COLS], 1.0).then_inc(v_ones_set, 1)
            pool.wait_ge(powers_set, 2)

            def rstd(i):
                pool.wait_ge(var_ready, i + 1)
                nc.gpsimd.tensor_tensor(ln_rstd[i][:, :], ln_var[i][:, :], neg_half_power[:, 0:TILES],
                                        ALU.pow).then_inc(rstd_ready, 1)

            def k_root():
                pool.wait_ge(k_ratio_ready, 1)
                nc.gpsimd.tensor_tensor(k_factor[:, :], k_ratio[:, :], half_power[0:CTX, 0:B],
                                        ALU.pow).then_inc(k_factor_ready, 1)

            def q_root(h):
                pool.wait_ge(q_ratio_ready, h + 1)
                nc.gpsimd.tensor_tensor(q_inv[h][:, :], q_ratio[h][:, :], half_power[:, 0:TILES],
                                        ALU.pow).then_inc(q_inv_ready, 1)

            def w_lo(e):
                pool.wait_ge(w_hi_ready, 2 * e + 2)
                nc.gpsimd.tensor_tensor(w1_lo[:, e, :], w1_raw[:, e % RAW, :], w1_hi[:, e, :].bitcast(f32),
                                        ALU.subtract).then_inc(w_lo_ready, 1)
                nc.gpsimd.tensor_tensor(w2_lo[:, e, :, :], w2_raw[:, e % RAW, :, :], w2_hi[:, e, :, :].bitcast(f32),
                                        ALU.subtract).then_inc(w_lo_ready, 1)

            def weigh(n):
                pool.wait_ge(silu_ready, n + 1)
                pool.wait_ge(route_b_ready, n // CHUNKS_PER_EXPERT + 1)
                if n >= SW:
                    pool.wait_ge(hid_ready, n - SW + 1)
                nc.gpsimd.tensor_tensor(silu_w[n % SW][:, :], silu_g[n % SG][:, :],
                                        route_b[(n // CHUNKS_PER_EXPERT) % 2][:, :],
                                        ALU.mult).then_inc(silu_w_ready, 1)

            rstd(ln_index(0, 0, 0))
            k_root()
            w_lo(0)
            q_root(0)
            w_lo(1)
            rstd(ln_index(0, 0, 1))
            w_lo(2)
            w_lo(3)
            for n in range(B * CHUNKS):
                weigh(n)
                if n == 0:
                    rstd(ln_index(0, 1, 0))
                if n in (1, 3, 5, 7):
                    w_lo(4 + n // 2)
                if n == 7:
                    q_root(1)
                if n == 9:
                    rstd(ln_index(0, 1, 1))
                if n == 21:
                    rstd(ln_index(1, 0, 0))
                if n == 28:
                    rstd(ln_index(1, 0, 1))
            rstd(ln_index(1, 1, 0))
            rstd(ln_index(1, 1, 1))

        @block.scalar
        def _(act):
            def w_hi(e):
                act.wait_ge(w1_in[e], 16)
                nc.scalar.activation(w1_hi[:, e, :], w1_raw[:, e % RAW, :], ACT.Copy).then_inc(w_hi_ready, 1)
                act.wait_ge(w2_in[e], 16)
                nc.scalar.activation(w2_hi[:, e, :, :], w2_raw[:, e % RAW, :, :], ACT.Copy).then_inc(w_hi_ready, 1)

            def softplus():
                act.wait_ge(scale_row_ps, 1)
                nc.scalar.activation(sp_in[:, 0:C], gate_ps[1][:, 0:C], ACT.Copy).then_inc(act_chain, 1)
                act.wait_ge(small_in, 16)
                a, _b = PACK["scale_bq"]
                nc.scalar.activation(sp_in[:, C:C + 1], small[:, a:a + 1], ACT.Copy).then_inc(scale_read, 1)
                act.wait_ge(act_chain, 1)
                act.wait_ge(scale_read, 1)
                nc.scalar.activation(sp_abs[:, :], sp_in[:, :], ACT.Abs).then_inc(act_chain, 1)
                act.wait_ge(act_chain, 2)
                nc.scalar.activation(sp_exp[:, :], sp_abs[:, :], ACT.Exp, scale=-1.0).then_inc(act_chain, 1)
                act.wait_ge(act_chain, 3)
                nc.scalar.activation(sp_ln[:, :], sp_exp[:, :], ACT.Ln, bias=1.0).then_inc(sp_ln_ready, 1)

            def k_squares(src, dst, ready, row, done):
                act.wait_ge(ready, 1)
                for b in range(B):
                    nc.scalar.activation(dst[:, b, :], src[:, b, :], ACT.Square,
                                         accum_out=k_sums[:, row, b:b + 1]).then_inc(done, 1)

            def ctx1_reads():
                act.wait_ge(k1T_ps_ready, 1)
                nc.scalar.activation(k1T[:, :], val_ps[0][:, 0:B * CTX], ACT.Copy).then_inc(k1T_ready, 1)
                act.wait_ge(v1_ps_ready, 1)
                nc.scalar.activation(v1[:, :, :], val_ps[1][0:CTX, 0:B * C].rearrange("p (b c) -> p b c", b=B),
                                     ACT.Copy).then_inc(v1_ready, 1)

            def wqk_read():
                act.wait_ge(wqk_ps_ready, 1)
                nc.scalar.activation(wq_k1T[:, :], val_ps[0][:, 0:B * CTX], ACT.Copy).then_inc(wqk_ready, 1)

            def abs_sums():
                act.wait_ge(tw_in, 16)
                for i in range(2):
                    if i:
                        act.wait_ge(abs_ready, i)
                    nc.scalar.activation(below[:, :], tw_raw[:, i, :], ACT.Abs,
                                         accum_out=abs_sum[:, i:i + 1]).then_inc(abs_ready, 1)

            def copy_T(dst, src, i, done):
                act.wait_ge(lnT_ps_ready, i + 1)
                nc.scalar.activation(dst[:, :], src[:, :], ACT.Copy).then_inc(done, 1)

            def q_first(h):
                act.wait_ge(q_ps_ready, h + 1)
                act.wait_ge(sp_ready, 1)
                nc.scalar.activation(q_relu[h][:, :], side1[:, :], ACT.Relu, bias=bq_inv_sp[:, :],
                                     scale=inv_sp[:, C:C + 1]).then_inc(q_relu_ready, 1)

            def q_square(h):
                act.wait_ge(q_act_ready, h + 1)
                nc.scalar.activation(q_sq[h][:, :], q_act[h][:, :], ACT.Square).then_inc(q_sq_ready, 1)

            def q_sixth(h):
                act.wait_ge(q_cube_ready, h + 1)
                nc.scalar.activation(q_six[h][:, :], q_cube[h][:, :], ACT.Square).then_inc(q_six_ready, 1)

            def xn2_round(h):
                act.wait_ge(xn2T_ready, h + 1)
                nc.scalar.activation(xn2_hi[h][:, :], xn2T[h][:, :], ACT.Copy).then_inc(xn2_hi_ready, 1)

            def route_tanh(h):
                act.wait_ge(gap_ready, h + 1)
                nc.scalar.activation(gap_tanh[h][:, :], gap[h][:, :], ACT.Tanh, scale=0.5).then_inc(gap_tanh_ready, 1)

            def silu(n):
                act.wait_ge(gate_ready, n + 1)
                if n >= SG:
                    act.wait_ge(silu_w_ready, n - SG + 1)
                nc.scalar.activation(silu_g[n % SG][:, :], gate_ps[n % 2][:, :], ACT.Silu).then_inc(silu_ready, 1)

            def read_spread(g):
                act.wait_ge(spread_ready, g + 1)
                if g >= 2:
                    act.wait_ge(silu_w_ready, CHUNKS_PER_EXPERT * (g - 1))
                nc.scalar.activation(route_b[g % 2][:, :], spread_ps[:, :], ACT.Copy).then_inc(route_b_ready, 1)

            def hid_round(n):
                act.wait_ge(hid_ready, n + 1)
                if n >= HL:
                    act.wait_ge(w2_done, n - HL + 1)
                nc.scalar.activation(hid_hi[n % HL][:, :], hid[n % AB][:, :], ACT.Copy).then_inc(hid_hi_ready, 1)

            def read_acc(h):
                act.wait_ge(acc_ready, h + 1)
                nc.scalar.activation(moeT[h][:, :], acc_ps[:, :], ACT.Copy).then_inc(moeT_ready, 1)

            def softmax_exp(h):
                act.wait_ge(s_shift_ready, h + 1)
                nc.scalar.activation(s_exp[h][:, :, :], s_shift[h][:, :, :], ACT.Exp,
                                     scale=float(1.0 / np.sqrt(C))).then_inc(s_exp_ready, 1)

            def read_probsT(h):
                act.wait_ge(probsT_ps_ready, h + 1)
                nc.scalar.activation(probsT[h][:, :], side1[0:CTX, :], ACT.Copy).then_inc(probsT_ready, 1)

            def ff_gelu(h, c):
                k = FF1_CHUNKS * h + c
                act.wait_ge(ff_ps_ready, k + 1)
                if h:
                    act.wait_ge(gelu_lo_ready, k - FF1_CHUNKS + 1)
                a, _b = PACK["b1"]
                nc.scalar.activation(gelu[c][:, :], ff_ps[c][:, :], ACT.Gelu,
                                     bias=small[:, a + c:a + c + 1]).then_inc(gelu_ready, 1)

            def ff_round(h, c):
                k = FF1_CHUNKS * h + c
                act.wait_ge(gelu_ready, k + 1)
                if h:
                    act.wait_ge(y_ps_ready, h)
                else:
                    act.wait_ge(w2_done, B * CHUNKS - HL + c + 1)
                nc.scalar.activation(gelu_hi[c][:, :], gelu[c][:, :], ACT.Copy).then_inc(gelu_hi_ready, 1)

            def finish(h):
                act.wait_ge(y_ps_ready, h + 1)
                a, b = PACK["b2"]
                nc.scalar.activation(yT[h][:, :], spread_ps[:, :], ACT.Identity, bias=small[:, a:b]).then_inc(y_ready, 1)

            softplus()
            copy_T(xn1T[0], side0, ln_index(0, 0, 0), xn1T_ready)
            k_squares(k_div, k_sq, k_div_ready, 0, k_sq_ready)
            k_squares(k_cube, k_six, k_cube_ready, 1, k_six_ready)
            q_first(0)
            w_hi(0)
            q_square(0)
            q_sixth(0)
            ctx1_reads()
            w_hi(1)
            wqk_read()
            w_hi(2)
            copy_T(xn2T[0], side0, ln_index(0, 0, 1), xn2T_ready)
            xn2_round(0)
            route_tanh(0)
            w_hi(3)
            for n in range(B * CHUNKS):
                silu(n)
                if n % CHUNKS_PER_EXPERT == 0:
                    read_spread(n // CHUNKS_PER_EXPERT)
                if n in (0, 1, 2, 3):
                    w_hi(4 + n)
                if n >= 1:
                    hid_round(n - 1)
                if n == 3:
                    copy_T(xn1T[1], side0, ln_index(0, 1, 0), xn1T_ready)
                if n == 4:
                    q_first(1)
                if n == 5:
                    q_square(1)
                if n == 6:
                    q_sixth(1)
                if n == 11:
                    copy_T(xn2T[1], side0, ln_index(0, 1, 1), xn2T_ready)
                    xn2_round(1)
                if n == 12:
                    route_tanh(1)
                if n == 14:
                    abs_sums()
                if n == 19:
                    read_acc(0)
                if n == 23:
                    copy_T(xn3T[0], side1, ln_index(1, 0, 0), xn3T_ready)
                if n == 25:
                    softmax_exp(0)
                if n == 26:
                    read_probsT(0)
                if n == 30:
                    copy_T(xn4_hi[0], side0, ln_index(1, 0, 1), xn4_hi_ready)
            hid_round(B * CHUNKS - 1)
            for c in range(FF1_CHUNKS):
                ff_gelu(0, c)
            read_acc(1)
            for c in range(FF1_CHUNKS):
                ff_round(0, c)
            copy_T(xn3T[1], side1, ln_index(1, 1, 0), xn3T_ready)
            finish(0)
            softmax_exp(1)
            read_probsT(1)
            copy_T(xn4_hi[1], side0, ln_index(1, 1, 1), xn4_hi_ready)
            for c in range(FF1_CHUNKS):
                ff_gelu(1, c)
                ff_round(1, c)
            finish(1)

        @block.vector
        def _(dve):
            links = [0]

            def link(ins):
                links[0] += 1
                ins.then_inc(dve_chain, 1)
                dve.wait_ge(dve_chain, links[0])

            def ln_begin(src, i):
                for t in range(TILES):
                    last = nc.vector.bn_stats(ln_stats[i][:, t, :], src[:, t, :])
                link(last)
                for t in range(TILES):
                    last = nc.vector.bn_aggr(ln_mv[i][:, t, :], ln_stats[i][:, t, :])
                link(last)
                nc.vector.tensor_scalar(ln_var[i][:, :], ln_mv[i][:, :, 1], LN_EPS, None, ALU.add).then_inc(var_ready, 1)

            def ln_end(src, i):
                dve.wait_ge(rstd_ready, i + 1)
                for t in range(TILES):
                    last = nc.vector.tensor_scalar(ln_out[i][:, t, :], src[:, t, :], ln_mv[i][:, t, 0:1],
                                                   ln_rstd[i][:, t:t + 1], ALU.subtract, ALU.mult)
                last.then_inc(ln_ready, 1)

            def softplus_end():
                dve.wait_ge(sp_ln_ready, 1)
                link(nc.vector.scalar_tensor_tensor(out=sp[:, :], in0=sp_in[:, :], scalar=0.0, in1=sp_ln[:, :],
                                                    op0=ALU.max, op1=ALU.add))
                link(nc.vector.reciprocal(inv_sp[:, :], sp[:, :]))
                a, b = PACK["scale_bq"]
                nc.vector.tensor_scalar(eps_inv_sp[:, :], inv_sp[:, C:C + 1], FOCUS_EPS, None, ALU.mult)
                nc.vector.tensor_tensor(bq_inv_sp[:, :], inv_sp[:, C:C + 1], small[:, a + 1:b], ALU.mult).then_inc(sp_ready, 1)

            def keys_first():
                dve.wait_ge(kv_ps_ready, 1)
                kv = gate_ps[0][0:CTX, :].rearrange("p (b k c) -> p b k c", b=B, k=2)
                link(nc.vector.tensor_scalar(k_act[:, :, :], kv[:, :, 0, :], 0.0, FOCUS_EPS, ALU.max, ALU.add))
                nc.vector.tensor_copy(v_ones[:, :, 0:C], kv[:, :, 1, :]).then_inc(kv_read, 1)
                nc.vector.tensor_tensor(k_div[:, :, :], k_act[:, :, :],
                                        inv_sp[0:CTX, 0:C].unsqueeze(1).broadcast_to([CTX, B, C]),
                                        ALU.mult).then_inc(k_div_ready, 1)

            def keys_cube():
                dve.wait_ge(k_sq_ready, B)
                nc.vector.tensor_tensor(k_cube[:, :, :], k_sq[:, :, :], k_div[:, :, :], ALU.mult).then_inc(k_cube_ready, 1)

            def keys_ratio():
                dve.wait_ge(k_six_ready, B)
                link(nc.vector.reciprocal(k_rec[:, :], k_sums[:, 1, :]))
                nc.vector.tensor_tensor(k_ratio[:, :], k_sums[:, 0, :], k_rec[:, :], ALU.mult).then_inc(k_ratio_ready, 1)

            def keys_end():
                dve.wait_ge(k_factor_ready, 1)
                for b in range(B):
                    last = nc.vector.tensor_scalar(k_feat[:, b, :], k_cube[:, b, :], k_factor[:, b:b + 1], None, ALU.mult)
                last.then_inc(k_feat_ready, 1)

            def kv_mask():
                dve.wait_ge(kvh_ps_ready, 1)
                nc.vector.tensor_tensor(kv_heads[:, :, :],
                                        acc_ps[:, 0:B * KV_COLS].rearrange("p (b c) -> p b c", b=B),
                                        packed("kv_mask").unsqueeze(1).broadcast_to([P, B, KV_COLS]),
                                        ALU.mult).then_inc(kvh_ready, 1)

            def select_round():
                nc.vector.tensor_tensor(select[:, :, :],
                                        ident[0:2 * EXPERTS, 0:EXPERTS].unsqueeze(2).broadcast_to([2 * EXPERTS, EXPERTS, P]),
                                        ident[0:2 * EXPERTS, EXPERTS:2 * EXPERTS].unsqueeze(2).broadcast_to([2 * EXPERTS, EXPERTS, P]),
                                        ALU.add).then_inc(select_ready, 1)

            def q_second(h):
                dve.wait_ge(q_relu_ready, h + 1)
                nc.vector.tensor_scalar(q_act[h][:, :], q_relu[h][:, :], eps_inv_sp[:, :], None, ALU.add).then_inc(q_act_ready, 1)

            def q_third(h):
                dve.wait_ge(q_sq_ready, h + 1)
                nc.vector.tensor_tensor(q_cube[h][:, :], q_sq[h][:, :], q_act[h][:, :], ALU.mult).then_inc(q_cube_ready, 1)

            def att0_begin(h):
                dve.wait_ge(att0_ps_ready, h + 1)
                link(nc.vector.reciprocal(q_rec[h][:, :], side0[:, 0:TILES]))
                nc.vector.tensor_tensor(q_ratio[h][:, :], side0[:, TILES:2 * TILES], q_rec[h][:, :],
                                        ALU.mult).then_inc(q_ratio_ready, 1)

            def att0_end(h):
                dve.wait_ge(q_inv_ready, h + 1)
                link(nc.vector.tensor_scalar(q_inv_eps[h][:, :], q_inv[h][:, :], FOCUS_EPS, None, ALU.mult))
                for i, ps in enumerate((side0[:, P:P + 2 * KV_COLS], side1[:, 0:2 * KV_COLS])):
                    nd = ps.rearrange("p (t c) -> p t c", t=2)
                    last = nc.vector.tensor_tensor(den[h][:, 2 * i:2 * i + 2, :], nd[:, :, C:KV_COLS],
                                                   q_inv_eps[h][:, 2 * i:2 * i + 2].unsqueeze(2).broadcast_to([P, 2, HEADS]),
                                                   ALU.add)
                link(last)
                link(nc.vector.reciprocal(inv_den[h][:, :, :], den[h][:, :, :]))
                for i, ps in enumerate((side0[:, P:P + 2 * KV_COLS], side1[:, 0:2 * KV_COLS])):
                    nd = ps.rearrange("p (t c) -> p t c", t=2)[:, :, 0:C]
                    last = nc.vector.tensor_tensor(
                        att0[h][:, 2 * i:2 * i + 2, :].rearrange("p t (g d) -> p t g d", g=HEADS),
                        nd.rearrange("p t (g d) -> p t g d", g=HEADS),
                        inv_den[h][:, 2 * i:2 * i + 2, :].unsqueeze(3).broadcast_to([P, 2, HEADS, HEAD_DIM]),
                        ALU.mult)
                last.then_inc(att0_read, 1)
                dve.wait_ge(att0_read, h + 1)
                link(nc.vector.tensor_tensor(x1[h][:, :, :], x_in[h][:, :, :], att0[h][:, :, :], ALU.add))

            def xn2_rest(h):
                dve.wait_ge(xn2_hi_ready, h + 1)
                nc.vector.tensor_tensor(xn2_lo[h][:, :], xn2T[h][:, :], xn2_hi[h][:, :].bitcast(f32),
                                        ALU.subtract).then_inc(xn2_lo_ready, 1)

            def route_top(h):
                dve.wait_ge(logits_ready, h + 1)
                lg = side1[:, 0:TILES * EXPERTS].rearrange("p (t e) -> p t e", t=TILES)
                for t in range(TILES):
                    last = nc.vector.max(top8[h][:, t, :], lg[:, t, :])
                link(last)
                nc.vector.tensor_tensor(gap[h][:, :], top8[h][:, :, 0], top8[h][:, :, 1], ALU.subtract).then_inc(gap_ready, 1)
                for t in range(TILES):
                    last = nc.vector.max_index(top8_at[h][:, t, :], top8[h][:, t, :], lg[:, t, :])
                last.then_inc(logits_read, 1)

            def route_weights(h):
                dve.wait_ge(gap_tanh_ready, h + 1)
                dve.wait_ge(logits_read, h + 1)
                nc.vector.tensor_scalar(top_w[h][:, 0, :], gap_tanh[h][:, :], 0.5, 0.5, ALU.mult, ALU.add)
                nc.vector.tensor_scalar(top_w[h][:, 1, :], gap_tanh[h][:, :], -0.5, 0.5, ALU.mult, ALU.add)
                for k in range(2):
                    last = nc.vector.tensor_tensor(pick[h][:, k, :, :],
                                                   packed("iota").unsqueeze(1).broadcast_to([P, TILES, EXPERTS]),
                                                   top8_at[h][:, :, k:k + 1].broadcast_to([P, TILES, EXPERTS]),
                                                   ALU.is_equal)
                link(last)
                for k in range(2):
                    last = nc.vector.tensor_tensor(pick_w[h][:, k, :, :], pick[h][:, k, :, :],
                                                   top_w[h][:, k, :].unsqueeze(2).broadcast_to([P, TILES, EXPERTS]),
                                                   ALU.mult)
                link(last)
                link(nc.vector.tensor_tensor(route[h][:, :, :], pick_w[h][:, 0, :, :], pick_w[h][:, 1, :, :], ALU.add))
                link(nc.vector.tensor_copy(route_hl[h][:, :, 0:EXPERTS], route[h][:, :, :]))
                nc.vector.tensor_tensor(route_hl[h][:, :, EXPERTS:2 * EXPERTS], route[h][:, :, :],
                                        route_hl[h][:, :, 0:EXPERTS].bitcast(f32), ALU.subtract).then_inc(route_ready, 1)

            def route_T(h):
                dve.wait_ge(routeT_ps_ready, h + 1)
                nc.vector.tensor_copy(routeT[h][:, :], side1[0:2 * EXPERTS, :]).then_inc(routeT_ready, 1)

            def hidden(n):
                dve.wait_ge(val_ready, n + 1)
                dve.wait_ge(silu_w_ready, n + 1)
                if n >= AB:
                    dve.wait_ge(hid_hi_ready, n - AB + 1)
                    dve.wait_ge(hid_lo_ready, n - AB + 1)
                nc.vector.tensor_tensor(hid[n % AB][:, :], val_ps[n % 2][:, :], silu_w[n % SW][:, :],
                                        ALU.mult).then_inc(hid_ready, 1)

            def hidden_rest(n):
                dve.wait_ge(hid_hi_ready, n + 1)
                if n >= HL:
                    dve.wait_ge(w2_done, n - HL + 1)
                nc.vector.tensor_tensor(hid_lo[n % HL][:, :], hid[n % AB][:, :], hid_hi[n % HL][:, :].bitcast(f32),
                                        ALU.subtract).then_inc(hid_lo_ready, 1)

            def thresholds():
                dve.wait_ge(abs_ps_ready, 1)
                link(nc.vector.tensor_scalar(t_scale[:, :], side0[:, 0:2], 1.0 / (FF1 * C), 1e-8, ALU.mult, ALU.max))
                nc.vector.tensor_scalar(t_hi[:, :], t_scale[:, :], 0.5, None, ALU.mult)
                link(nc.vector.tensor_scalar(t_lo[:, :], t_scale[:, :], -0.5, None, ALU.mult))

            def ternary(i):
                if i:
                    dve.wait_ge(tern_ready, i)
                link(nc.vector.tensor_scalar(below[:, :], tw_raw[:, i, :], t_lo[:, i:i + 1], None, ALU.is_lt))
                nc.vector.scalar_tensor_tensor(out=tern[:, i, :], in0=tw_raw[:, i, :], scalar=t_hi[:, i:i + 1],
                                               in1=below[:, :], op0=ALU.is_gt, op1=ALU.subtract).then_inc(tern_ready, 1)

            def add_moe(h):
                dve.wait_ge(moe_ps_ready, h + 1)
                nc.vector.tensor_tensor(x2[h][:, :, :], side0[:, :].rearrange("p (t c) -> p t c", t=TILES),
                                        x1[h][:, :, :], ALU.add).then_inc(x2_ready, 1)
                dve.wait_ge(x2_ready, h + 1)

            def softmax_shift(h):
                dve.wait_ge(score_ps_ready, h + 1)
                sc = side0[:, 0:TILES * CTX].rearrange("p (t k) -> p t k", t=TILES)
                link(nc.vector.tensor_reduce(s_max[h][:, :], sc, AX.X, ALU.max))
                nc.vector.tensor_tensor(s_shift[h][:, :, :], sc, s_max[h][:, :].unsqueeze(2).broadcast_to([P, TILES, CTX]),
                                        ALU.subtract).then_inc(s_shift_ready, 1)

            def softmax_end(h):
                dve.wait_ge(s_exp_ready, h + 1)
                link(nc.vector.tensor_reduce(s_sum[h][:, :], s_exp[h][:, :, :], AX.X, ALU.add))
                link(nc.vector.reciprocal(s_inv[h][:, :], s_sum[h][:, :]))
                nc.vector.tensor_tensor(probs[h][:, :, :], s_exp[h][:, :, :],
                                        s_inv[h][:, :].unsqueeze(2).broadcast_to([P, TILES, CTX]),
                                        ALU.mult).then_inc(probs_ready, 1)

            def add_att1(h):
                dve.wait_ge(att1_ps_ready, h + 1)
                nc.vector.tensor_tensor(x3[h][:, :, :], side0[:, :].rearrange("p (t c) -> p t c", t=TILES),
                                        x2[h][:, :, :], ALU.add).then_inc(x3_ready, 1)
                dve.wait_ge(x3_ready, h + 1)

            def xn4_rest(h):
                dve.wait_ge(xn4_hi_ready, h + 1)
                nc.vector.tensor_tensor(xn4_lo[h][:, :], side0[:, :], xn4_hi[h][:, :].bitcast(f32),
                                        ALU.subtract).then_inc(xn4_lo_ready, 1)

            def ff_rest(h, c):
                k = FF1_CHUNKS * h + c
                dve.wait_ge(gelu_hi_ready, k + 1)
                nc.vector.tensor_tensor(gelu_lo[c][:, :], gelu[c][:, :], gelu_hi[c][:, :].bitcast(f32),
                                        ALU.subtract).then_inc(gelu_lo_ready, 1)

            dve.wait_ge(x_loaded[0], 16)
            ln_begin(x_in[0], ln_index(0, 0, 0))
            dve.wait_ge(small_in, 16)
            ln_end(x_in[0], ln_index(0, 0, 0))
            softplus_end()
            keys_first()
            keys_cube()
            keys_ratio()
            q_second(0)
            keys_end()
            q_third(0)
            kv_mask()
            select_round()
            att0_begin(0)
            att0_end(0)
            ln_begin(x1[0], ln_index(0, 0, 1))
            ln_end(x1[0], ln_index(0, 0, 1))
            dve.wait_ge(x_loaded[1], 16)
            ln_begin(x_in[1], ln_index(0, 1, 0))
            xn2_rest(0)
            route_top(0)
            route_weights(0)
            route_T(0)
            for n in range(B * CHUNKS):
                hidden(n)
                if n >= 1:
                    hidden_rest(n - 1)
                if n == 1:
                    ln_end(x_in[1], ln_index(0, 1, 0))
                if n == 4:
                    q_second(1)
                if n == 5:
                    q_third(1)
                if n == 7:
                    att0_begin(1)
                if n == 8:
                    att0_end(1)
                    ln_begin(x1[1], ln_index(0, 1, 1))
                if n == 10:
                    ln_end(x1[1], ln_index(0, 1, 1))
                if n == 12:
                    xn2_rest(1)
                    route_top(1)
                if n == 13:
                    route_weights(1)
                if n == 14:
                    route_T(1)
                if n == 16:
                    thresholds()
                    ternary(0)
                if n == 17:
                    ternary(1)
                if n == 20:
                    add_moe(0)
                    ln_begin(x2[0], ln_index(1, 0, 0))
                if n == 22:
                    ln_end(x2[0], ln_index(1, 0, 0))
                if n == 24:
                    softmax_shift(0)
                if n == 25:
                    softmax_end(0)
                if n == 27:
                    add_att1(0)
                    ln_begin(x3[0], ln_index(1, 0, 1))
                if n == 29:
                    ln_end(x3[0], ln_index(1, 0, 1))
                if n == 30:
                    xn4_rest(0)
            hidden_rest(B * CHUNKS - 1)
            add_moe(1)
            ln_begin(x2[1], ln_index(1, 1, 0))
            ln_end(x2[1], ln_index(1, 1, 0))
            for c in range(FF1_CHUNKS):
                ff_rest(0, c)
            softmax_shift(1)
            softmax_end(1)
            add_att1(1)
            ln_begin(x3[1], ln_index(1, 1, 1))
            ln_end(x3[1], ln_index(1, 1, 1))
            xn4_rest(1)
            for c in range(FF1_CHUNKS):
                ff_rest(1, c)

        @block.tensor
        def _(pe):
            def ln_T(dst, i):
                pe.wait_ge(ln_ready, i + 1)
                for t in range(TILES):
                    last = nc.tensor.transpose(dst[:, t * P:(t + 1) * P], ln_out[i][:, t, :], ident)
                last.then_inc(lnT_ps_ready, 1)

            def bias_rows():
                pe.wait_ge(ones_set, 1)
                pe.wait_ge(rows_in, 16)
                nc.tensor.matmul(gate_ps[1][:, 0:C], ones[0:1, :], row_sb[:, 4 * C:5 * C],
                                 start=True, stop=True).then_inc(scale_row_ps, 1)
                nc.tensor.matmul(gate_ps[0][0:CTX, :], ones[0:1, 0:CTX], row_sb[:, 0:4 * C], start=True, stop=False)

            def ctx0_keys_values():
                a, b = PACK["Wkv0"]
                pe.wait_ge(small_in, 16)
                for i in range(B):
                    last = nc.tensor.matmul(gate_ps[0][0:CTX, i * 2 * C:(i + 1) * 2 * C], ctxT[:, i * CTX:(i + 1) * CTX],
                                            small[:, a:b], start=False, stop=(i == B - 1))
                last.then_inc(kv_ps_ready, 1)

            def ctx1_keys_values():
                a, _b = PACK["Wkv1"]
                nc.tensor.matmul(val_ps[0][:, 0:B * CTX], small[:, a:a + C], ctxT, start=True, stop=True).then_inc(k1T_ps_ready, 1)
                for i in range(B):
                    last = nc.tensor.matmul(val_ps[1][0:CTX, i * C:(i + 1) * C], ctxT[:, i * CTX:(i + 1) * CTX],
                                            small[:, a + C:a + 2 * C], start=True, stop=True)
                last.then_inc(v1_ps_ready, 1)

            def ctx1_wq_keys():
                pe.wait_ge(k1T_ready, 1)
                nc.tensor.matmul(val_ps[0][:, 0:B * CTX], packed("Wq1T"), k1T[:, :], start=True, stop=True).then_inc(wqk_ps_ready, 1)

            def head_sums():
                pe.wait_ge(k_feat_ready, 1)
                pe.wait_ge(kv_read, 1)
                pe.wait_ge(v_ones_set, 1)
                for i in range(B):
                    last = nc.tensor.matmul(acc_ps[:, i * KV_COLS:(i + 1) * KV_COLS], k_feat[:, i, :], v_ones[:, i, :],
                                            start=True, stop=True)
                last.then_inc(kvh_ps_ready, 1)

            def q_project(h):
                pe.wait_ge(xn1T_ready, h + 1)
                if h:
                    pe.wait_ge(routeT_ready, h)
                nc.tensor.matmul(side1[:, :], packed("Wq0"), xn1T[h][:, :], start=True, stop=True).then_inc(q_ps_ready, 1)

            def att0_products(h):
                pe.wait_ge(kvh_ready, 1)
                pe.wait_ge(q_cube_ready, h + 1)
                pe.wait_ge(q_relu_ready, h + 1)
                for t in range(TILES):
                    ps = side0[:, P + t * KV_COLS:P + (t + 1) * KV_COLS] if t < 2 else side1[:, (t - 2) * KV_COLS:(t - 1) * KV_COLS]
                    nc.tensor.matmul(ps, q_cube[h][:, t * P:(t + 1) * P], kv_heads[:, h, :], start=True, stop=True)
                pe.wait_ge(q_sq_ready, h + 1)
                for t in range(TILES):
                    nc.tensor.matmul(side0[:, t:t + 1], q_sq[h][:, t * P:(t + 1) * P], ones[:, 0:1], start=True, stop=True)
                pe.wait_ge(q_six_ready, h + 1)
                for t in range(TILES):
                    last = nc.tensor.matmul(side0[:, TILES + t:TILES + t + 1], q_six[h][:, t * P:(t + 1) * P], ones[:, 0:1],
                                            start=True, stop=True)
                last.then_inc(att0_ps_ready, 1)

            def router(h):
                pe.wait_ge(xn2T_ready, h + 1)
                pe.wait_ge(att0_read, h + 1)
                for t in range(TILES):
                    last = nc.tensor.matmul(side1[:, t * EXPERTS:(t + 1) * EXPERTS], xn2T[h][:, t * P:(t + 1) * P],
                                            packed("WrT"), start=True, stop=True)
                last.then_inc(logits_ready, 1)

            def route_turn(h):
                pe.wait_ge(route_ready, h + 1)
                pe.wait_ge(logits_read, h + 1)
                for t in range(TILES):
                    last = nc.tensor.transpose(side1[0:2 * EXPERTS, t * P:(t + 1) * P],
                                               route_hl[h][:, t, :].bitcast(f32), ident)
                last.then_inc(routeT_ps_ready, 1)

            def spread(g):
                h, e = divmod(g, EXPERTS)
                pe.wait_ge(routeT_ready, h + 1)
                pe.wait_ge(select_ready, 1)
                if g:
                    pe.wait_ge(route_b_ready, g)
                nc.tensor.matmul(spread_ps[:, :], select[:, e, :], routeT[h][:, :], start=True, stop=True).then_inc(spread_ready, 1)

            def up(ps, h, e, col, done):
                hi, lo = w1_hi[:, e, col:col + P], w1_lo[:, e, col:col + P]
                nc.tensor.matmul(ps, lo, xn2_hi[h][:, :], start=True, stop=False)
                nc.tensor.matmul(ps, hi, xn2_lo[h][:, :], start=False, stop=False)
                nc.tensor.matmul(ps, hi, xn2_hi[h][:, :], start=False, stop=True).then_inc(done, 1)

            def chunk_up(n):
                h, j = divmod(n, CHUNKS)
                e, c = divmod(j, CHUNKS_PER_EXPERT)
                pe.wait_ge(xn2_lo_ready, h + 1)
                if h == 0:
                    pe.wait_ge(w_lo_ready, 2 * e + 2)
                if n == 0:
                    pe.wait_ge(kv_read, 1)
                    pe.wait_ge(wqk_ready, 1)
                if n == 1:
                    pe.wait_ge(scale_read, 1)
                    pe.wait_ge(act_chain, 1)
                    pe.wait_ge(v1_ready, 1)
                if n >= 2:
                    pe.wait_ge(silu_ready, n - 1)
                up(gate_ps[n % 2][:, :], h, e, FFN + c * P, gate_ready)
                if n >= 2:
                    pe.wait_ge(hid_ready, n - 1)
                up(val_ps[n % 2][:, :], h, e, c * P, val_ready)

            def chunk_down(m):
                h, j = divmod(m, CHUNKS)
                e, c = divmod(j, CHUNKS_PER_EXPERT)
                if m == 0:
                    pe.wait_ge(kvh_ready, 1)
                if j == 0 and h:
                    pe.wait_ge(moeT_ready, h)
                pe.wait_ge(hid_lo_ready, m + 1)
                hi, lo = hid_hi[m % HL][:, :], hid_lo[m % HL][:, :]
                nc.tensor.matmul(acc_ps[:, :], w2_lo[:, e, c, :], hi, start=(j == 0), stop=False)
                nc.tensor.matmul(acc_ps[:, :], w2_hi[:, e, c, :], lo, start=False, stop=False)
                nc.tensor.matmul(acc_ps[:, :], w2_hi[:, e, c, :], hi, start=False, stop=(j == CHUNKS - 1)).then_inc(w2_done, 1)
                if j == CHUNKS - 1:
                    pe.wait_ge(w2_done, m + 1)
                    pe.sem_inc(acc_ready, 1)

            def ternary_sum():
                pe.wait_ge(abs_ready, 2)
                pe.wait_ge(xn2T_ready, B)
                nc.tensor.matmul(side0[:, 0:2], ones[:, :], abs_sum[:, :], start=True, stop=True).then_inc(abs_ps_ready, 1)

            def moe_turn(h):
                pe.wait_ge(moeT_ready, h + 1)
                if h == 0:
                    pe.wait_ge(tern_ready, 1)
                for t in range(TILES):
                    last = nc.tensor.transpose(side0[:, t * P:(t + 1) * P], moeT[h][:, t * P:(t + 1) * P], ident)
                last.then_inc(moe_ps_ready, 1)

            def scores(h):
                pe.wait_ge(xn3T_ready, h + 1)
                pe.wait_ge(x2_ready, h + 1)
                pe.wait_ge(wqk_ready, 1)
                for t in range(TILES):
                    last = nc.tensor.matmul(side0[:, t * CTX:(t + 1) * CTX], xn3T[h][:, t * P:(t + 1) * P],
                                            wq_k1T[:, h * CTX:(h + 1) * CTX], start=True, stop=True)
                last.then_inc(score_ps_ready, 1)

            def probs_turn(h):
                pe.wait_ge(probs_ready, h + 1)
                for t in range(TILES):
                    last = nc.tensor.transpose(side1[0:CTX, t * P:(t + 1) * P], probs[h][:, t, :], ident)
                last.then_inc(probsT_ps_ready, 1)

            def att1_products(h):
                pe.wait_ge(probsT_ready, h + 1)
                for t in range(TILES):
                    last = nc.tensor.matmul(side0[:, t * C:(t + 1) * C], probsT[h][:, t * P:(t + 1) * P], v1[:, h, :],
                                            start=True, stop=True)
                last.then_inc(att1_ps_ready, 1)

            def residual_T(h):
                pe.wait_ge(x3_ready, h + 1)
                if h == 0:
                    pe.wait_ge(route_b_ready, B * EXPERTS)
                else:
                    pe.wait_ge(y_ready, h)
                for t in range(TILES):
                    nc.tensor.matmul(spread_ps[:, t * P:(t + 1) * P], x3[h][:, t, :], ident, start=(t == 0), stop=False,
                                     skip_group_check=True)

            def ff_up(h, c):
                pe.wait_ge(xn4_lo_ready, h + 1)
                pe.wait_ge(tern_ready, 2)
                if h == 0:
                    pe.wait_ge(silu_ready, B * CHUNKS)
                    if c >= 2:
                        pe.wait_ge(hid_ready, B * CHUNKS)
                else:
                    pe.wait_ge(gelu_ready, c + 1)
                w = tern[:, 0, c * P:(c + 1) * P]
                nc.tensor.matmul(ff_ps[c][:, :], w, xn4_lo[h][:, :], start=True, stop=False)
                nc.tensor.matmul(ff_ps[c][:, :], w, xn4_hi[h][:, :], start=False, stop=True).then_inc(ff_ps_ready, 1)

            def ff_down(h, c):
                pe.wait_ge(gelu_lo_ready, FF1_CHUNKS * h + c + 1)
                w = tern[:, 1, c * P:(c + 1) * P]
                nc.tensor.matmul(spread_ps[:, :], w, gelu_lo[c][:, :], start=False, stop=False, skip_group_check=True)
                last = nc.tensor.matmul(spread_ps[:, :], w, gelu_hi[c][:, :], start=False, stop=(c == FF1_CHUNKS - 1),
                                        skip_group_check=True)
                if c == FF1_CHUNKS - 1:
                    last.then_inc(y_ps_ready, 1)

            bias_rows()
            ctx0_keys_values()
            ln_T(side0, ln_index(0, 0, 0))
            ctx1_keys_values()
            q_project(0)
            ctx1_wq_keys()
            head_sums()
            pe.wait_ge(xn1T_ready, 1)
            att0_products(0)
            pe.wait_ge(att0_read, 1)
            ln_T(side0, ln_index(0, 0, 1))
            router(0)
            route_turn(0)
            for n in range(B * CHUNKS):
                if n % CHUNKS_PER_EXPERT == 0:
                    spread(n // CHUNKS_PER_EXPERT)
                chunk_up(n)
                if n >= W2_LAG:
                    chunk_down(n - W2_LAG)
                if n == 2:
                    pe.wait_ge(xn2T_ready, 1)
                    ln_T(side0, ln_index(0, 1, 0))
                if n == 3:
                    q_project(1)
                if n == 7:
                    att0_products(1)
                if n == 10:
                    pe.wait_ge(att0_read, 2)
                    ln_T(side0, ln_index(0, 1, 1))
                if n == 11:
                    router(1)
                if n == 13:
                    route_turn(1)
                if n == 15:
                    ternary_sum()
                if n == 19:
                    moe_turn(0)
                if n == 22:
                    pe.wait_ge(routeT_ready, 2)
                    ln_T(side1, ln_index(1, 0, 0))
                if n == 23:
                    scores(0)
                if n == 25:
                    probs_turn(0)
                if n == 26:
                    att1_products(0)
                if n == 29:
                    ln_T(side0, ln_index(1, 0, 1))
            residual_T(0)
            ff_up(0, 0)
            ff_up(0, 1)
            for m in range(B * CHUNKS - W2_LAG, B * CHUNKS):
                chunk_down(m)
            ff_up(0, 2)
            ff_up(0, 3)
            pe.wait_ge(xn4_lo_ready, 1)
            moe_turn(1)
            for c in range(FF1_CHUNKS):
                ff_down(0, c)
            ln_T(side1, ln_index(1, 1, 0))
            scores(1)
            probs_turn(1)
            att1_products(1)
            residual_T(1)
            ln_T(side0, ln_index(1, 1, 1))
            for c in range(FF1_CHUNKS):
                ff_up(1, c)
            for c in range(FF1_CHUNKS):
                ff_down(1, c)


def kernel(x, ctx_1024, L0_xattn_Wq, L0_xattn_bq, L0_xattn_Wk, L0_xattn_bk, L0_xattn_Wv, L0_xattn_bv,
           L0_xattn_scale, L0_ffn_Wr, L0_ffn_W1, L0_ffn_W2, L1_xattn_Wq, L1_xattn_Wkv, L1_ffn_W1,
           L1_ffn_b1, L1_ffn_W2, L1_ffn_b2):
    import concourse.bacc as bacc
    from concourse.bass_utils import run_bass_kernel_spmd

    f = np.float32
    a = [np.asarray(v) for v in (ctx_1024, L0_xattn_Wq, L0_xattn_bq, L0_xattn_Wk, L0_xattn_bk, L0_xattn_Wv,
                                 L0_xattn_bv, L0_xattn_scale, L0_ffn_Wr, L0_ffn_W1, L0_ffn_W2, L1_xattn_Wq,
                                 L1_xattn_Wkv, L1_ffn_W1, L1_ffn_b1, L1_ffn_W2, L1_ffn_b2)]
    ctx_, wq0, bq, wk0, bk, wv0, bv, scale, wr, w1, w2, wq1, wkv1, tw1, b1, tw2, b2 = a
    head = np.arange(C) // HEAD_DIM
    kv_mask = np.concatenate([head[:, None] == head[None, :], head[:, None] == np.arange(HEADS)[None, :]], 1).astype(f)
    iota = np.tile(np.arange(EXPERTS, dtype=f), (P, 1))
    parts = {
        "ctxT": ctx_.reshape(B * CTX, C).T, "Wkv0": np.concatenate([wk0, wv0], 1), "Wq0": wq0,
        "scale_bq": np.stack([scale.reshape(C), bq], 1), "ident": np.eye(C, dtype=f), "Wkv1": wkv1, "Wq1T": wq1.T,
        "WrT": wr.T, "b1": b1.reshape(FF1_CHUNKS, P).T, "b2": b2.reshape(C, 1), "kv_mask": kv_mask, "iota": iota,
    }
    arrays = {
        "x": np.ascontiguousarray(np.asarray(x)),
        "pack": np.ascontiguousarray(np.concatenate([parts[k] for k in PACK], 1)),
        "rows": np.concatenate([bk, bv, bk, bv, scale.reshape(C)]).reshape(1, ROW_COLS),
        "w1": np.ascontiguousarray(w1.transpose(2, 0, 1)),
        "w2": np.ascontiguousarray(w2.reshape(EXPERTS, C, CHUNKS_PER_EXPERT, P).transpose(3, 0, 2, 1)),
        "ternary_w": np.ascontiguousarray(np.stack([tw1.T, tw2.reshape(C, FF1_CHUNKS, P).transpose(2, 1, 0).reshape(P, FF1)], 1)),
    }
    nc = bacc.Bacc("TRN2", target_bir_lowering=False, num_devices=1)
    args = [nc.dram_tensor(n, v.shape, mybir.dt.from_np(v.dtype), kind="ExternalInput").ap() for n, v in arrays.items()]
    out = nc.dram_tensor("out", (P, B, N_TOK), mybir.dt.float32, kind="ExternalOutput").ap()
    build(nc, *args, out)
    r = run_bass_kernel_spmd(nc, [arrays], core_ids=[0])
    got = np.asarray(r.results[0]["out"])
    return np.ascontiguousarray(got.reshape(C, B, TILES, P).transpose(1, 3, 2, 0).reshape(B, N_TOK, C))
```

```python
import concourse.bass as bass
from concourse import mybir
from contextlib import ExitStack
import numpy as np

P = 128
B, N_TOK, C = 2, 512, 128
CTX = 77
HEADS = 16
HEAD_DIM = C // HEADS
EXPERTS, FFN = 8, 256
TILES = N_TOK // P
CHUNKS_PER_EXPERT = FFN // P
CHUNKS = EXPERTS * CHUNKS_PER_EXPERT
FF1 = 4 * C
FF1_CHUNKS = FF1 // P
KV_COLS = C + HEADS
W2_LAG = 3
CATCH_UP = 11
WARM = [8, 8, 10, 6, 16, 4]
RAW = 4
FOCUS_EPS = 1e-6
LN_EPS = 1e-5

PACK = {}
_at = 0
for _name, _width in (("ctxT", B * CTX), ("Wkv0", 2 * C), ("Wq0", C), ("scale_bq", 2), ("ident", C),
                      ("Wkv1", 2 * C), ("Wq1T", C), ("WrT", EXPERTS), ("b1", FF1_CHUNKS), ("b2", 1),
                      ("kv_mask", KV_COLS), ("iota", EXPERTS)):
    PACK[_name] = (_at, _at + _width)
    _at += _width
PACK_COLS = _at
ROW_COLS = B * 2 * C


def build(nc, x, pack, rows, w1, w2, ternary_w, out):
    f32, f32r, u32 = mybir.dt.float32, mybir.dt.float32r, mybir.dt.uint32
    ALU, ACT, AX = mybir.AluOpType, mybir.ActivationFunctionType, mybir.AxisListType
    ctx = ExitStack()
    with ctx:
        def sb(name, shape, dt=f32):
            return ctx.enter_context(nc.sbuf_tensor(name, shape, dt))

        def sem(name):
            return ctx.enter_context(nc.semaphore(name))

        def bank(name):
            return ctx.enter_context(nc.psum_tensor(name, [P, 512], f32))

        def per_half(name, shape, dt=f32):
            return [sb(f"{name}_{h}", shape, dt) for h in range(B)]

        small = sb("small", [P, PACK_COLS])
        row_sb = sb("row_sb", [1, ROW_COLS])
        w1_raw = sb("w1_raw", [P, RAW, 2 * FFN])
        w2_raw = sb("w2_raw", [P, RAW, CHUNKS_PER_EXPERT, C])
        tw_raw = sb("tw_raw", [P, 2, FF1])
        x_in = per_half("x_in", [P, TILES, C])

        def packed(name):
            a, b = PACK[name]
            return small[:, a:b]

        ctxT, ident = packed("ctxT"), packed("ident")

        w1_hi = sb("w1_hi", [P, EXPERTS, 2 * FFN], f32r)
        w1_lo = sb("w1_lo", [P, EXPERTS, 2 * FFN], f32r)
        w2_hi = sb("w2_hi", [P, EXPERTS, CHUNKS_PER_EXPERT, C], f32r)
        w2_lo = sb("w2_lo", [P, EXPERTS, CHUNKS_PER_EXPERT, C], f32r)
        below = sb("below", [P, FF1])
        tern = sb("tern", [P, 2, FF1], f32r)
        select = sb("select", [2 * EXPERTS, EXPERTS, P], f32r)
        ones = sb("ones", [P, P])
        half_power = sb("half_power", [P, 4])
        neg_half_power = sb("neg_half_power", [P, 4])
        abs_sum = sb("abs_sum", [P, 2])
        t_scale = sb("t_scale", [P, 2])
        t_hi = sb("t_hi", [P, 2])
        t_lo = sb("t_lo", [P, 2])

        sp_abs = sb("sp_abs", [P, 1])
        sp_exp = sb("sp_exp", [P, 1])
        sp_ln = sb("sp_ln", [P, 1])
        sp = sb("sp", [P, 1])
        inv_sp = sb("inv_sp", [P, 1])
        inv_diag = sb("inv_diag", [P, C])
        eps_inv_sp = sb("eps_inv_sp", [P, 1])
        bq_inv_sp = sb("bq_inv_sp", [P, 1])
        k_act = sb("k_act", [CTX, B, C])
        k_div = sb("k_div", [CTX, B, C])
        k_sq = sb("k_sq", [CTX, B, C])
        k_cube = sb("k_cube", [CTX, B, C])
        k_six = sb("k_six", [CTX, B, C])
        k_sums = sb("k_sums", [CTX, 2, B])
        k_rec = sb("k_rec", [CTX, B])
        k_ratio = sb("k_ratio", [CTX, B])
        k_factor = sb("k_factor", [CTX, B])
        k_feat = sb("k_feat", [CTX, B, C])
        v_ones = sb("v_ones", [CTX, B, KV_COLS])
        kv_heads = sb("kv_heads", [P, B, KV_COLS])
        k1T = sb("k1T", [P, B * CTX])
        wq_k1T = sb("wq_k1T", [P, B * CTX])
        v1 = sb("v1", [CTX, B, C])

        LN = range(8)
        ln_stats = [sb(f"ln_stats_{i}", [P, TILES, 6]) for i in LN]
        ln_mv = [sb(f"ln_mv_{i}", [P, TILES, 2]) for i in LN]
        ln_var = [sb(f"ln_var_{i}", [P, TILES]) for i in LN]
        ln_rstd = [sb(f"ln_rstd_{i}", [P, TILES]) for i in LN]
        ln_out_ring = [sb(f"ln_out_{h}", [P, TILES, C]) for h in range(B)]
        ln_out = [ln_out_ring[i // 2 % B] for i in LN]
        xn1T = per_half("xn1T", [P, N_TOK])
        q_relu = [sb("q_relu", [P, N_TOK])] * B
        q_act = [sb("q_act", [P, N_TOK])] * B
        q_sq = per_half("q_sq", [P, N_TOK])
        q_cube = per_half("q_cube", [P, N_TOK])
        q_six = per_half("q_six", [P, N_TOK])
        q_rec = per_half("q_rec", [P, TILES])
        q_ratio = per_half("q_ratio", [P, TILES])
        q_inv = per_half("q_inv", [P, TILES])
        q_inv_eps = per_half("q_inv_eps", [P, TILES])
        den = per_half("den", [P, TILES, HEADS])
        inv_den = per_half("inv_den", [P, TILES, HEADS])
        att0 = [sb("att0", [P, TILES, C])] * B
        x1 = x_in
        xn2T = sb("xn2T", [P, N_TOK])
        xn2_hi = per_half("xn2_hi", [P, N_TOK], f32r)
        xn2_lo = per_half("xn2_lo", [P, N_TOK], f32r)
        top8 = per_half("top8", [P, TILES, 8])
        top8_at = per_half("top8_at", [P, TILES, 8], u32)
        gap = per_half("gap", [P, TILES])
        gap_tanh = per_half("gap_tanh", [P, TILES])
        top_w = per_half("top_w", [P, 2, TILES])
        pick = per_half("pick", [P, 2, TILES, EXPERTS])
        pick_w = per_half("pick_w", [P, 2, TILES, EXPERTS])
        route = per_half("route", [P, TILES, EXPERTS])
        route_hl = per_half("route_hl", [P, TILES, 2 * EXPERTS], f32r)
        routeT = per_half("routeT", [2 * EXPERTS, N_TOK], f32r)
        moeT = [sb("moeT", [P, N_TOK])] * B
        x2 = per_half("x2", [P, TILES, C])
        xn3T = [sb("xn3T", [P, N_TOK])] * B
        s_max = per_half("s_max", [P, TILES])
        s_shift = [sb("s_shift", [P, TILES, CTX])] * B
        s_exp = per_half("s_exp", [P, TILES, CTX])
        s_sum = per_half("s_sum", [P, TILES])
        s_inv = per_half("s_inv", [P, TILES])
        probsT = [sb("probsT", [CTX, N_TOK])] * B
        x3 = x1
        xn4_hi = per_half("xn4_hi", [P, N_TOK], f32r)
        xn4_lo = per_half("xn4_lo", [P, N_TOK], f32r)
        yT = q_six

        SG, SW, AB, HL = 3, 3, 3, 4
        silu_g = [sb(f"silu_g_{i}", [P, N_TOK]) for i in range(SG)]
        gated = [sb(f"gated_{i}", [P, N_TOK]) for i in range(SW)]
        hid = [sb(f"hid_{i}", [P, N_TOK]) for i in range(AB)]
        hid_hi = [sb(f"hid_hi_{i}", [P, N_TOK], f32r) for i in range(HL)]
        hid_lo = [sb(f"hid_lo_{i}", [P, N_TOK], f32r) for i in range(HL)]
        route_b = [sb(f"route_b_{i}", [P, N_TOK]) for i in range(2)]
        gelu = [q_relu[0], q_act[0], q_sq[0], q_sq[1]]
        gelu_hi, gelu_lo = hid_hi, hid_lo

        gate_ps = [bank("gate_ps_0"), bank("gate_ps_1")]
        val_ps = [bank("val_ps_0"), bank("val_ps_1")]
        acc_ps = bank("acc_ps")
        spread_ps = bank("spread_ps")
        side0 = bank("side0")
        side1 = bank("side1")
        y_ps = [spread_ps, side0]
        layer1_ps = [side0, acc_ps]
        q_ps = [side1, gate_ps[1]]
        ff_ps = [gate_ps[0], gate_ps[1], val_ps[0], val_ps[1]]

        small_in, rows_in, tw_in = sem("small_in"), sem("rows_in"), sem("tw_in")
        x_loaded = [sem(f"x_loaded_{h}") for h in range(B)]
        w1_in = [sem(f"w1_in_{e}") for e in range(EXPERTS)]
        w2_in = [sem(f"w2_in_{e}") for e in range(EXPERTS)]
        ones_set, powers_set, v_ones_set = sem("ones_set"), sem("powers_set"), sem("v_ones_set")
        inv_diag_ready, inv_row_ps_ready = sem("inv_diag_ready"), sem("inv_row_ps_ready")
        sp_ln_ready, sp_ready = sem("sp_ln_ready"), sem("sp_ready")
        kv_ps_ready, kv_read = sem("kv_ps_ready"), sem("kv_read")
        k_div_ready, k_sq_ready, k_cube_ready, k_six_ready = (
            sem("k_div_ready"), sem("k_sq_ready"), sem("k_cube_ready"), sem("k_six_ready"))
        k_ratio_ready, k_factor_ready, k_feat_ready = (
            sem("k_ratio_ready"), sem("k_factor_ready"), sem("k_feat_ready"))
        kvh_ps_ready, kvh_ready = sem("kvh_ps_ready"), sem("kvh_ready")
        k1T_ps_ready, k1T_ready = sem("k1T_ps_ready"), sem("k1T_ready")
        wqk_ps_ready, wqk_ready = sem("wqk_ps_ready"), sem("wqk_ready")
        v1_ps_ready, v1_ready = sem("v1_ps_ready"), sem("v1_ready")
        abs_ready, abs_ps_ready, tern_ready, select_ready = (
            sem("abs_ready"), sem("abs_ps_ready"), sem("tern_ready"), sem("select_ready"))
        w_hi_ready, w_lo_ready = sem("w_hi_ready"), sem("w_lo_ready")
        var_ready, rstd_ready, ln_ready, lnT_ps_ready = (
            [sem(f"{name}_{i}") for i in LN] for name in ("var_ready", "rstd_ready", "ln_ready", "lnT_ps_ready"))
        xn1T_ready, q_ps_ready, q_relu_ready, q_act_ready = (
            sem("xn1T_ready"), sem("q_ps_ready"), sem("q_relu_ready"), sem("q_act_ready"))
        q_sq_ready, q_cube_ready, q_six_ready = (
            sem("q_sq_ready"), sem("q_cube_ready"), sem("q_six_ready"))
        att0_ps_ready, q_ratio_ready, q_inv_ready, att0_read = (
            sem("att0_ps_ready"), sem("q_ratio_ready"), sem("q_inv_ready"), sem("att0_read"))
        xn2_hi_ready, xn2T_ready, xn2_lo_ready = sem("xn2_hi_ready"), sem("xn2T_ready"), sem("xn2_lo_ready")
        logits_ready, logits_read, gap_ready, gap_tanh_ready = (
            sem("logits_ready"), sem("logits_read"), sem("gap_ready"), sem("gap_tanh_ready"))
        route_ready, routeT_ps_ready, routeT_ready = (
            sem("route_ready"), sem("routeT_ps_ready"), sem("routeT_ready"))
        spread_ready, route_b_ready = sem("spread_ready"), sem("route_b_ready")
        gate_ready, val_ready = sem("gate_ready"), sem("val_ready")
        silu_ready, gated_ready, hid_ready = sem("silu_ready"), sem("gated_ready"), sem("hid_ready")
        hid_hi_ready, hid_lo_ready, w2_done = sem("hid_hi_ready"), sem("hid_lo_ready"), sem("w2_done")
        acc_ready, moeT_ready, moe_ps_ready, x2_ready = (
            sem("acc_ready"), sem("moeT_ready"), sem("moe_ps_ready"), sem("x2_ready"))
        xn3T_ready, score_ps_ready, s_shift_ready, s_exp_ready = (
            sem("xn3T_ready"), sem("score_ps_ready"), sem("s_shift_ready"), sem("s_exp_ready"))
        probsT_ps_ready, probsT_ready = sem("probsT_ps_ready"), sem("probsT_ready")
        att1_ps_ready, x3_ready = sem("att1_ps_ready"), sem("x3_ready")
        xn4_hi_ready, xn4_lo_ready = sem("xn4_hi_ready"), sem("xn4_lo_ready")
        ff_ps_ready, gelu_ready, gelu_hi_ready, gelu_lo_ready = (
            sem("ff_ps_ready"), sem("gelu_ready"), sem("gelu_hi_ready"), sem("gelu_lo_ready"))
        y_ps_ready, y_ready, y_stored = sem("y_ps_ready"), sem("y_ready"), sem("y_stored")
        dve_chain, act_chain, pool_chain = sem("dve_chain"), sem("act_chain"), sem("pool_chain")

        def ln_index(layer, h, which):
            return 4 * layer + 2 * h + which

        block = ctx.enter_context(nc.Block())

        @block.sync
        def _(sp_q):
            sp_q.dma_start(x_in[0][:, :, :], x[0].rearrange("(p t) c -> p t c", t=TILES)).then_inc(x_loaded[0], 16)
            sp_q.dma_start(row_sb[:, :], rows).then_inc(rows_in, 16)
            sp_q.dma_start(small[:, :], pack).then_inc(small_in, 16)
            sp_q.dma_start(x_in[1][:, :, :], x[1].rearrange("(p t) c -> p t c", t=TILES)).then_inc(x_loaded[1], 16)
            for e in range(EXPERTS):
                if e >= RAW:
                    sp_q.wait_ge(w_lo_ready, 2 * (e - RAW) + 2)
                sp_q.dma_start(w1_raw[:, e % RAW, :], w1[:, e, :]).then_inc(w1_in[e], 16)
                sp_q.dma_start(w2_raw[:, e % RAW, :, :], w2[:, e, :, :]).then_inc(w2_in[e], 16)
                if e == RAW - 1:
                    sp_q.dma_start(tw_raw[:, :, :], ternary_w).then_inc(tw_in, 16)
            for h in range(B):
                sp_q.wait_ge(y_ready, h + 1)
                sp_q.dma_start(out[:, h, :], yT[h][:, :]).then_inc(y_stored, 16)
            sp_q.wait_ge(y_stored, 16 * B)

        @block.gpsimd
        def _(pool):
            nc.gpsimd.memset(ones[:, :], 1.0).then_inc(ones_set, 1)
            nc.gpsimd.memset(half_power[:, :], 0.5).then_inc(powers_set, 1)
            nc.gpsimd.memset(neg_half_power[:, :], -0.5).then_inc(powers_set, 1)
            nc.gpsimd.memset(v_ones[:, :, C:KV_COLS], 1.0).then_inc(v_ones_set, 1)
            pool.wait_ge(powers_set, 2)

            def rstd(i):
                pool.wait_ge(var_ready[i], 1)
                nc.gpsimd.tensor_tensor(ln_rstd[i][:, :], ln_var[i][:, :], neg_half_power[:, 0:TILES],
                                        ALU.pow).then_inc(rstd_ready[i], 1)

            def k_root():
                pool.wait_ge(k_ratio_ready, 1)
                nc.gpsimd.tensor_tensor(k_factor[:, :], k_ratio[:, :], half_power[0:CTX, 0:B],
                                        ALU.pow).then_inc(k_factor_ready, 1)

            def q_root(h):
                pool.wait_ge(q_ratio_ready, h + 1)
                nc.gpsimd.tensor_tensor(q_inv[h][:, :], q_ratio[h][:, :], half_power[:, 0:TILES],
                                        ALU.pow).then_inc(q_inv_ready, 1)

            def w1_rest(e):
                pool.wait_ge(w_hi_ready, 2 * e + 1)
                nc.gpsimd.tensor_tensor(w1_lo[:, e, :], w1_raw[:, e % RAW, :], w1_hi[:, e, :].bitcast(f32),
                                        ALU.subtract).then_inc(w_lo_ready, 1)

            def w2_rest(e):
                pool.wait_ge(w_hi_ready, 2 * e + 2)
                nc.gpsimd.tensor_tensor(w2_lo[:, e, :, :], w2_raw[:, e % RAW, :, :], w2_hi[:, e, :, :].bitcast(f32),
                                        ALU.subtract).then_inc(w_lo_ready, 1)

            def weigh(n):
                pool.wait_ge(gated_ready, n + 1)
                pool.wait_ge(route_b_ready, n // CHUNKS_PER_EXPERT + 1)
                if n >= AB:
                    pool.wait_ge(hid_lo_ready, n - AB + 1)
                nc.gpsimd.tensor_tensor(hid[n % AB][:, :], gated[n % SW][:, :],
                                        route_b[(n // CHUNKS_PER_EXPERT) % 2][:, :],
                                        ALU.mult).then_inc(hid_ready, 1)

            def ff_round(h, c):
                k = FF1_CHUNKS * h + c
                pool.wait_ge(gelu_ready, k + 1)
                if h:
                    pool.wait_ge(y_ps_ready, h)
                else:
                    pool.wait_ge(w2_done, B * CHUNKS - HL + c + 1)
                nc.gpsimd.tensor_scalar(gelu_hi[c][:, :], gelu[c][:, :], 1.0, 0.0, ALU.mult, ALU.add).then_inc(gelu_hi_ready, 1)

            rstd(ln_index(0, 0, 0))
            w1_rest(0)
            w2_rest(0)
            k_root()
            w1_rest(1)
            w2_rest(1)
            rstd(ln_index(0, 1, 0))
            w1_rest(2)
            w2_rest(2)
            q_root(0)
            w1_rest(3)
            w2_rest(3)
            w1_rest(4)
            rstd(ln_index(0, 0, 1))
            w2_rest(4)
            for e in range(5, 8):
                w1_rest(e)
                w2_rest(e)
            for n in range(B * CHUNKS):
                weigh(n)
                if n == 1:
                    q_root(1)
                if n == 4:
                    rstd(ln_index(0, 1, 1))
                if n == 21:
                    rstd(ln_index(1, 0, 0))
            rstd(ln_index(1, 0, 1))
            rstd(ln_index(1, 1, 0))
            for c in range(FF1_CHUNKS):
                ff_round(0, c)
            rstd(ln_index(1, 1, 1))
            for c in range(FF1_CHUNKS):
                ff_round(1, c)

        @block.scalar
        def _(act):
            def w_hi(e):
                act.wait_ge(w1_in[e], 16)
                nc.scalar.activation(w1_hi[:, e, :], w1_raw[:, e % RAW, :], ACT.Copy).then_inc(w_hi_ready, 1)
                act.wait_ge(w2_in[e], 16)
                nc.scalar.activation(w2_hi[:, e, :, :], w2_raw[:, e % RAW, :, :], ACT.Copy).then_inc(w_hi_ready, 1)

            def softplus():
                act.wait_ge(small_in, 16)
                a, _b = PACK["scale_bq"]
                nc.scalar.activation(sp_abs[:, :], small[:, a:a + 1], ACT.Abs).then_inc(act_chain, 1)
                act.wait_ge(act_chain, 1)
                nc.scalar.activation(sp_exp[:, :], sp_abs[:, :], ACT.Exp, scale=-1.0).then_inc(act_chain, 1)
                act.wait_ge(act_chain, 2)
                nc.scalar.activation(sp_ln[:, :], sp_exp[:, :], ACT.Ln, bias=1.0).then_inc(sp_ln_ready, 1)

            def k_squares(src, dst, ready, row, done):
                act.wait_ge(ready, 1)
                for b in range(B):
                    nc.scalar.activation(dst[:, b, :], src[:, b, :], ACT.Square,
                                         accum_out=k_sums[:, row, b:b + 1]).then_inc(done, 1)

            def ctx1_reads():
                act.wait_ge(k1T_ps_ready, 1)
                nc.scalar.activation(k1T[:, :], val_ps[0][:, 0:B * CTX], ACT.Copy).then_inc(k1T_ready, 1)
                act.wait_ge(v1_ps_ready, 1)
                nc.scalar.activation(v1[:, :, :], val_ps[1][0:CTX, 0:B * C].rearrange("p (b c) -> p b c", b=B),
                                     ACT.Copy).then_inc(v1_ready, 1)

            def wqk_read():
                act.wait_ge(wqk_ps_ready, 1)
                nc.scalar.activation(wq_k1T[:, :], val_ps[0][:, 0:B * CTX], ACT.Copy).then_inc(wqk_ready, 1)

            def abs_sums():
                act.wait_ge(tw_in, 16)
                for i in range(2):
                    if i:
                        act.wait_ge(abs_ready, i)
                    nc.scalar.activation(below[:, :], tw_raw[:, i, :], ACT.Abs,
                                         accum_out=abs_sum[:, i:i + 1]).then_inc(abs_ready, 1)

            def copy_T(dst, src, i, done):
                act.wait_ge(lnT_ps_ready[i], 1)
                nc.scalar.activation(dst[:, :], src[:, :], ACT.Copy).then_inc(done, 1)

            def q_first(h):
                act.wait_ge(q_ps_ready, h + 1)
                act.wait_ge(sp_ready, 1)
                nc.scalar.activation(q_relu[h][:, :], q_ps[h][:, :], ACT.Relu, bias=bq_inv_sp[:, :],
                                     scale=inv_sp[:, :]).then_inc(q_relu_ready, 1)

            def q_square(h):
                act.wait_ge(q_act_ready, h + 1)
                nc.scalar.activation(q_sq[h][:, :], q_act[h][:, :], ACT.Square).then_inc(q_sq_ready, 1)

            def q_sixth(h):
                act.wait_ge(q_cube_ready, h + 1)
                nc.scalar.activation(q_six[h][:, :], q_cube[h][:, :], ACT.Square).then_inc(q_six_ready, 1)

            def xn2_columns(h):
                if h:
                    act.wait_ge(xn2_lo_ready, h)
                    act.wait_ge(logits_ready, h)
                copy_T(xn2T, side0, ln_index(0, h, 1), xn2T_ready)
                nc.scalar.activation(xn2_hi[h][:, :], side0[:, :], ACT.Copy).then_inc(xn2_hi_ready, 1)

            def route_tanh(h):
                act.wait_ge(gap_ready, h + 1)
                nc.scalar.activation(gap_tanh[h][:, :], gap[h][:, :], ACT.Tanh, scale=0.5).then_inc(gap_tanh_ready, 1)

            def silu(n):
                act.wait_ge(gate_ready, n + 1)
                if n >= SG:
                    act.wait_ge(gated_ready, n - SG + 1)
                nc.scalar.activation(silu_g[n % SG][:, :], gate_ps[n % 2][:, :], ACT.Silu).then_inc(silu_ready, 1)

            def read_spread(g):
                act.wait_ge(spread_ready, g + 1)
                if g >= 2:
                    act.wait_ge(hid_ready, CHUNKS_PER_EXPERT * (g - 1))
                nc.scalar.activation(route_b[g % 2][:, :], spread_ps[:, :], ACT.Copy).then_inc(route_b_ready, 1)

            def hid_round(n):
                act.wait_ge(hid_ready, n + 1)
                if n >= HL:
                    act.wait_ge(w2_done, n - HL + 1)
                nc.scalar.activation(hid_hi[n % HL][:, :], hid[n % AB][:, :], ACT.Copy).then_inc(hid_hi_ready, 1)

            def read_acc(h):
                act.wait_ge(acc_ready, h + 1)
                nc.scalar.activation(moeT[h][:, :], acc_ps[:, :], ACT.Copy).then_inc(moeT_ready, 1)

            def softmax_exp(h):
                act.wait_ge(s_shift_ready, h + 1)
                nc.scalar.activation(s_exp[h][:, :, :], s_shift[h][:, :, :], ACT.Exp,
                                     scale=float(1.0 / np.sqrt(C))).then_inc(s_exp_ready, 1)

            def read_probsT(h):
                act.wait_ge(probsT_ps_ready, h + 1)
                nc.scalar.activation(probsT[h][:, :], side1[0:CTX, :], ACT.Copy).then_inc(probsT_ready, 1)

            def ff_gelu(h, c):
                k = FF1_CHUNKS * h + c
                act.wait_ge(ff_ps_ready, k + 1)
                if h:
                    act.wait_ge(gelu_lo_ready, k - FF1_CHUNKS + 1)
                a, _b = PACK["b1"]
                nc.scalar.activation(gelu[c][:, :], ff_ps[c][:, :], ACT.Gelu,
                                     bias=small[:, a + c:a + c + 1]).then_inc(gelu_ready, 1)

            def finish(h):
                act.wait_ge(y_ps_ready, h + 1)
                a, b = PACK["b2"]
                nc.scalar.activation(yT[h][:, :], y_ps[h][:, :], ACT.Identity, bias=small[:, a:b]).then_inc(y_ready, 1)

            nc.scalar.preload_act_table_set("natural_log_exp_and_others")
            softplus()
            w_hi(0)
            copy_T(xn1T[0], side0, ln_index(0, 0, 0), xn1T_ready)
            k_squares(k_div, k_sq, k_div_ready, 0, k_sq_ready)
            q_first(0)
            k_squares(k_cube, k_six, k_cube_ready, 1, k_six_ready)
            q_square(0)
            w_hi(1)
            q_sixth(0)
            ctx1_reads()
            w_hi(2)
            w_hi(3)
            copy_T(xn1T[1], spread_ps, ln_index(0, 1, 0), xn1T_ready)
            q_first(1)
            wqk_read()
            q_square(1)
            w_hi(4)
            q_sixth(1)
            w_hi(5)
            w_hi(6)
            xn2_columns(0)
            w_hi(7)
            route_tanh(0)
            for n in range(B * CHUNKS):
                silu(n)
                if n == 2:
                    read_spread(0)
                if n == 3:
                    read_spread(1)
                if n % CHUNKS_PER_EXPERT == 0 and n >= 4:
                    read_spread(n // CHUNKS_PER_EXPERT)
                if n >= 2:
                    hid_round(n - 2)
                if n == 7:
                    xn2_columns(1)
                if n == 11:
                    route_tanh(1)
                if n == 12:
                    abs_sums()
                if n == 19:
                    read_acc(0)
                if n == 24:
                    copy_T(xn3T[0], side1, ln_index(1, 0, 0), xn3T_ready)
            hid_round(B * CHUNKS - 2)
            softmax_exp(0)
            hid_round(B * CHUNKS - 1)
            read_probsT(0)
            read_acc(1)
            copy_T(xn4_hi[0], side0, ln_index(1, 0, 1), xn4_hi_ready)
            copy_T(xn3T[1], side1, ln_index(1, 1, 0), xn3T_ready)
            softmax_exp(1)
            for c in range(FF1_CHUNKS):
                ff_gelu(0, c)
            read_probsT(1)
            finish(0)
            copy_T(xn4_hi[1], acc_ps, ln_index(1, 1, 1), xn4_hi_ready)
            for c in range(FF1_CHUNKS):
                ff_gelu(1, c)
            finish(1)

        @block.vector
        def _(dve):
            links = [0]

            def link(ins):
                links[0] += 1
                ins.then_inc(dve_chain, 1)
                dve.wait_ge(dve_chain, links[0])

            def ln_begin(src, i):
                for t in range(TILES):
                    last = nc.vector.bn_stats(ln_stats[i][:, t, :], src[:, t, :])
                link(last)
                for t in range(TILES):
                    last = nc.vector.bn_aggr(ln_mv[i][:, t, :], ln_stats[i][:, t, :])
                link(last)
                nc.vector.tensor_scalar(ln_var[i][:, :], ln_mv[i][:, :, 1], LN_EPS, None, ALU.add).then_inc(var_ready[i], 1)

            def ln_end(src, i):
                dve.wait_ge(rstd_ready[i], 1)
                for t in range(TILES):
                    nc.vector.tensor_scalar(ln_out[i][:, t, :], src[:, t, :], ln_mv[i][:, t, 0:1],
                                            ln_rstd[i][:, t:t + 1], ALU.subtract, ALU.mult).then_inc(ln_ready[i], 1)

            def softplus_end():
                dve.wait_ge(small_in, 16)
                dve.wait_ge(sp_ln_ready, 1)
                a, b = PACK["scale_bq"]
                link(nc.vector.scalar_tensor_tensor(out=sp[:, :], in0=small[:, a:a + 1], scalar=0.0, in1=sp_ln[:, :],
                                                    op0=ALU.max, op1=ALU.add))
                link(nc.vector.reciprocal(inv_sp[:, :], sp[:, :]))
                nc.vector.tensor_scalar(inv_diag[:, :], ident, inv_sp[:, :], None, ALU.mult).then_inc(inv_diag_ready, 1)
                nc.vector.tensor_scalar(eps_inv_sp[:, :], inv_sp[:, :], FOCUS_EPS, None, ALU.mult)
                nc.vector.tensor_tensor(bq_inv_sp[:, :], inv_sp[:, :], small[:, a + 1:b], ALU.mult).then_inc(sp_ready, 1)

            def keys_first():
                dve.wait_ge(kv_ps_ready, 1)
                kv = gate_ps[0][0:CTX, :].rearrange("p (b k c) -> p b k c", b=B, k=2)
                link(nc.vector.tensor_scalar(k_act[:, :, :], kv[:, :, 0, :], 0.0, FOCUS_EPS, ALU.max, ALU.add))
                dve.wait_ge(inv_row_ps_ready, 1)
                nc.vector.tensor_tensor(k_div[:, :, :], k_act[:, :, :],
                                        gate_ps[1][0:CTX, 0:C].unsqueeze(1).broadcast_to([CTX, B, C]),
                                        ALU.mult).then_inc(k_div_ready, 1)
                nc.vector.tensor_copy(v_ones[:, :, 0:C], kv[:, :, 1, :]).then_inc(kv_read, 1)

            def keys_cube():
                dve.wait_ge(k_sq_ready, B)
                nc.vector.tensor_tensor(k_cube[:, :, :], k_sq[:, :, :], k_div[:, :, :], ALU.mult).then_inc(k_cube_ready, 1)

            def keys_ratio():
                dve.wait_ge(k_six_ready, B)
                link(nc.vector.reciprocal(k_rec[:, :], k_sums[:, 1, :]))
                nc.vector.tensor_tensor(k_ratio[:, :], k_sums[:, 0, :], k_rec[:, :], ALU.mult).then_inc(k_ratio_ready, 1)

            def keys_end():
                dve.wait_ge(k_factor_ready, 1)
                for b in range(B):
                    last = nc.vector.tensor_scalar(k_feat[:, b, :], k_cube[:, b, :], k_factor[:, b:b + 1], None, ALU.mult)
                last.then_inc(k_feat_ready, 1)

            def kv_mask():
                dve.wait_ge(kvh_ps_ready, 1)
                nc.vector.tensor_tensor(kv_heads[:, :, :],
                                        acc_ps[:, 0:B * KV_COLS].rearrange("p (b c) -> p b c", b=B),
                                        packed("kv_mask").unsqueeze(1).broadcast_to([P, B, KV_COLS]),
                                        ALU.mult).then_inc(kvh_ready, 1)

            def select_round():
                nc.vector.tensor_tensor(select[:, :, :],
                                        ident[0:2 * EXPERTS, 0:EXPERTS].unsqueeze(2).broadcast_to([2 * EXPERTS, EXPERTS, P]),
                                        ident[0:2 * EXPERTS, EXPERTS:2 * EXPERTS].unsqueeze(2).broadcast_to([2 * EXPERTS, EXPERTS, P]),
                                        ALU.add).then_inc(select_ready, 1)

            def q_second(h):
                dve.wait_ge(q_relu_ready, h + 1)
                nc.vector.tensor_scalar(q_act[h][:, :], q_relu[h][:, :], eps_inv_sp[:, :], None, ALU.add).then_inc(q_act_ready, 1)

            def q_third(h):
                dve.wait_ge(q_sq_ready, h + 1)
                nc.vector.tensor_tensor(q_cube[h][:, :], q_sq[h][:, :], q_act[h][:, :], ALU.mult).then_inc(q_cube_ready, 1)

            def att0_begin(h):
                dve.wait_ge(att0_ps_ready, h + 1)
                link(nc.vector.reciprocal(q_rec[h][:, :], side0[:, 0:TILES]))
                nc.vector.tensor_tensor(q_ratio[h][:, :], side0[:, TILES:2 * TILES], q_rec[h][:, :],
                                        ALU.mult).then_inc(q_ratio_ready, 1)

            def att0_end(h):
                dve.wait_ge(q_inv_ready, h + 1)
                link(nc.vector.tensor_scalar(q_inv_eps[h][:, :], q_inv[h][:, :], FOCUS_EPS, None, ALU.mult))
                for i, ps in enumerate((side0[:, P:P + 2 * KV_COLS], side1[:, 0:2 * KV_COLS])):
                    nd = ps.rearrange("p (t c) -> p t c", t=2)
                    last = nc.vector.tensor_tensor(den[h][:, 2 * i:2 * i + 2, :], nd[:, :, C:KV_COLS],
                                                   q_inv_eps[h][:, 2 * i:2 * i + 2].unsqueeze(2).broadcast_to([P, 2, HEADS]),
                                                   ALU.add)
                link(last)
                link(nc.vector.reciprocal(inv_den[h][:, :, :], den[h][:, :, :]))
                for i, ps in enumerate((side0[:, P:P + 2 * KV_COLS], side1[:, 0:2 * KV_COLS])):
                    nd = ps.rearrange("p (t c) -> p t c", t=2)[:, :, 0:C]
                    last = nc.vector.tensor_tensor(
                        att0[h][:, 2 * i:2 * i + 2, :].rearrange("p t (g d) -> p t g d", g=HEADS),
                        nd.rearrange("p t (g d) -> p t g d", g=HEADS),
                        inv_den[h][:, 2 * i:2 * i + 2, :].unsqueeze(3).broadcast_to([P, 2, HEADS, HEAD_DIM]),
                        ALU.mult)
                last.then_inc(att0_read, 1)
                dve.wait_ge(att0_read, h + 1)
                link(nc.vector.tensor_tensor(x1[h][:, :, :], x_in[h][:, :, :], att0[h][:, :, :], ALU.add))

            def xn2_rest(h):
                dve.wait_ge(xn2T_ready, h + 1)
                dve.wait_ge(xn2_hi_ready, h + 1)
                nc.vector.tensor_tensor(xn2_lo[h][:, :], xn2T[:, :], xn2_hi[h][:, :].bitcast(f32),
                                        ALU.subtract).then_inc(xn2_lo_ready, 1)

            def route_top(h):
                dve.wait_ge(logits_ready, h + 1)
                lg = side1[:, 0:TILES * EXPERTS].rearrange("p (t e) -> p t e", t=TILES)
                for t in range(TILES):
                    last = nc.vector.max(top8[h][:, t, :], lg[:, t, :])
                link(last)
                nc.vector.tensor_tensor(gap[h][:, :], top8[h][:, :, 0], top8[h][:, :, 1], ALU.subtract).then_inc(gap_ready, 1)
                for t in range(TILES):
                    last = nc.vector.max_index(top8_at[h][:, t, :], top8[h][:, t, :], lg[:, t, :])
                last.then_inc(logits_read, 1)

            def route_weights(h):
                dve.wait_ge(gap_tanh_ready, h + 1)
                dve.wait_ge(logits_read, h + 1)
                nc.vector.tensor_scalar(top_w[h][:, 0, :], gap_tanh[h][:, :], 0.5, 0.5, ALU.mult, ALU.add)
                nc.vector.tensor_scalar(top_w[h][:, 1, :], gap_tanh[h][:, :], -0.5, 0.5, ALU.mult, ALU.add)
                for k in range(2):
                    last = nc.vector.tensor_tensor(pick[h][:, k, :, :],
                                                   packed("iota").unsqueeze(1).broadcast_to([P, TILES, EXPERTS]),
                                                   top8_at[h][:, :, k:k + 1].broadcast_to([P, TILES, EXPERTS]),
                                                   ALU.is_equal)
                link(last)
                for k in range(2):
                    last = nc.vector.tensor_tensor(pick_w[h][:, k, :, :], pick[h][:, k, :, :],
                                                   top_w[h][:, k, :].unsqueeze(2).broadcast_to([P, TILES, EXPERTS]),
                                                   ALU.mult)
                link(last)
                link(nc.vector.tensor_tensor(route[h][:, :, :], pick_w[h][:, 0, :, :], pick_w[h][:, 1, :, :], ALU.add))
                link(nc.vector.tensor_copy(route_hl[h][:, :, 0:EXPERTS], route[h][:, :, :]))
                nc.vector.tensor_tensor(route_hl[h][:, :, EXPERTS:2 * EXPERTS], route[h][:, :, :],
                                        route_hl[h][:, :, 0:EXPERTS].bitcast(f32), ALU.subtract).then_inc(route_ready, 1)

            def route_T(h):
                dve.wait_ge(routeT_ps_ready, h + 1)
                nc.vector.tensor_copy(routeT[h][:, :], side1[0:2 * EXPERTS, :]).then_inc(routeT_ready, 1)

            def hidden(n):
                dve.wait_ge(val_ready, n + 1)
                dve.wait_ge(silu_ready, n + 1)
                if n >= SW:
                    dve.wait_ge(hid_ready, n - SW + 1)
                nc.vector.tensor_tensor(gated[n % SW][:, :], val_ps[n % 2][:, :], silu_g[n % SG][:, :],
                                        ALU.mult).then_inc(gated_ready, 1)

            def hidden_rest(n):
                dve.wait_ge(hid_hi_ready, n + 1)
                if n >= HL:
                    dve.wait_ge(w2_done, n - HL + 1)
                nc.vector.tensor_tensor(hid_lo[n % HL][:, :], hid[n % AB][:, :], hid_hi[n % HL][:, :].bitcast(f32),
                                        ALU.subtract).then_inc(hid_lo_ready, 1)

            def thresholds():
                dve.wait_ge(abs_ps_ready, 1)
                link(nc.vector.tensor_scalar(t_scale[:, :], side0[:, 0:2], 1.0 / (FF1 * C), 1e-8, ALU.mult, ALU.max))
                nc.vector.tensor_scalar(t_hi[:, :], t_scale[:, :], 0.5, None, ALU.mult)
                link(nc.vector.tensor_scalar(t_lo[:, :], t_scale[:, :], -0.5, None, ALU.mult))

            def ternary(i):
                if i:
                    dve.wait_ge(tern_ready, i)
                link(nc.vector.tensor_scalar(below[:, :], tw_raw[:, i, :], t_lo[:, i:i + 1], None, ALU.is_lt))
                nc.vector.scalar_tensor_tensor(out=tern[:, i, :], in0=tw_raw[:, i, :], scalar=t_hi[:, i:i + 1],
                                               in1=below[:, :], op0=ALU.is_gt, op1=ALU.subtract).then_inc(tern_ready, 1)

            def add_moe(h):
                dve.wait_ge(moe_ps_ready, h + 1)
                nc.vector.tensor_tensor(x2[h][:, :, :], layer1_ps[h][:, :].rearrange("p (t c) -> p t c", t=TILES),
                                        x1[h][:, :, :], ALU.add).then_inc(x2_ready, 1)
                dve.wait_ge(x2_ready, h + 1)

            def softmax_shift(h):
                dve.wait_ge(score_ps_ready, h + 1)
                sc = layer1_ps[h][:, 0:TILES * CTX].rearrange("p (t k) -> p t k", t=TILES)
                link(nc.vector.tensor_reduce(s_max[h][:, :], sc, AX.X, ALU.max))
                nc.vector.tensor_tensor(s_shift[h][:, :, :], sc, s_max[h][:, :].unsqueeze(2).broadcast_to([P, TILES, CTX]),
                                        ALU.subtract).then_inc(s_shift_ready, 1)

            def softmax_sum(h):
                dve.wait_ge(s_exp_ready, h + 1)
                link(nc.vector.tensor_reduce(s_sum[h][:, :], s_exp[h][:, :, :], AX.X, ALU.add))
                link(nc.vector.reciprocal(s_inv[h][:, :], s_sum[h][:, :]))

            def add_att1(h):
                dve.wait_ge(att1_ps_ready, h + 1)
                for t in range(TILES):
                    nc.vector.scalar_tensor_tensor(out=x3[h][:, t, :], in0=layer1_ps[h][:, t * P:(t + 1) * P],
                                                   scalar=s_inv[h][:, t:t + 1], in1=x2[h][:, t, :],
                                                   op0=ALU.mult, op1=ALU.add).then_inc(x3_ready, 1)
                dve.wait_ge(x3_ready, TILES * (h + 1))

            def xn4_rest(h):
                dve.wait_ge(xn4_hi_ready, h + 1)
                nc.vector.tensor_tensor(xn4_lo[h][:, :], layer1_ps[h][:, :], xn4_hi[h][:, :].bitcast(f32),
                                        ALU.subtract).then_inc(xn4_lo_ready, 1)

            def ff_rest(h, c):
                k = FF1_CHUNKS * h + c
                dve.wait_ge(gelu_hi_ready, k + 1)
                nc.vector.tensor_tensor(gelu_lo[c][:, :], gelu[c][:, :], gelu_hi[c][:, :].bitcast(f32),
                                        ALU.subtract).then_inc(gelu_lo_ready, 1)

            dve.wait_ge(x_loaded[0], 16)
            ln_begin(x_in[0], ln_index(0, 0, 0))
            ln_end(x_in[0], ln_index(0, 0, 0))
            softplus_end()
            keys_first()
            keys_cube()
            dve.wait_ge(x_loaded[1], 16)
            ln_begin(x_in[1], ln_index(0, 1, 0))
            q_second(0)
            keys_ratio()
            q_third(0)
            keys_end()
            kv_mask()
            ln_end(x_in[1], ln_index(0, 1, 0))
            select_round()
            att0_begin(0)
            q_second(1)
            att0_end(0)
            ln_begin(x1[0], ln_index(0, 0, 1))
            q_third(1)
            ln_end(x1[0], ln_index(0, 0, 1))
            xn2_rest(0)
            route_top(0)
            route_weights(0)
            for n in range(B * CHUNKS):
                hidden(n)
                if n == 0:
                    route_T(0)
                if n >= 2:
                    hidden_rest(n - 2)
                if n == 3:
                    att0_begin(1)
                if n == 4:
                    att0_end(1)
                    ln_begin(x1[1], ln_index(0, 1, 1))
                if n == 5:
                    ln_end(x1[1], ln_index(0, 1, 1))
                if n == 8:
                    xn2_rest(1)
                if n == 10:
                    route_top(1)
                if n == 11:
                    route_weights(1)
                if n == 13:
                    route_T(1)
                if n == 14:
                    thresholds()
                    ternary(0)
                if n == 15:
                    ternary(1)
                if n == 20:
                    add_moe(0)
                    ln_begin(x2[0], ln_index(1, 0, 0))
                if n == 22:
                    ln_end(x2[0], ln_index(1, 0, 0))
                if n == 26:
                    softmax_shift(0)
            hidden_rest(B * CHUNKS - 2)
            hidden_rest(B * CHUNKS - 1)
            softmax_sum(0)
            add_att1(0)
            ln_begin(x3[0], ln_index(1, 0, 1))
            add_moe(1)
            ln_begin(x2[1], ln_index(1, 1, 0))
            ln_end(x3[0], ln_index(1, 0, 1))
            ln_end(x2[1], ln_index(1, 1, 0))
            xn4_rest(0)
            softmax_shift(1)
            softmax_sum(1)
            for c in range(2):
                ff_rest(0, c)
            add_att1(1)
            ln_begin(x3[1], ln_index(1, 1, 1))
            for c in range(2, FF1_CHUNKS):
                ff_rest(0, c)
            ln_end(x3[1], ln_index(1, 1, 1))
            xn4_rest(1)
            for c in range(FF1_CHUNKS):
                ff_rest(1, c)

        @block.tensor
        def _(pe):
            def ln_T(dst, i):
                for t in range(TILES):
                    pe.wait_ge(ln_ready[i], t + 1)
                    last = nc.tensor.transpose(dst[:, t * P:(t + 1) * P], ln_out[i][:, t, :], ident)
                last.then_inc(lnT_ps_ready[i], 1)

            def keep_warm(ps, passes):
                for _ in range(passes):
                    nc.tensor.matmul(ps[:, 0:P], ones[:, :], ones[:, :], start=True, stop=True)

            def bias_rows():
                pe.wait_ge(rows_in, 16)
                nc.tensor.matmul(gate_ps[0][0:CTX, :], ones[0:1, 0:CTX], row_sb[:, :], start=True, stop=False)

            def inverse_row():
                pe.wait_ge(inv_diag_ready, 1)
                nc.tensor.matmul(gate_ps[1][0:CTX, 0:C], ones[:, 0:CTX], inv_diag[:, :],
                                 start=True, stop=True).then_inc(inv_row_ps_ready, 1)

            def ctx0_keys_values():
                a, b = PACK["Wkv0"]
                pe.wait_ge(small_in, 16)
                for i in range(B):
                    last = nc.tensor.matmul(gate_ps[0][0:CTX, i * 2 * C:(i + 1) * 2 * C], ctxT[:, i * CTX:(i + 1) * CTX],
                                            small[:, a:b], start=False, stop=(i == B - 1))
                last.then_inc(kv_ps_ready, 1)

            def ctx1_keys_values():
                a, _b = PACK["Wkv1"]
                nc.tensor.matmul(val_ps[0][:, 0:B * CTX], small[:, a:a + C], ctxT, start=True, stop=True).then_inc(k1T_ps_ready, 1)
                for i in range(B):
                    last = nc.tensor.matmul(val_ps[1][0:CTX, i * C:(i + 1) * C], ctxT[:, i * CTX:(i + 1) * CTX],
                                            small[:, a + C:a + 2 * C], start=True, stop=True)
                last.then_inc(v1_ps_ready, 1)

            def ctx1_wq_keys():
                pe.wait_ge(k1T_ready, 1)
                nc.tensor.matmul(val_ps[0][:, 0:B * CTX], packed("Wq1T"), k1T[:, :], start=True, stop=True).then_inc(wqk_ps_ready, 1)

            def head_sums():
                pe.wait_ge(k_feat_ready, 1)
                pe.wait_ge(kv_read, 1)
                pe.wait_ge(v_ones_set, 1)
                for i in range(B):
                    last = nc.tensor.matmul(acc_ps[:, i * KV_COLS:(i + 1) * KV_COLS], k_feat[:, i, :], v_ones[:, i, :],
                                            start=True, stop=True)
                last.then_inc(kvh_ps_ready, 1)

            def q_project(h):
                pe.wait_ge(xn1T_ready, h + 1)
                if h:
                    pe.wait_ge(k_div_ready, 1)
                nc.tensor.matmul(q_ps[h][:, :], packed("Wq0"), xn1T[h][:, :], start=True, stop=True).then_inc(q_ps_ready, 1)

            def att0_products(h):
                pe.wait_ge(kvh_ready, 1)
                pe.wait_ge(q_cube_ready, h + 1)
                if h:
                    pe.wait_ge(routeT_ready, h)
                    pe.wait_ge(xn2T_ready, h)
                else:
                    pe.wait_ge(q_relu_ready, 1)
                    pe.wait_ge(xn1T_ready, 1)
                for t in range(TILES):
                    ps = side0[:, P + t * KV_COLS:P + (t + 1) * KV_COLS] if t < 2 else side1[:, (t - 2) * KV_COLS:(t - 1) * KV_COLS]
                    nc.tensor.matmul(ps, q_cube[h][:, t * P:(t + 1) * P], kv_heads[:, h, :], start=True, stop=True)
                pe.wait_ge(q_sq_ready, h + 1)
                for t in range(TILES):
                    nc.tensor.matmul(side0[:, t:t + 1], q_sq[h][:, t * P:(t + 1) * P], ones[:, 0:1], start=True, stop=True)
                pe.wait_ge(q_six_ready, h + 1)
                for t in range(TILES):
                    last = nc.tensor.matmul(side0[:, TILES + t:TILES + t + 1], q_six[h][:, t * P:(t + 1) * P], ones[:, 0:1],
                                            start=True, stop=True)
                last.then_inc(att0_ps_ready, 1)

            def router(h):
                pe.wait_ge(xn2T_ready, h + 1)
                pe.wait_ge(att0_read, h + 1)
                for t in range(TILES):
                    last = nc.tensor.matmul(side1[:, t * EXPERTS:(t + 1) * EXPERTS], xn2T[:, t * P:(t + 1) * P],
                                            packed("WrT"), start=True, stop=True)
                last.then_inc(logits_ready, 1)

            def route_turn(h):
                pe.wait_ge(route_ready, h + 1)
                pe.wait_ge(logits_read, h + 1)
                for t in range(TILES):
                    last = nc.tensor.transpose(side1[0:2 * EXPERTS, t * P:(t + 1) * P],
                                               route_hl[h][:, t, :].bitcast(f32), ident)
                last.then_inc(routeT_ps_ready, 1)

            def spread(g):
                h, e = divmod(g, EXPERTS)
                pe.wait_ge(routeT_ready, h + 1)
                pe.wait_ge(select_ready, 1)
                if g:
                    pe.wait_ge(route_b_ready, g)
                nc.tensor.matmul(spread_ps[:, :], select[:, e, :], routeT[h][:, :], start=True, stop=True).then_inc(spread_ready, 1)

            def up(n, h, e):
                c = n % CHUNKS_PER_EXPERT
                gate, val = gate_ps[n % 2][:, :], val_ps[n % 2][:, :]
                for ps, col, done in ((gate, FFN + c * P, gate_ready), (val, c * P, val_ready)):
                    hi, lo = w1_hi[:, e, col:col + P], w1_lo[:, e, col:col + P]
                    if ps is val and n >= 2:
                        pe.wait_ge(gated_ready, n - 1)
                    nc.tensor.matmul(ps, lo, xn2_hi[h][:, :], start=True, stop=False)
                    nc.tensor.matmul(ps, hi, xn2_hi[h][:, :], start=False, stop=False)
                    pe.wait_ge(xn2_lo_ready, h + 1)
                    nc.tensor.matmul(ps, hi, xn2_lo[h][:, :], start=False, stop=True).then_inc(done, 1)

            def chunk_up(n):
                h, j = divmod(n, CHUNKS)
                e, c = divmod(j, CHUNKS_PER_EXPERT)
                pe.wait_ge(xn2_hi_ready, h + 1)
                if h == 0:
                    pe.wait_ge(w_lo_ready, 2 * e + 2)
                if n == 0:
                    pe.wait_ge(kv_read, 1)
                    pe.wait_ge(wqk_ready, 1)
                if n == 1:
                    pe.wait_ge(q_relu_ready, 2)
                    pe.wait_ge(v1_ready, 1)
                if n >= 2:
                    pe.wait_ge(silu_ready, n - 1)
                up(n, h, e)

            def downs(n):
                if n == CATCH_UP:
                    return [n - W2_LAG - 1, n - W2_LAG]
                lag = W2_LAG + 1 if n < CATCH_UP else W2_LAG
                return [n - lag] if n >= lag else []

            def chunk_down(m):
                h, j = divmod(m, CHUNKS)
                e, c = divmod(j, CHUNKS_PER_EXPERT)
                if m == 0:
                    pe.wait_ge(kvh_ready, 1)
                if j == 0 and h:
                    pe.wait_ge(moeT_ready, h)
                pe.wait_ge(hid_lo_ready, m + 1)
                hi, lo = hid_hi[m % HL][:, :], hid_lo[m % HL][:, :]
                nc.tensor.matmul(acc_ps[:, :], w2_lo[:, e, c, :], hi, start=(j == 0), stop=False)
                nc.tensor.matmul(acc_ps[:, :], w2_hi[:, e, c, :], lo, start=False, stop=False)
                nc.tensor.matmul(acc_ps[:, :], w2_hi[:, e, c, :], hi, start=False, stop=(j == CHUNKS - 1)).then_inc(w2_done, 1)
                if j == CHUNKS - 1:
                    pe.wait_ge(w2_done, m + 1)
                    pe.sem_inc(acc_ready, 1)

            def ternary_sum():
                pe.wait_ge(abs_ready, 2)
                pe.wait_ge(xn2T_ready, B)
                nc.tensor.matmul(side0[:, 0:2], ones[:, :], abs_sum[:, :], start=True, stop=True).then_inc(abs_ps_ready, 1)

            def moe_turn(h):
                pe.wait_ge(moeT_ready, h + 1)
                if h == 0:
                    pe.wait_ge(tern_ready, 1)
                for t in range(TILES):
                    last = nc.tensor.transpose(layer1_ps[h][:, t * P:(t + 1) * P], moeT[h][:, t * P:(t + 1) * P], ident)
                last.then_inc(moe_ps_ready, 1)

            def scores(h):
                pe.wait_ge(xn3T_ready, h + 1)
                pe.wait_ge(x2_ready, h + 1)
                pe.wait_ge(wqk_ready, 1)
                for t in range(TILES):
                    last = nc.tensor.matmul(layer1_ps[h][:, t * CTX:(t + 1) * CTX], xn3T[h][:, t * P:(t + 1) * P],
                                            wq_k1T[:, h * CTX:(h + 1) * CTX], start=True, stop=True)
                last.then_inc(score_ps_ready, 1)

            def probs_turn(h):
                pe.wait_ge(s_exp_ready, h + 1)
                for t in range(TILES):
                    last = nc.tensor.transpose(side1[0:CTX, t * P:(t + 1) * P], s_exp[h][:, t, :], ident)
                last.then_inc(probsT_ps_ready, 1)

            def att1_products(h):
                pe.wait_ge(probsT_ready, h + 1)
                for t in range(TILES):
                    last = nc.tensor.matmul(layer1_ps[h][:, t * C:(t + 1) * C], probsT[h][:, t * P:(t + 1) * P], v1[:, h, :],
                                            start=True, stop=True)
                last.then_inc(att1_ps_ready, 1)

            def residual_T(h):
                pe.wait_ge(x3_ready, TILES * (h + 1))
                if h == 0:
                    pe.wait_ge(route_b_ready, B * EXPERTS)
                else:
                    pe.wait_ge(xn4_lo_ready, h)
                for t in range(TILES):
                    nc.tensor.matmul(y_ps[h][:, t * P:(t + 1) * P], x3[h][:, t, :], ident, start=(t == 0), stop=False,
                                     skip_group_check=True)

            def ff_up(h, c):
                pe.wait_ge(xn4_lo_ready, h + 1)
                pe.wait_ge(tern_ready, 2)
                if h == 0:
                    pe.wait_ge(silu_ready, B * CHUNKS)
                    if c >= 2:
                        pe.wait_ge(gated_ready, B * CHUNKS)
                else:
                    pe.wait_ge(gelu_ready, c + 1)
                w = tern[:, 0, c * P:(c + 1) * P]
                nc.tensor.matmul(ff_ps[c][:, :], w, xn4_lo[h][:, :], start=True, stop=False)
                nc.tensor.matmul(ff_ps[c][:, :], w, xn4_hi[h][:, :], start=False, stop=True).then_inc(ff_ps_ready, 1)

            def ff_down(h, c):
                pe.wait_ge(gelu_lo_ready, FF1_CHUNKS * h + c + 1)
                w = tern[:, 1, c * P:(c + 1) * P]
                nc.tensor.matmul(y_ps[h][:, :], w, gelu_lo[c][:, :], start=False, stop=False, skip_group_check=True)
                last = nc.tensor.matmul(y_ps[h][:, :], w, gelu_hi[c][:, :], start=False, stop=(c == FF1_CHUNKS - 1),
                                        skip_group_check=True)
                if c == FF1_CHUNKS - 1:
                    last.then_inc(y_ps_ready, 1)

            pe.wait_ge(ones_set, 1)
            keep_warm(acc_ps, WARM[0])
            bias_rows()
            keep_warm(acc_ps, WARM[1])
            ctx0_keys_values()
            inverse_row()
            ln_T(side0, ln_index(0, 0, 0))
            ctx1_keys_values()
            q_project(0)
            keep_warm(spread_ps, WARM[2])
            head_sums()
            keep_warm(spread_ps, WARM[3])
            att0_products(0)
            ln_T(spread_ps, ln_index(0, 1, 0))
            q_project(1)
            ctx1_wq_keys()
            pe.wait_ge(v1_ready, 1)
            keep_warm(val_ps[1], WARM[4])
            pe.wait_ge(att0_read, 1)
            ln_T(side0, ln_index(0, 0, 1))
            keep_warm(val_ps[1], WARM[5])
            router(0)
            for n in range(B * CHUNKS):
                chunk_up(n)
                if n == 1:
                    route_turn(0)
                if n == 2:
                    spread(0)
                if n == 3:
                    spread(1)
                if n % CHUNKS_PER_EXPERT == 1 and 5 <= n + 2 < B * CHUNKS:
                    spread(n // CHUNKS_PER_EXPERT + 1)
                for m in downs(n):
                    chunk_down(m)
                if n == 2:
                    att0_products(1)
                if n == 6:
                    pe.wait_ge(att0_read, 2)
                    ln_T(side0, ln_index(0, 1, 1))
                if n == 9:
                    router(1)
                if n == 12:
                    route_turn(1)
                if n == 13:
                    ternary_sum()
                if n == 19:
                    moe_turn(0)
                if n == 23:
                    pe.wait_ge(routeT_ready, 2)
                    ln_T(side1, ln_index(1, 0, 0))
                if n == 25:
                    scores(0)
            chunk_down(B * CHUNKS - 3)
            chunk_down(B * CHUNKS - 2)
            probs_turn(0)
            chunk_down(B * CHUNKS - 1)
            att1_products(0)
            moe_turn(1)
            residual_T(0)
            ln_T(side0, ln_index(1, 0, 1))
            pe.wait_ge(probsT_ready, 1)
            ln_T(side1, ln_index(1, 1, 0))
            scores(1)
            for c in range(FF1_CHUNKS):
                ff_up(0, c)
            probs_turn(1)
            att1_products(1)
            for c in range(FF1_CHUNKS):
                ff_down(0, c)
            residual_T(1)
            ln_T(acc_ps, ln_index(1, 1, 1))
            for c in range(FF1_CHUNKS):
                ff_up(1, c)
            for c in range(FF1_CHUNKS):
                ff_down(1, c)


def kernel(x, ctx_1024, L0_xattn_Wq, L0_xattn_bq, L0_xattn_Wk, L0_xattn_bk, L0_xattn_Wv, L0_xattn_bv,
           L0_xattn_scale, L0_ffn_Wr, L0_ffn_W1, L0_ffn_W2, L1_xattn_Wq, L1_xattn_Wkv, L1_ffn_W1,
           L1_ffn_b1, L1_ffn_W2, L1_ffn_b2):
    import concourse.bacc as bacc
    from concourse.bass_utils import run_bass_kernel_spmd

    f = np.float32
    a = [np.asarray(v) for v in (ctx_1024, L0_xattn_Wq, L0_xattn_bq, L0_xattn_Wk, L0_xattn_bk, L0_xattn_Wv,
                                 L0_xattn_bv, L0_xattn_scale, L0_ffn_Wr, L0_ffn_W1, L0_ffn_W2, L1_xattn_Wq,
                                 L1_xattn_Wkv, L1_ffn_W1, L1_ffn_b1, L1_ffn_W2, L1_ffn_b2)]
    ctx_, wq0, bq, wk0, bk, wv0, bv, scale, wr, w1, w2, wq1, wkv1, tw1, b1, tw2, b2 = a
    head = np.arange(C) // HEAD_DIM
    kv_mask = np.concatenate([head[:, None] == head[None, :], head[:, None] == np.arange(HEADS)[None, :]], 1).astype(f)
    iota = np.tile(np.arange(EXPERTS, dtype=f), (P, 1))
    parts = {
        "ctxT": ctx_.reshape(B * CTX, C).T, "Wkv0": np.concatenate([wk0, wv0], 1), "Wq0": wq0,
        "scale_bq": np.stack([scale.reshape(C), bq], 1), "ident": np.eye(C, dtype=f), "Wkv1": wkv1, "Wq1T": wq1.T,
        "WrT": wr.T, "b1": b1.reshape(FF1_CHUNKS, P).T, "b2": b2.reshape(C, 1), "kv_mask": kv_mask, "iota": iota,
    }
    arrays = {
        "x": np.ascontiguousarray(np.asarray(x)),
        "pack": np.ascontiguousarray(np.concatenate([parts[k] for k in PACK], 1)),
        "rows": np.concatenate([bk, bv, bk, bv]).reshape(1, ROW_COLS),
        "w1": np.ascontiguousarray(w1.transpose(2, 0, 1)),
        "w2": np.ascontiguousarray(w2.reshape(EXPERTS, C, CHUNKS_PER_EXPERT, P).transpose(3, 0, 2, 1)),
        "ternary_w": np.ascontiguousarray(np.stack([tw1.T, tw2.reshape(C, FF1_CHUNKS, P).transpose(2, 1, 0).reshape(P, FF1)], 1)),
    }
    nc = bacc.Bacc("TRN2", target_bir_lowering=False, num_devices=1)
    args = [nc.dram_tensor(n, v.shape, mybir.dt.from_np(v.dtype), kind="ExternalInput").ap() for n, v in arrays.items()]
    out = nc.dram_tensor("out", (P, B, N_TOK), mybir.dt.float32, kind="ExternalOutput").ap()
    build(nc, *args, out)
    r = run_bass_kernel_spmd(nc, [arrays], core_ids=[0])
    got = np.asarray(r.results[0]["out"])
    return np.ascontiguousarray(got.reshape(C, B, TILES, P).transpose(1, 3, 2, 0).reshape(B, N_TOK, C))
```

```python
import concourse.bass as bass
from concourse import mybir
from contextlib import ExitStack
import numpy as np

P = 128
B, N_TOK, C = 2, 512, 128
CTX = 77
HEADS = 16
HEAD_DIM = C // HEADS
EXPERTS, FFN = 8, 256
TILES = N_TOK // P
CHUNKS_PER_EXPERT = FFN // P
CHUNKS = EXPERTS * CHUNKS_PER_EXPERT
FF1 = 4 * C
FF1_CHUNKS = FF1 // P
KV_COLS = C + HEADS
W2_LAG = 3
CATCH_UP = 11
TAIL_WARM = [9, 3, 2, 7, 3]
WARM = [5, 1, 3, 2, 8, 0]
PARTS0 = [(0, 0, TILES // 2), (0, TILES // 2, TILES), (1, 0, TILES)]
PARTS = [(0, 0, TILES), (1, 0, TILES // 2), (1, TILES // 2, TILES)]
RAW = 4
FOCUS_EPS = 1e-6
LN_EPS = 1e-5

PIECES = [(0, 0, N_TOK), (1, 0, N_TOK // 2), (1, N_TOK // 2, N_TOK)]

PACK = {}
_at = 0
for _name, _width in (("scale_bq", 2), ("ctxT", B * CTX), ("Wkv0", 2 * C), ("ident", C), ("Wq0", C),
                      ("Wkv1", 2 * C), ("Wq1T", C), ("WrT", EXPERTS), ("b1", FF1_CHUNKS), ("b2", 1),
                      ("kv_mask", KV_COLS), ("iota", EXPERTS)):
    PACK[_name] = (_at, _at + _width)
    _at += _width
PACK_COLS = _at
FIRST_COLS = PACK["Wq0"][1]
ROW_COLS = B * 2 * C


def build(nc, x, pack, rows, w1, w2, ternary_w, out):
    f32, f32r, u32 = mybir.dt.float32, mybir.dt.float32r, mybir.dt.uint32
    ALU, ACT, AX = mybir.AluOpType, mybir.ActivationFunctionType, mybir.AxisListType
    ctx = ExitStack()
    with ctx:
        def sb(name, shape, dt=f32):
            return ctx.enter_context(nc.sbuf_tensor(name, shape, dt))

        def sem(name):
            return ctx.enter_context(nc.semaphore(name))

        def bank(name):
            return ctx.enter_context(nc.psum_tensor(name, [P, 512], f32))

        def per_half(name, shape, dt=f32):
            return [sb(f"{name}_{h}", shape, dt) for h in range(B)]

        small = sb("small", [P, PACK_COLS])
        row_sb = sb("row_sb", [1, ROW_COLS])
        w1_raw = sb("w1_raw", [P, RAW, 2 * FFN])
        w2_raw = sb("w2_raw", [P, RAW, CHUNKS_PER_EXPERT, C])
        tw_raw = sb("tw_raw", [P, 2, FF1])
        x_in = per_half("x_in", [P, TILES, C])

        def packed(name):
            a, b = PACK[name]
            return small[:, a:b]

        ctxT, ident = packed("ctxT"), packed("ident")

        w1_hi = sb("w1_hi", [P, EXPERTS, 2 * FFN], f32r)
        w1_lo = sb("w1_lo", [P, EXPERTS, 2 * FFN], f32r)
        w2_hi = sb("w2_hi", [P, EXPERTS, CHUNKS_PER_EXPERT, C], f32r)
        w2_lo = sb("w2_lo", [P, EXPERTS, CHUNKS_PER_EXPERT, C], f32r)
        below = sb("below", [P, FF1])
        tern = sb("tern", [P, 2, FF1], f32r)
        select = sb("select", [2 * EXPERTS, EXPERTS, P], f32r)
        ones = sb("ones", [P, P])
        half_power = sb("half_power", [P, 4])
        neg_half_power = sb("neg_half_power", [P, 4])
        abs_sum = sb("abs_sum", [P, 2])
        t_scale = sb("t_scale", [P, 2])
        t_hi = sb("t_hi", [P, 2])
        t_lo = sb("t_lo", [P, 2])

        sp_abs = sb("sp_abs", [P, 1])
        sp_exp = sb("sp_exp", [P, 1])
        sp_ln = sb("sp_ln", [P, 1])
        sp = sb("sp", [P, 1])
        inv_sp = sb("inv_sp", [P, 1])
        inv_diag = sb("inv_diag", [P, C])
        eps_inv_sp = sb("eps_inv_sp", [P, 1])
        bq_inv_sp = sb("bq_inv_sp", [P, 1])
        k_act = sb("k_act", [CTX, B, C])
        k_div = sb("k_div", [CTX, B, C])
        k_sq = sb("k_sq", [CTX, B, C])
        k_cube = sb("k_cube", [CTX, B, C])
        k_six = sb("k_six", [CTX, B, C])
        k_sums = sb("k_sums", [CTX, 2, B])
        k_rec = sb("k_rec", [CTX, B])
        k_ratio = sb("k_ratio", [CTX, B])
        k_factor = sb("k_factor", [CTX, B])
        k_feat = sb("k_feat", [CTX, B, C])
        v_ones = sb("v_ones", [CTX, B, KV_COLS])
        kv_heads = sb("kv_heads", [P, B, KV_COLS])
        k1T = sb("k1T", [P, B * CTX])
        wq_k1T = sb("wq_k1T", [P, B * CTX])
        v1 = sb("v1", [CTX, B, C])

        LN = range(2 * len(PARTS0) + 2 * len(PARTS))
        ln_stats = [sb(f"ln_stats_{i}", [P, TILES, 6]) for i in LN]
        ln_mv = [sb(f"ln_mv_{i}", [P, TILES, 2]) for i in LN]
        ln_var = [sb(f"ln_var_{i}", [P, TILES]) for i in LN]
        ln_shift = sb("ln_shift", [P, TILES])
        ln_rstd = [sb(f"ln_rstd_{i}", [P, TILES]) for i in LN]
        ln_out_ring = [sb(f"ln_out_{h}", [P, TILES, C]) for h in range(B)]
        ln_out = [ln_out_ring[h] for h, _t0, _t1 in PARTS0 + PARTS0 + PARTS + PARTS]
        xn1T = per_half("xn1T", [P, N_TOK])
        q_relu = per_half("q_relu", [P, N_TOK])
        q_sq = per_half("q_sq", [P, N_TOK])
        q_cube = per_half("q_cube", [P, N_TOK])
        q_six = per_half("q_six", [P, N_TOK])
        q_rec = per_half("q_rec", [P, TILES])
        q_ratio = per_half("q_ratio", [P, TILES])
        q_inv = per_half("q_inv", [P, TILES])
        q_inv_eps = per_half("q_inv_eps", [P, TILES])
        den = per_half("den", [P, TILES, HEADS])
        inv_den = per_half("inv_den", [P, TILES, HEADS])
        att0 = [sb("att0", [P, TILES, C])] * B
        x1 = x_in
        xn2T = sb("xn2T", [P, N_TOK])
        xn2_hi = per_half("xn2_hi", [P, N_TOK], f32r)
        xn2_lo = per_half("xn2_lo", [P, N_TOK], f32r)
        top8 = per_half("top8", [P, TILES, 8])
        top8_at = per_half("top8_at", [P, TILES, 8], u32)
        gap = per_half("gap", [P, TILES])
        gap_tanh = per_half("gap_tanh", [P, TILES])
        top_w = per_half("top_w", [P, 2, TILES])
        pick = per_half("pick", [P, 2, TILES, EXPERTS])
        pick_w = per_half("pick_w", [P, 2, TILES, EXPERTS])
        route = per_half("route", [P, TILES, EXPERTS])
        route_hl = per_half("route_hl", [P, TILES, 2 * EXPERTS], f32r)
        routeT = per_half("routeT", [2 * EXPERTS, N_TOK], f32r)
        moeT = [sb("moeT", [P, N_TOK])] * B
        x2 = per_half("x2", [P, TILES, C])
        xn3T = [sb("xn3T", [P, N_TOK])] * B
        s_max = per_half("s_max", [P, TILES])
        s_shift = [sb("s_shift", [P, TILES, CTX])] * B
        s_exp = per_half("s_exp", [P, TILES, CTX])
        s_sum = per_half("s_sum", [P, TILES])
        s_inv = per_half("s_inv", [P, TILES])
        probsT = [sb("probsT", [CTX, N_TOK])] * B
        x3 = x1
        xn4_hi = per_half("xn4_hi", [P, N_TOK], f32r)
        xn4_lo = per_half("xn4_lo", [P, N_TOK], f32r)
        yT = q_six

        SG, SW, AB, HL = 3, 3, 3, 4
        silu_g = [sb(f"silu_g_{i}", [P, N_TOK]) for i in range(SG)]
        gated = [sb(f"gated_{i}", [P, N_TOK]) for i in range(SW)]
        hid = [sb(f"hid_{i}", [P, N_TOK]) for i in range(AB)]
        hid_hi = [sb(f"hid_hi_{i}", [P, N_TOK], f32r) for i in range(HL)]
        hid_lo = [sb(f"hid_lo_{i}", [P, N_TOK], f32r) for i in range(HL)]
        route_b = [sb(f"route_b_{i}", [P, N_TOK]) for i in range(2)]
        gelu = [[q_relu[0], q_relu[1], q_sq[0], q_sq[1]], [silu_g[0], silu_g[1], silu_g[2], gated[0]]]
        gelu_hi = [hid_hi, [xn2_hi[0], xn2_hi[1], xn4_hi[0], hid_hi[0]]]
        gelu_lo = [hid_lo, [xn2_lo[0], xn2_lo[1], xn4_lo[0], hid_lo[0]]]

        gate_ps = [bank("gate_ps_0"), bank("gate_ps_1")]
        val_ps = [bank("val_ps_0"), bank("val_ps_1")]
        acc_ps = bank("acc_ps")
        spread_ps = bank("spread_ps")
        side0 = bank("side0")
        side1 = bank("side1")
        y_ps = [spread_ps, side0]
        part_ps = [side0, val_ps[0], val_ps[1]]
        part_turn_ps = [side1, val_ps[0], val_ps[1]]
        att0_ps = [(side0, None), (side1, None), (acc_ps, spread_ps)]
        att0_in = [att0_ps[0], att0_ps[1], (xn3T[0], moeT[0])]
        q_ps = [side0, side1, gate_ps[1]]
        xn1T_ps = [side0, side1, spread_ps]
        xn2T_ps = [side0, side1, side0]
        logits_ps = [gate_ps[1], side1]
        ff_ps = [[gate_ps[0], gate_ps[1], acc_ps, side1], [val_ps[0], val_ps[1], gate_ps[0], gate_ps[1]]]

        small_in, rest_in, rows_in, tw_in = sem("small_in"), sem("rest_in"), sem("rows_in"), sem("tw_in")
        x_loaded = [sem(f"x_loaded_{h}") for h in range(B)]
        w1_in = [sem(f"w1_in_{e}") for e in range(EXPERTS)]
        w2_in = [sem(f"w2_in_{e}") for e in range(EXPERTS)]
        ones_set, powers_set, v_ones_set = sem("ones_set"), sem("powers_set"), sem("v_ones_set")
        inv_diag_ready, inv_row_ps_ready = sem("inv_diag_ready"), sem("inv_row_ps_ready")
        sp_ln_ready, sp_ready = sem("sp_ln_ready"), sem("sp_ready")
        kv_ps_ready, kv_read = sem("kv_ps_ready"), sem("kv_read")
        k_div_ready, k_sq_ready, k_cube_ready, k_six_ready = (
            sem("k_div_ready"), sem("k_sq_ready"), sem("k_cube_ready"), sem("k_six_ready"))
        k_ratio_ready, k_factor_ready, k_feat_ready = (
            sem("k_ratio_ready"), sem("k_factor_ready"), sem("k_feat_ready"))
        kvh_ps_ready, kvh_ready = sem("kvh_ps_ready"), sem("kvh_ready")
        k1T_ps_ready, k1T_ready = sem("k1T_ps_ready"), sem("k1T_ready")
        wqk_ps_ready, wqk_ready = sem("wqk_ps_ready"), sem("wqk_ready")
        v1_ps_ready, v1_ready = sem("v1_ps_ready"), sem("v1_ready")
        abs_ready, abs_ps_ready, tern_ready, select_ready = (
            sem("abs_ready"), sem("abs_ps_ready"), sem("tern_ready"), sem("select_ready"))
        w_hi_ready, w_lo_ready = sem("w_hi_ready"), sem("w_lo_ready")
        var_ready, rstd_ready, lnT_ps_ready = sem("var_ready"), sem("rstd_ready"), sem("lnT_ps_ready")
        ln_ready = [sem(f"ln_ready_{i}") for i in LN]
        xn1T_ready, q_ps_ready, q_relu_ready = sem("xn1T_ready"), sem("q_ps_ready"), sem("q_relu_ready")
        q_sq_ready, q_cube_ready, q_six_ready = (
            sem("q_sq_ready"), sem("q_cube_ready"), sem("q_six_ready"))
        q_sums_ready, att0_ps_ready, att0_kept, q_ratio_ready, q_inv_ready, att0_read = (
            sem("q_sums_ready"), sem("att0_ps_ready"), sem("att0_kept"), sem("q_ratio_ready"), sem("q_inv_ready"), sem("att0_read"))
        xn2_hi_ready, xn2T_ready, xn2_lo_ready = sem("xn2_hi_ready"), sem("xn2T_ready"), sem("xn2_lo_ready")
        logits_ready, logits_read, gap_ready, gap_tanh_ready = (
            sem("logits_ready"), sem("logits_read"), sem("gap_ready"), sem("gap_tanh_ready"))
        route_ready, routeT_ps_ready, routeT_ready = (
            sem("route_ready"), sem("routeT_ps_ready"), sem("routeT_ready"))
        spread_ready, route_b_ready = sem("spread_ready"), sem("route_b_ready")
        gate_ready, val_ready = sem("gate_ready"), sem("val_ready")
        silu_ready, gated_ready, hid_ready = sem("silu_ready"), sem("gated_ready"), sem("hid_ready")
        hid_hi_ready, hid_lo_ready, w2_done = sem("hid_hi_ready"), sem("hid_lo_ready"), sem("w2_done")
        moeT_ready, moe_ps_ready, x2_ready = (
            sem("moeT_ready"), sem("moe_ps_ready"), sem("x2_ready"))
        xn3T_ready, score_ps_ready, s_shift_ready, s_exp_ready = (
            sem("xn3T_ready"), sem("score_ps_ready"), sem("s_shift_ready"), sem("s_exp_ready"))
        probsT_ps_ready, probsT_ready = sem("probsT_ps_ready"), sem("probsT_ready")
        att1_ps_ready, x3_ready = sem("att1_ps_ready"), sem("x3_ready")
        xn4_hi_ready, xn4_lo_ready = sem("xn4_hi_ready"), sem("xn4_lo_ready")
        ff_ps_ready, gelu_ready, ff_done = sem("ff_ps_ready"), sem("gelu_ready"), sem("ff_done")
        gelu_hi_ready, gelu_lo_ready, shift_ready = sem("gelu_hi_ready"), sem("gelu_lo_ready"), sem("shift_ready")
        y_ready, y_stored = [sem(f"y_ready_{i}") for i in range(len(PIECES))], sem("y_stored")
        dve_chain, act_chain = sem("dve_chain"), sem("act_chain")

        def ln0(k, which):
            return len(PARTS0) * which + k

        def ln1(k, which):
            return 2 * len(PARTS0) + len(PARTS) * which + k

        def cols0(k):
            return slice(PARTS0[k][1] * P, PARTS0[k][2] * P)

        def att0_pairs(k):
            _h, t0, t1 = PARTS0[k]
            first, second = att0_in[k]
            return [(t0, first[:, P:P + 2 * KV_COLS])] + ([(t0 + 2, second[:, 0:2 * KV_COLS])] if t1 - t0 > 2 else [])

        def part_cols(k):
            return slice(PARTS[k][1] * P, PARTS[k][2] * P)

        def rests(n):
            return {2: [], 3: [0], 4: [1], 5: [2, 3]}.get(n, [n - 2] if n > 5 else [])

        block = ctx.enter_context(nc.Block())

        @block.sync
        def _(sp_q):
            sp_q.dma_start(x_in[0][:, :, :], x[0].rearrange("(p t) c -> p t c", t=TILES)).then_inc(x_loaded[0], 16)
            sp_q.dma_start(small[:, 0:FIRST_COLS], pack[:, 0:FIRST_COLS]).then_inc(small_in, 16)
            sp_q.dma_start(x_in[1][:, :, :], x[1].rearrange("(p t) c -> p t c", t=TILES)).then_inc(x_loaded[1], 16)
            sp_q.dma_start(small[:, FIRST_COLS:], pack[:, FIRST_COLS:]).then_inc(rest_in, 16)
            for e in range(EXPERTS):
                if e >= RAW:
                    sp_q.wait_ge(w_lo_ready, 2 * (e - RAW) + 2)
                sp_q.dma_start(w1_raw[:, e % RAW, :], w1[:, e, :]).then_inc(w1_in[e], 16)
                sp_q.dma_start(w2_raw[:, e % RAW, :, :], w2[:, e, :, :]).then_inc(w2_in[e], 16)
                if e == RAW - 1:
                    sp_q.dma_start(tw_raw[:, :, :], ternary_w).then_inc(tw_in, 16)
            for (h, c0, c1), ready in zip(PIECES, y_ready):
                sp_q.wait_ge(ready, 1)
                sp_q.dma_start(out[:, h, c0:c1], yT[h][:, c0:c1]).then_inc(y_stored, 16)
            sp_q.wait_ge(y_stored, 16 * len(PIECES))

        @block.gpsimd
        def _(pool):
            nc.gpsimd.memset(ones[:, :], 1.0).then_inc(ones_set, 1)
            nc.gpsimd.memset(half_power[:, :], 0.5).then_inc(powers_set, 1)
            nc.gpsimd.memset(neg_half_power[:, :], -0.5).then_inc(powers_set, 1)
            nc.gpsimd.memset(v_ones[:, :, C:KV_COLS], 1.0).then_inc(v_ones_set, 1)
            pool.wait_ge(powers_set, 2)

            def rstd(i, t0=0, t1=TILES):
                pool.wait_ge(var_ready, i + 1)
                nc.gpsimd.tensor_tensor(ln_rstd[i][:, t0:t1], ln_var[i][:, t0:t1], neg_half_power[:, t0:t1],
                                        ALU.pow).then_inc(rstd_ready, 1)

            def k_root():
                pool.wait_ge(k_ratio_ready, 1)
                nc.gpsimd.tensor_tensor(k_factor[:, :], k_ratio[:, :], half_power[0:CTX, 0:B],
                                        ALU.pow).then_inc(k_factor_ready, 1)

            def q_root(k):
                h, t0, t1 = PARTS0[k]
                pool.wait_ge(q_ratio_ready, k + 1)
                nc.gpsimd.tensor_tensor(q_inv[h][:, t0:t1], q_ratio[h][:, t0:t1], half_power[:, t0:t1],
                                        ALU.pow).then_inc(q_inv_ready, 1)

            def w1_rest(e):
                pool.wait_ge(w_hi_ready, 2 * e + 1)
                nc.gpsimd.tensor_tensor(w1_lo[:, e, :], w1_raw[:, e % RAW, :], w1_hi[:, e, :].bitcast(f32),
                                        ALU.subtract).then_inc(w_lo_ready, 1)

            def w2_rest(e):
                pool.wait_ge(w_hi_ready, 2 * e + 2)
                nc.gpsimd.tensor_tensor(w2_lo[:, e, :, :], w2_raw[:, e % RAW, :, :], w2_hi[:, e, :, :].bitcast(f32),
                                        ALU.subtract).then_inc(w_lo_ready, 1)

            def weigh(n):
                pool.wait_ge(gated_ready, n + 1)
                pool.wait_ge(route_b_ready, n // CHUNKS_PER_EXPERT + 1)
                if n >= AB:
                    pool.wait_ge(hid_lo_ready, n - AB + 1)
                nc.gpsimd.tensor_tensor(hid[n % AB][:, :], gated[n % SW][:, :],
                                        route_b[(n // CHUNKS_PER_EXPERT) % 2][:, :],
                                        ALU.mult).then_inc(hid_ready, 1)

            def ff_round(h, c):
                pool.wait_ge(gelu_ready, FF1_CHUNKS * h + c + 1)
                if h:
                    pool.wait_ge(val_ready, B * CHUNKS)
                    pool.wait_ge(ff_ps_ready, FF1_CHUNKS)
                    if c == FF1_CHUNKS - 1:
                        pool.wait_ge(ff_done, 1)
                else:
                    pool.wait_ge(w2_done, B * CHUNKS - HL + c + 1)
                nc.gpsimd.tensor_scalar(gelu_hi[h][c][:, :], gelu[h][c][:, :], 1.0, 0.0, ALU.mult, ALU.add).then_inc(gelu_hi_ready, 1)

            for k in (0, 1):
                rstd(ln0(k, 0), *PARTS0[k][1:])
            w1_rest(0)
            w2_rest(0)
            k_root()
            rstd(ln0(2, 0))
            w1_rest(1)
            w2_rest(1)
            for k in (0, 1):
                q_root(k)
            w1_rest(2)
            w2_rest(2)
            w1_rest(3)
            w2_rest(3)
            for k in (0, 1):
                rstd(ln0(k, 1), *PARTS0[k][1:])
            for e in range(4, 7):
                w1_rest(e)
                w2_rest(e)
            for n in range(B * CHUNKS - 1):
                weigh(n)
                if n == 2:
                    q_root(2)
                if n == 4:
                    w1_rest(7)
                if n == 5:
                    w2_rest(7)
                if n == 8:
                    rstd(ln0(2, 1))
                if n == 22:
                    rstd(ln1(0, 0))
            for k in (1, 2):
                rstd(ln1(k, 0), *PARTS[k][1:])
            rstd(ln1(0, 1))
            for k in (1, 2):
                rstd(ln1(k, 1), *PARTS[k][1:])
            for c in range(FF1_CHUNKS):
                ff_round(0, c)
            for c in range(FF1_CHUNKS):
                ff_round(1, c)

        @block.scalar
        def _(act):
            def w_hi(e):
                act.wait_ge(w1_in[e], 16)
                nc.scalar.activation(w1_hi[:, e, :], w1_raw[:, e % RAW, :], ACT.Copy).then_inc(w_hi_ready, 1)
                act.wait_ge(w2_in[e], 16)
                nc.scalar.activation(w2_hi[:, e, :, :], w2_raw[:, e % RAW, :, :], ACT.Copy).then_inc(w_hi_ready, 1)

            def softplus():
                act.wait_ge(small_in, 16)
                a, _b = PACK["scale_bq"]
                nc.scalar.activation(sp_abs[:, :], small[:, a:a + 1], ACT.Abs).then_inc(act_chain, 1)
                act.wait_ge(act_chain, 1)
                nc.scalar.activation(sp_exp[:, :], sp_abs[:, :], ACT.Exp, scale=-1.0).then_inc(act_chain, 1)
                act.wait_ge(act_chain, 2)
                nc.scalar.activation(sp_ln[:, :], sp_exp[:, :], ACT.Ln, bias=1.0).then_inc(sp_ln_ready, 1)

            def k_squares(src, dst, ready, row, done):
                act.wait_ge(ready, 1)
                for b in range(B):
                    nc.scalar.activation(dst[:, b, :], src[:, b, :], ACT.Square,
                                         accum_out=k_sums[:, row, b:b + 1]).then_inc(done, 1)

            def ctx1_reads():
                act.wait_ge(k1T_ps_ready, 1)
                nc.scalar.activation(k1T[:, :], val_ps[0][:, 0:B * CTX], ACT.Copy).then_inc(k1T_ready, 1)
                act.wait_ge(v1_ps_ready, 1)
                nc.scalar.activation(v1[:, :, :], val_ps[1][0:CTX, 0:B * C].rearrange("p (b c) -> p b c", b=B),
                                     ACT.Copy).then_inc(v1_ready, 1)

            def wqk_read():
                act.wait_ge(wqk_ps_ready, 1)
                nc.scalar.activation(wq_k1T[:, :], val_ps[0][:, 0:B * CTX], ACT.Copy).then_inc(wqk_ready, 1)

            def abs_sums():
                act.wait_ge(tw_in, 16)
                for i in range(2):
                    if i:
                        act.wait_ge(abs_ready, i)
                    nc.scalar.activation(below[:, :], tw_raw[:, i, :], ACT.Abs,
                                         accum_out=abs_sum[:, i:i + 1]).then_inc(abs_ready, 1)

            def copy_T(dst, src, i, done):
                act.wait_ge(lnT_ps_ready, i + 1)
                nc.scalar.activation(dst, src, ACT.Copy).then_inc(done, 1)

            def xn1_columns(k):
                h, t0, t1 = PARTS0[k]
                copy_T(xn1T[h][:, cols0(k)], xn1T_ps[k][:, 0:(t1 - t0) * P], ln0(k, 0), xn1T_ready)

            def q_first(k):
                h, t0, t1 = PARTS0[k]
                act.wait_ge(q_ps_ready, k + 1)
                act.wait_ge(sp_ready, 1)
                nc.scalar.activation(q_relu[h][:, cols0(k)], q_ps[k][:, 0:(t1 - t0) * P], ACT.Relu, bias=bq_inv_sp[:, :],
                                     scale=inv_sp[:, :]).then_inc(q_relu_ready, 1)

            def q_square(k):
                h = PARTS0[k][0]
                act.wait_ge(q_relu_ready, k + 1)
                nc.scalar.activation(q_sq[h][:, cols0(k)], q_relu[h][:, cols0(k)], ACT.Square,
                                     bias=eps_inv_sp[:, :]).then_inc(q_sq_ready, 1)

            def q_sixth(k):
                h = PARTS0[k][0]
                act.wait_ge(q_cube_ready, k + 1)
                nc.scalar.activation(q_six[h][:, cols0(k)], q_cube[h][:, cols0(k)], ACT.Square).then_inc(q_six_ready, 1)

            def xn2_whole(k):
                h, t0, t1 = PARTS0[k]
                if h:
                    act.wait_ge(xn2_lo_ready, h)
                    act.wait_ge(logits_ready, h)
                copy_T(xn2T[:, cols0(k)], xn2T_ps[k][:, 0:(t1 - t0) * P], ln0(k, 1), xn2T_ready)

            def xn2_rounded(k):
                h, t0, t1 = PARTS0[k]
                nc.scalar.activation(xn2_hi[h][:, cols0(k)], xn2T_ps[k][:, 0:(t1 - t0) * P], ACT.Copy).then_inc(xn2_hi_ready, 1)

            def keep_att0():
                act.wait_ge(att0_ps_ready, 3)
                act.wait_ge(q_sums_ready, 3)
                for bank_sb, bank_ps, cols in zip(att0_in[2], att0_ps[2], (P + 2 * KV_COLS, 2 * KV_COLS)):
                    nc.scalar.activation(bank_sb[:, 0:cols], bank_ps[:, 0:cols], ACT.Copy).then_inc(att0_kept, 1)

            def route_tanh(h):
                act.wait_ge(gap_ready, h + 1)
                nc.scalar.activation(gap_tanh[h][:, :], gap[h][:, :], ACT.Tanh, scale=0.5).then_inc(gap_tanh_ready, 1)

            def silu(n):
                act.wait_ge(gate_ready, n + 1)
                if n >= SG:
                    act.wait_ge(gated_ready, n - SG + 1)
                nc.scalar.activation(silu_g[n % SG][:, :], gate_ps[n % 2][:, :], ACT.Silu).then_inc(silu_ready, 1)

            def read_spread(g):
                act.wait_ge(spread_ready, g + 1)
                if g >= 2:
                    act.wait_ge(hid_ready, CHUNKS_PER_EXPERT * (g - 1))
                nc.scalar.activation(route_b[g % 2][:, :], spread_ps[:, :], ACT.Copy).then_inc(route_b_ready, 1)

            def hid_round(n):
                act.wait_ge(hid_ready, n + 1)
                if n >= HL:
                    act.wait_ge(w2_done, n - HL + 1)
                nc.scalar.activation(hid_hi[n % HL][:, :], hid[n % AB][:, :], ACT.Copy).then_inc(hid_hi_ready, 1)

            def read_acc(k):
                h = PARTS[k][0]
                act.wait_ge(w2_done, CHUNKS * (h + 1))
                nc.scalar.activation(moeT[h][:, part_cols(k)], acc_ps[:, part_cols(k)], ACT.Copy).then_inc(moeT_ready, 1)

            def xn3_columns(k):
                h, t0, t1 = PARTS[k]
                copy_T(xn3T[h][:, part_cols(k)], part_turn_ps[k][:, 0:(t1 - t0) * P], ln1(k, 0), xn3T_ready)

            def softmax_exp(k):
                h, t0, t1 = PARTS[k]
                act.wait_ge(s_shift_ready, k + 1)
                nc.scalar.activation(s_exp[h][:, t0:t1, :], s_shift[h][:, t0:t1, :], ACT.Exp,
                                     scale=float(1.0 / np.sqrt(C))).then_inc(s_exp_ready, 1)

            def read_probsT(k):
                h, t0, t1 = PARTS[k]
                act.wait_ge(probsT_ps_ready, k + 1)
                nc.scalar.activation(probsT[h][:, part_cols(k)], part_turn_ps[k][0:CTX, 0:(t1 - t0) * P],
                                     ACT.Copy).then_inc(probsT_ready, 1)

            def normalise(src, i):
                act.wait_ge(shift_ready, 1)
                for t in range(TILES):
                    nc.scalar.activation(ln_out[i][:, t, :], src[:, t, :], ACT.Identity, bias=ln_shift[:, t:t + 1],
                                         scale=ln_rstd[i][:, t:t + 1]).then_inc(ln_ready[i], 1)

            def xn4_columns(k):
                h, t0, t1 = PARTS[k]
                copy_T(xn4_hi[h][:, part_cols(k)], part_ps[k][:, 0:(t1 - t0) * P], ln1(k, 1), xn4_hi_ready)

            def ff_gelu(h, c):
                act.wait_ge(ff_ps_ready, FF1_CHUNKS * h + c + 1)
                if h and c == 0:
                    act.wait_ge(hid_ready, B * CHUNKS)
                a, _b = PACK["b1"]
                nc.scalar.activation(gelu[h][c][:, :], ff_ps[h][c][:, :], ACT.Gelu,
                                     bias=small[:, a + c:a + c + 1]).then_inc(gelu_ready, 1)

            def finish_last():
                act.wait_ge(ff_done, B * FF1_CHUNKS)
                a, b = PACK["b2"]
                for (h, c0, c1), ready in zip(PIECES[1:], y_ready[1:]):
                    nc.scalar.activation(yT[h][:, c0:c1], y_ps[h][:, c0:c1], ACT.Identity,
                                         bias=small[:, a:b]).then_inc(ready, 1)

            act.dma_start(row_sb[:, :], rows).then_inc(rows_in, 16)
            nc.scalar.preload_act_table_set("natural_log_exp_and_others")
            softplus()
            nc.scalar.preload_act_table_set("silu_and_others")
            w_hi(0)
            for k in (0, 1):
                xn1_columns(k)
            k_squares(k_div, k_sq, k_div_ready, 0, k_sq_ready)
            k_squares(k_cube, k_six, k_cube_ready, 1, k_six_ready)
            for k in (0, 1):
                q_first(k)
            for k in (0, 1):
                q_square(k)
            w_hi(1)
            for k in (0, 1):
                q_sixth(k)
            ctx1_reads()
            w_hi(2)
            w_hi(3)
            w_hi(4)
            xn1_columns(2)
            q_first(2)
            wqk_read()
            q_square(2)
            q_sixth(2)
            w_hi(5)
            for k in (0, 1):
                xn2_whole(k)
            for k in (0, 1):
                xn2_rounded(k)
            keep_att0()
            route_tanh(0)
            for n in range(B * CHUNKS):
                if n == CHUNKS + W2_LAG:
                    read_acc(0)
                silu(n)
                if n < 2:
                    w_hi(n + 6)
                if n == 2:
                    read_spread(0)
                if n == 3:
                    read_spread(1)
                if n == 4:
                    read_spread(2)
                if n % CHUNKS_PER_EXPERT == 0 and n >= 6:
                    read_spread(n // CHUNKS_PER_EXPERT)
                for m in rests(n):
                    hid_round(m)
                if n == 11:
                    xn2_whole(2)
                    xn2_rounded(2)
                if n == 13:
                    route_tanh(1)
                if n == 14:
                    abs_sums()
                if n == 27:
                    xn3_columns(0)
            hid_round(B * CHUNKS - 2)
            hid_round(B * CHUNKS - 1)
            nc.scalar.preload_act_table_set("exp_and_others")
            softmax_exp(0)
            for k in (1, 2):
                read_acc(k)
            read_probsT(0)
            for k in (1, 2):
                xn3_columns(k)
            for k in (1, 2):
                softmax_exp(k)
            for k in (1, 2):
                read_probsT(k)
            normalise(x3[0], ln1(0, 1))
            xn4_columns(0)
            nc.scalar.preload_act_table_set("gelu_and_others")
            ff_gelu(0, 0)
            xn4_columns(1)
            xn4_columns(2)
            for c in range(1, FF1_CHUNKS):
                ff_gelu(0, c)
            for c in range(FF1_CHUNKS):
                ff_gelu(1, c)
            finish_last()

        @block.vector
        def _(dve):
            links = [0]

            def link(ins):
                links[0] += 1
                ins.then_inc(dve_chain, 1)
                dve.wait_ge(dve_chain, links[0])

            def ln_sums(src, i, t0=0, t1=TILES):
                for t in range(t0, t1):
                    last = nc.vector.bn_stats(ln_stats[i][:, t, :], src[:, t, :])
                link(last)

            def ln_var_sum(i, t0=0, t1=TILES):
                for t in range(t0, t1):
                    last = nc.vector.bn_aggr(ln_mv[i][:, t, :], ln_stats[i][:, t, :])
                link(last)
                nc.vector.tensor_scalar(ln_var[i][:, t0:t1], ln_mv[i][:, t0:t1, 1], LN_EPS, None,
                                        ALU.add).then_inc(var_ready, 1)

            def ln_begin(src, i, t0=0, t1=TILES):
                ln_sums(src, i, t0, t1)
                ln_var_sum(i, t0, t1)

            def ln_end(src, i, t0=0, t1=TILES):
                dve.wait_ge(rstd_ready, i + 1)
                for t in range(t0, t1):
                    nc.vector.tensor_scalar(ln_out[i][:, t, :], src[:, t, :], ln_mv[i][:, t, 0:1],
                                            ln_rstd[i][:, t:t + 1], ALU.subtract, ALU.mult).then_inc(ln_ready[i], 1)

            def softplus_end():
                dve.wait_ge(small_in, 16)
                dve.wait_ge(sp_ln_ready, 1)
                a, b = PACK["scale_bq"]
                link(nc.vector.scalar_tensor_tensor(out=sp[:, :], in0=small[:, a:a + 1], scalar=0.0, in1=sp_ln[:, :],
                                                    op0=ALU.max, op1=ALU.add))
                link(nc.vector.reciprocal(inv_sp[:, :], sp[:, :]))
                nc.vector.tensor_scalar(inv_diag[:, :], ident, inv_sp[:, :], None, ALU.mult).then_inc(inv_diag_ready, 1)
                nc.vector.tensor_scalar(eps_inv_sp[:, :], inv_sp[:, :], FOCUS_EPS, None, ALU.mult)
                nc.vector.tensor_tensor(bq_inv_sp[:, :], inv_sp[:, :], small[:, a + 1:b], ALU.mult).then_inc(sp_ready, 1)

            def keys_first():
                dve.wait_ge(kv_ps_ready, 1)
                kv = gate_ps[0][0:CTX, :].rearrange("p (b k c) -> p b k c", b=B, k=2)
                link(nc.vector.tensor_scalar(k_act[:, :, :], kv[:, :, 0, :], 0.0, FOCUS_EPS, ALU.max, ALU.add))
                dve.wait_ge(inv_row_ps_ready, 1)
                nc.vector.tensor_tensor(k_div[:, :, :], k_act[:, :, :],
                                        gate_ps[1][0:CTX, 0:C].unsqueeze(1).broadcast_to([CTX, B, C]),
                                        ALU.mult).then_inc(k_div_ready, 1)
                nc.vector.tensor_copy(v_ones[:, :, 0:C], kv[:, :, 1, :]).then_inc(kv_read, 1)

            def keys_cube():
                dve.wait_ge(k_sq_ready, B)
                nc.vector.tensor_tensor(k_cube[:, :, :], k_sq[:, :, :], k_div[:, :, :], ALU.mult).then_inc(k_cube_ready, 1)

            def keys_ratio():
                dve.wait_ge(k_six_ready, B)
                link(nc.vector.reciprocal(k_rec[:, :], k_sums[:, 1, :]))
                nc.vector.tensor_tensor(k_ratio[:, :], k_sums[:, 0, :], k_rec[:, :], ALU.mult).then_inc(k_ratio_ready, 1)

            def keys_end():
                dve.wait_ge(k_factor_ready, 1)
                for b in range(B):
                    last = nc.vector.tensor_scalar(k_feat[:, b, :], k_cube[:, b, :], k_factor[:, b:b + 1], None, ALU.mult)
                last.then_inc(k_feat_ready, 1)

            def kv_mask():
                dve.wait_ge(kvh_ps_ready, 1)
                dve.wait_ge(rest_in, 16)
                nc.vector.tensor_tensor(kv_heads[:, :, :],
                                        acc_ps[:, 0:B * KV_COLS].rearrange("p (b c) -> p b c", b=B),
                                        packed("kv_mask").unsqueeze(1).broadcast_to([P, B, KV_COLS]),
                                        ALU.mult).then_inc(kvh_ready, 1)

            def select_round():
                nc.vector.tensor_tensor(select[:, :, :],
                                        ident[0:2 * EXPERTS, 0:EXPERTS].unsqueeze(2).broadcast_to([2 * EXPERTS, EXPERTS, P]),
                                        ident[0:2 * EXPERTS, EXPERTS:2 * EXPERTS].unsqueeze(2).broadcast_to([2 * EXPERTS, EXPERTS, P]),
                                        ALU.add).then_inc(select_ready, 1)

            def q_third(k):
                h = PARTS0[k][0]
                dve.wait_ge(q_sq_ready, k + 1)
                nc.vector.scalar_tensor_tensor(out=q_cube[h][:, cols0(k)], in0=q_relu[h][:, cols0(k)],
                                               scalar=eps_inv_sp[:, :], in1=q_sq[h][:, cols0(k)],
                                               op0=ALU.add, op1=ALU.mult).then_inc(q_cube_ready, 1)

            def att0_begin(k):
                h, t0, t1 = PARTS0[k]
                n = t1 - t0
                dve.wait_ge(q_sums_ready, k + 1)
                if h:
                    dve.wait_ge(att0_kept, 2)
                link(nc.vector.reciprocal(q_rec[h][:, t0:t1], att0_in[k][0][:, 0:n]))
                nc.vector.tensor_tensor(q_ratio[h][:, t0:t1], att0_in[k][0][:, TILES:TILES + n], q_rec[h][:, t0:t1],
                                        ALU.mult).then_inc(q_ratio_ready, 1)

            def att0_norm(k):
                h, t0, t1 = PARTS0[k]
                dve.wait_ge(q_inv_ready, k + 1)
                dve.wait_ge(att0_ps_ready, k + 1)
                link(nc.vector.tensor_scalar(q_inv_eps[h][:, t0:t1], q_inv[h][:, t0:t1], FOCUS_EPS, None, ALU.mult))
                for t, ps in att0_pairs(k):
                    last = nc.vector.tensor_tensor(den[h][:, t:t + 2, :],
                                                   ps.rearrange("p (t c) -> p t c", t=2)[:, :, C:KV_COLS],
                                                   q_inv_eps[h][:, t:t + 2].unsqueeze(2).broadcast_to([P, 2, HEADS]),
                                                   ALU.add)
                link(last)
                link(nc.vector.reciprocal(inv_den[h][:, t0:t1, :], den[h][:, t0:t1, :]))

            def att0_end(k):
                h, t0, t1 = PARTS0[k]
                for t, ps in att0_pairs(k):
                    last = nc.vector.tensor_tensor(
                        att0[h][:, t:t + 2, :].rearrange("p t (g d) -> p t g d", g=HEADS),
                        ps.rearrange("p (t c) -> p t c", t=2)[:, :, 0:C].rearrange("p t (g d) -> p t g d", g=HEADS),
                        inv_den[h][:, t:t + 2, :].unsqueeze(3).broadcast_to([P, 2, HEADS, HEAD_DIM]),
                        ALU.mult)
                last.then_inc(att0_read, 1)
                dve.wait_ge(att0_read, k + 1)
                link(nc.vector.tensor_tensor(x1[h][:, t0:t1, :], x_in[h][:, t0:t1, :], att0[h][:, t0:t1, :], ALU.add))

            def xn2_rest(h):
                dve.wait_ge(xn2T_ready, h + 2)
                dve.wait_ge(xn2_hi_ready, h + 2)
                nc.vector.tensor_tensor(xn2_lo[h][:, :], xn2T[:, :], xn2_hi[h][:, :].bitcast(f32),
                                        ALU.subtract).then_inc(xn2_lo_ready, 1)

            def route_top(h):
                dve.wait_ge(logits_ready, h + 1)
                lg = logits_ps[h][:, 0:TILES * EXPERTS].rearrange("p (t e) -> p t e", t=TILES)
                for t in range(TILES):
                    last = nc.vector.max(top8[h][:, t, :], lg[:, t, :])
                link(last)
                nc.vector.tensor_tensor(gap[h][:, :], top8[h][:, :, 0], top8[h][:, :, 1], ALU.subtract).then_inc(gap_ready, 1)
                for t in range(TILES):
                    last = nc.vector.max_index(top8_at[h][:, t, :], top8[h][:, t, :], lg[:, t, :])
                last.then_inc(logits_read, 1)

            def route_weights(h):
                dve.wait_ge(gap_tanh_ready, h + 1)
                dve.wait_ge(logits_read, h + 1)
                nc.vector.tensor_scalar(top_w[h][:, 0, :], gap_tanh[h][:, :], 0.5, 0.5, ALU.mult, ALU.add)
                nc.vector.tensor_scalar(top_w[h][:, 1, :], gap_tanh[h][:, :], -0.5, 0.5, ALU.mult, ALU.add)
                for k in range(2):
                    last = nc.vector.tensor_tensor(pick[h][:, k, :, :],
                                                   packed("iota").unsqueeze(1).broadcast_to([P, TILES, EXPERTS]),
                                                   top8_at[h][:, :, k:k + 1].broadcast_to([P, TILES, EXPERTS]),
                                                   ALU.is_equal)
                link(last)
                for k in range(2):
                    last = nc.vector.tensor_tensor(pick_w[h][:, k, :, :], pick[h][:, k, :, :],
                                                   top_w[h][:, k, :].unsqueeze(2).broadcast_to([P, TILES, EXPERTS]),
                                                   ALU.mult)
                link(last)
                link(nc.vector.tensor_tensor(route[h][:, :, :], pick_w[h][:, 0, :, :], pick_w[h][:, 1, :, :], ALU.add))
                link(nc.vector.tensor_copy(route_hl[h][:, :, 0:EXPERTS], route[h][:, :, :]))
                nc.vector.tensor_tensor(route_hl[h][:, :, EXPERTS:2 * EXPERTS], route[h][:, :, :],
                                        route_hl[h][:, :, 0:EXPERTS].bitcast(f32), ALU.subtract).then_inc(route_ready, 1)

            def route_T(h):
                dve.wait_ge(routeT_ps_ready, h + 1)
                nc.vector.tensor_copy(routeT[h][:, :], side1[0:2 * EXPERTS, :]).then_inc(routeT_ready, 1)

            def hidden(n):
                dve.wait_ge(val_ready, n + 1)
                dve.wait_ge(silu_ready, n + 1)
                if n >= SW:
                    dve.wait_ge(hid_ready, n - SW + 1)
                nc.vector.tensor_tensor(gated[n % SW][:, :], val_ps[n % 2][:, :], silu_g[n % SG][:, :],
                                        ALU.mult).then_inc(gated_ready, 1)

            def weigh_last(n):
                dve.wait_ge(gated_ready, n + 1)
                dve.wait_ge(route_b_ready, n // CHUNKS_PER_EXPERT + 1)
                dve.wait_ge(hid_ready, n)
                dve.wait_ge(hid_lo_ready, n - AB + 1)
                nc.vector.tensor_tensor(hid[n % AB][:, :], gated[n % SW][:, :],
                                        route_b[(n // CHUNKS_PER_EXPERT) % 2][:, :],
                                        ALU.mult).then_inc(hid_ready, 1)

            def hidden_rest(n):
                dve.wait_ge(hid_hi_ready, n + 1)
                if n >= HL:
                    dve.wait_ge(w2_done, n - HL + 1)
                nc.vector.tensor_tensor(hid_lo[n % HL][:, :], hid[n % AB][:, :], hid_hi[n % HL][:, :].bitcast(f32),
                                        ALU.subtract).then_inc(hid_lo_ready, 1)

            def thresholds():
                dve.wait_ge(abs_ps_ready, 1)
                link(nc.vector.tensor_scalar(t_scale[:, :], side0[:, 0:2], 1.0 / (FF1 * C), 1e-8, ALU.mult, ALU.max))
                nc.vector.tensor_scalar(t_hi[:, :], t_scale[:, :], 0.5, None, ALU.mult)
                link(nc.vector.tensor_scalar(t_lo[:, :], t_scale[:, :], -0.5, None, ALU.mult))

            def ternary(i):
                if i:
                    dve.wait_ge(tern_ready, i)
                link(nc.vector.tensor_scalar(below[:, :], tw_raw[:, i, :], t_lo[:, i:i + 1], None, ALU.is_lt))
                nc.vector.scalar_tensor_tensor(out=tern[:, i, :], in0=tw_raw[:, i, :], scalar=t_hi[:, i:i + 1],
                                               in1=below[:, :], op0=ALU.is_gt, op1=ALU.subtract).then_inc(tern_ready, 1)

            def add_moe(k):
                h, t0, t1 = PARTS[k]
                dve.wait_ge(moe_ps_ready, k + 1)
                nc.vector.tensor_tensor(x2[h][:, t0:t1, :],
                                        part_ps[k][:, 0:(t1 - t0) * P].rearrange("p (t c) -> p t c", t=t1 - t0),
                                        x1[h][:, t0:t1, :], ALU.add).then_inc(x2_ready, 1)

            def x2_sums(k):
                h, t0, t1 = PARTS[k]
                dve.wait_ge(x2_ready, k + 1)
                ln_sums(x2[h], ln1(k, 0), t0, t1)

            def softmax_shift(k):
                h, t0, t1 = PARTS[k]
                dve.wait_ge(score_ps_ready, k + 1)
                sc = part_ps[k][:, 0:(t1 - t0) * CTX].rearrange("p (t k) -> p t k", t=t1 - t0)
                link(nc.vector.tensor_reduce(s_max[h][:, t0:t1], sc, AX.X, ALU.max))
                nc.vector.tensor_tensor(s_shift[h][:, t0:t1, :], sc,
                                        s_max[h][:, t0:t1].unsqueeze(2).broadcast_to([P, t1 - t0, CTX]),
                                        ALU.subtract).then_inc(s_shift_ready, 1)

            def softmax_sum(k):
                h, t0, t1 = PARTS[k]
                dve.wait_ge(s_exp_ready, k + 1)
                link(nc.vector.tensor_reduce(s_sum[h][:, t0:t1], s_exp[h][:, t0:t1, :], AX.X, ALU.add))
                link(nc.vector.reciprocal(s_inv[h][:, t0:t1], s_sum[h][:, t0:t1]))

            def add_att1(k):
                h, t0, t1 = PARTS[k]
                dve.wait_ge(att1_ps_ready, k + 1)
                for t in range(t0, t1):
                    nc.vector.scalar_tensor_tensor(out=x3[h][:, t, :], in0=part_ps[k][:, (t - t0) * P:(t - t0 + 1) * P],
                                                   scalar=s_inv[h][:, t:t + 1], in1=x2[h][:, t, :],
                                                   op0=ALU.mult, op1=ALU.add).then_inc(x3_ready, 1)
                dve.wait_ge(x3_ready, TILES * h + t1)

            def xn4_rest(k):
                h, t0, t1 = PARTS[k]
                dve.wait_ge(xn4_hi_ready, k + 1)
                nc.vector.tensor_tensor(xn4_lo[h][:, part_cols(k)], part_ps[k][:, 0:(t1 - t0) * P],
                                        xn4_hi[h][:, part_cols(k)].bitcast(f32), ALU.subtract).then_inc(xn4_lo_ready, 1)

            def ln_shift_out(i):
                dve.wait_ge(rstd_ready, i + 1)
                nc.vector.scalar_tensor_tensor(out=ln_shift[:, :], in0=ln_mv[i][:, :, 0], scalar=-1.0,
                                               in1=ln_rstd[i][:, :], op0=ALU.mult, op1=ALU.mult).then_inc(shift_ready, 1)

            def ff_rest(h, c):
                dve.wait_ge(gelu_hi_ready, FF1_CHUNKS * h + c + 1)
                nc.vector.tensor_tensor(gelu_lo[h][c][:, :], gelu[h][c][:, :], gelu_hi[h][c][:, :].bitcast(f32),
                                        ALU.subtract).then_inc(gelu_lo_ready, 1)

            def finish_first():
                dve.wait_ge(ff_done, FF1_CHUNKS)
                a, b = PACK["b2"]
                nc.vector.tensor_scalar(yT[0][:, :], y_ps[0][:, :], small[:, a:b], None, ALU.add).then_inc(y_ready[0], 1)

            dve.wait_ge(x_loaded[0], 16)
            for k in (0, 1):
                ln_begin(x_in[0], ln0(k, 0), *PARTS0[k][1:])
            softplus_end()
            for k in (0, 1):
                ln_end(x_in[0], ln0(k, 0), *PARTS0[k][1:])
            keys_first()
            keys_cube()
            dve.wait_ge(x_loaded[1], 16)
            ln_sums(x_in[1], ln0(2, 0))
            keys_ratio()
            ln_var_sum(ln0(2, 0))
            keys_end()
            for k in (0, 1):
                q_third(k)
            kv_mask()
            for k in (0, 1):
                att0_begin(k)
            ln_end(x_in[1], ln0(2, 0))
            for k in (0, 1):
                att0_norm(k)
                att0_end(k)
                ln_begin(x1[0], ln0(k, 1), *PARTS0[k][1:])
            q_third(2)
            for k in (0, 1):
                ln_end(x1[0], ln0(k, 1), *PARTS0[k][1:])
            select_round()
            xn2_rest(0)
            route_top(0)
            route_weights(0)
            for n in range(B * CHUNKS):
                hidden(n)
                if n == 0:
                    route_T(0)
                for m in rests(n):
                    hidden_rest(m)
                if n == 3:
                    att0_begin(2)
                if n == 5:
                    att0_norm(2)
                if n == 6:
                    att0_end(2)
                if n == 7:
                    ln_sums(x1[1], ln0(2, 1))
                if n == 8:
                    ln_var_sum(ln0(2, 1))
                if n == 10:
                    ln_end(x1[1], ln0(2, 1))
                if n == 12:
                    xn2_rest(1)
                if n == 12:
                    route_top(1)
                if n == 13:
                    route_weights(1)
                if n == 14:
                    route_T(1)
                if n == 17:
                    thresholds()
                if n == 19:
                    ternary(0)
                if n == 20:
                    ternary(1)
                if n == 21:
                    add_moe(0)
                if n == 22:
                    x2_sums(0)
                if n == 23:
                    ln_var_sum(ln1(0, 0))
                if n == 24:
                    ln_end(x2[0], ln1(0, 0))
                if n == 29:
                    softmax_shift(0)
            weigh_last(B * CHUNKS - 1)
            hidden_rest(B * CHUNKS - 2)
            hidden_rest(B * CHUNKS - 1)
            softmax_sum(0)
            A, Z = 1, 2
            (A0, A1), (Z0, Z1) = PARTS[A][1:], PARTS[Z][1:]
            add_moe(A)
            add_moe(Z)
            x2_sums(A)
            ln_var_sum(ln1(A, 0), A0, A1)
            x2_sums(Z)
            ln_var_sum(ln1(Z, 0), Z0, Z1)
            ln_end(x2[1], ln1(A, 0), A0, A1)
            ln_end(x2[1], ln1(Z, 0), Z0, Z1)
            add_att1(0)
            softmax_shift(A)
            softmax_shift(Z)
            ln_begin(x3[0], ln1(0, 1))
            softmax_sum(A)
            softmax_sum(Z)
            ln_shift_out(ln1(0, 1))
            add_att1(A)
            ln_begin(x3[1], ln1(A, 1), A0, A1)
            add_att1(Z)
            ln_begin(x3[1], ln1(Z, 1), Z0, Z1)
            xn4_rest(0)
            ln_end(x3[1], ln1(A, 1), A0, A1)
            ln_end(x3[1], ln1(Z, 1), Z0, Z1)
            xn4_rest(A)
            xn4_rest(Z)
            for c in range(FF1_CHUNKS):
                ff_rest(0, c)
            ff_rest(1, 0)
            ff_rest(1, 1)
            ff_rest(1, 2)
            ff_rest(1, 3)
            finish_first()

        @block.tensor
        def _(pe):
            def ln_T(dst, i, t0=0, t1=TILES):
                for t in range(t0, t1):
                    pe.wait_ge(ln_ready[i], t - t0 + 1)
                    last = nc.tensor.transpose(dst[:, (t - t0) * P:(t - t0 + 1) * P], ln_out[i][:, t, :], ident)
                last.then_inc(lnT_ps_ready, 1)

            def keep_warm(ps, passes):
                for _ in range(passes):
                    nc.tensor.matmul(ps[:, 0:P], ones[:, :], ones[:, :], start=True, stop=True)

            def bias_rows():
                pe.wait_ge(rows_in, 16)
                nc.tensor.matmul(gate_ps[0][0:CTX, :], ones[0:1, 0:CTX], row_sb[:, :], start=True, stop=False)

            def inverse_row():
                pe.wait_ge(inv_diag_ready, 1)
                nc.tensor.matmul(gate_ps[1][0:CTX, 0:C], ones[:, 0:CTX], inv_diag[:, :],
                                 start=True, stop=True).then_inc(inv_row_ps_ready, 1)

            def ctx0_keys_values():
                a, b = PACK["Wkv0"]
                pe.wait_ge(small_in, 16)
                for i in range(B):
                    last = nc.tensor.matmul(gate_ps[0][0:CTX, i * 2 * C:(i + 1) * 2 * C], ctxT[:, i * CTX:(i + 1) * CTX],
                                            small[:, a:b], start=False, stop=(i == B - 1))
                last.then_inc(kv_ps_ready, 1)

            def ctx1_keys_values():
                a, _b = PACK["Wkv1"]
                pe.wait_ge(rest_in, 16)
                nc.tensor.matmul(val_ps[0][:, 0:B * CTX], small[:, a:a + C], ctxT, start=True, stop=True).then_inc(k1T_ps_ready, 1)
                for i in range(B):
                    last = nc.tensor.matmul(val_ps[1][0:CTX, i * C:(i + 1) * C], ctxT[:, i * CTX:(i + 1) * CTX],
                                            small[:, a + C:a + 2 * C], start=True, stop=True)
                last.then_inc(v1_ps_ready, 1)

            def ctx1_wq_keys():
                pe.wait_ge(k1T_ready, 1)
                nc.tensor.matmul(val_ps[0][:, 0:B * CTX], packed("Wq1T"), k1T[:, :], start=True, stop=True).then_inc(wqk_ps_ready, 1)

            def head_sums():
                pe.wait_ge(k_feat_ready, 1)
                pe.wait_ge(kv_read, 1)
                pe.wait_ge(v_ones_set, 1)
                for i in range(B):
                    last = nc.tensor.matmul(acc_ps[:, i * KV_COLS:(i + 1) * KV_COLS], k_feat[:, i, :], v_ones[:, i, :],
                                            start=True, stop=True)
                last.then_inc(kvh_ps_ready, 1)

            def q_project(k):
                h, t0, t1 = PARTS0[k]
                pe.wait_ge(xn1T_ready, k + 1)
                if h:
                    pe.wait_ge(k_div_ready, 1)
                nc.tensor.matmul(q_ps[k][:, 0:(t1 - t0) * P], packed("Wq0"), xn1T[h][:, cols0(k)],
                                 start=True, stop=True).then_inc(q_ps_ready, 1)

            def sum_squares(k):
                h, t0, t1 = PARTS0[k]
                pe.wait_ge(q_sq_ready, k + 1)
                if h:
                    pe.wait_ge(kvh_ready, 1)
                for t in range(t0, t1):
                    nc.tensor.matmul(att0_ps[k][0][:, t - t0:t - t0 + 1], q_sq[h][:, t * P:(t + 1) * P], ones[:, 0:1],
                                     start=True, stop=True)

            def sum_sixths(k):
                h, t0, t1 = PARTS0[k]
                pe.wait_ge(q_six_ready, k + 1)
                for t in range(t0, t1):
                    last = nc.tensor.matmul(att0_ps[k][0][:, TILES + t - t0:TILES + t - t0 + 1],
                                            q_six[h][:, t * P:(t + 1) * P], ones[:, 0:1], start=True, stop=True)
                last.then_inc(q_sums_ready, 1)

            def att0_products(k):
                h, t0, t1 = PARTS0[k]
                pe.wait_ge(kvh_ready, 1)
                pe.wait_ge(q_cube_ready, k + 1)
                if h:
                    pe.wait_ge(xn1T_ready, k + 1)
                else:
                    pe.wait_ge(q_ratio_ready, k + 1)
                for t in range(t0, t1):
                    second, i = divmod(t - t0, 2)
                    at = (0 if second else P) + i * KV_COLS
                    last = nc.tensor.matmul(att0_ps[k][second][:, at:at + KV_COLS], q_cube[h][:, t * P:(t + 1) * P],
                                            kv_heads[:, h, :], start=True, stop=True)
                last.then_inc(att0_ps_ready, 1)

            def router(h):
                pe.wait_ge(xn2T_ready, h + 2)
                if h == 0:
                    pe.wait_ge(q_relu_ready, 3)
                else:
                    pe.wait_ge(routeT_ready, 1)
                for t in range(TILES):
                    last = nc.tensor.matmul(logits_ps[h][:, t * EXPERTS:(t + 1) * EXPERTS], xn2T[:, t * P:(t + 1) * P],
                                            packed("WrT"), start=True, stop=True)
                last.then_inc(logits_ready, 1)

            def route_turn(h):
                pe.wait_ge(route_ready, h + 1)
                pe.wait_ge(logits_read, h + 1)
                pe.wait_ge(xn2_hi_ready, h + 2)
                for t in range(TILES):
                    last = nc.tensor.transpose(side1[0:2 * EXPERTS, t * P:(t + 1) * P],
                                               route_hl[h][:, t, :].bitcast(f32), ident)
                last.then_inc(routeT_ps_ready, 1)

            def spread(g):
                h, e = divmod(g, EXPERTS)
                pe.wait_ge(routeT_ready, h + 1)
                pe.wait_ge(select_ready, 1)
                if g:
                    pe.wait_ge(route_b_ready, g)
                else:
                    pe.wait_ge(att0_kept, 2)
                nc.tensor.matmul(spread_ps[:, :], select[:, e, :], routeT[h][:, :], start=True, stop=True).then_inc(spread_ready, 1)

            def up(n, h, e):
                c = n % CHUNKS_PER_EXPERT
                gate, val = gate_ps[n % 2][:, :], val_ps[n % 2][:, :]
                for ps, col, done in ((gate, FFN + c * P, gate_ready), (val, c * P, val_ready)):
                    hi, lo = w1_hi[:, e, col:col + P], w1_lo[:, e, col:col + P]
                    if ps is val and n >= 2:
                        pe.wait_ge(gated_ready, n - 1)
                    nc.tensor.matmul(ps, lo, xn2_hi[h][:, :], start=True, stop=False)
                    nc.tensor.matmul(ps, hi, xn2_hi[h][:, :], start=False, stop=False)
                    pe.wait_ge(xn2_lo_ready, h + 1)
                    nc.tensor.matmul(ps, hi, xn2_lo[h][:, :], start=False, stop=True).then_inc(done, 1)

            def chunk_up(n):
                h, j = divmod(n, CHUNKS)
                e, c = divmod(j, CHUNKS_PER_EXPERT)
                pe.wait_ge(xn2_hi_ready, h + 2)
                if h == 0:
                    pe.wait_ge(w_lo_ready, 2 * e + 2)
                if n == 0:
                    pe.wait_ge(kv_read, 1)
                    pe.wait_ge(wqk_ready, 1)
                if n == 1:
                    pe.wait_ge(logits_read, 1)
                    pe.wait_ge(v1_ready, 1)
                if n >= 2:
                    pe.wait_ge(silu_ready, n - 1)
                up(n, h, e)

            def downs(n):
                if n == CATCH_UP:
                    return [n - W2_LAG - 1, n - W2_LAG]
                lag = W2_LAG + 1 if n < CATCH_UP else W2_LAG
                return [n - lag] if n >= lag else []

            def chunk_down(m):
                h, j = divmod(m, CHUNKS)
                e, c = divmod(j, CHUNKS_PER_EXPERT)
                if m == 0:
                    pe.wait_ge(att0_kept, 2)
                if j == 0 and h:
                    pe.wait_ge(moeT_ready, h)
                pe.wait_ge(hid_lo_ready, m + 1)
                hi, lo = hid_hi[m % HL][:, :], hid_lo[m % HL][:, :]
                nc.tensor.matmul(acc_ps[:, :], w2_lo[:, e, c, :], hi, start=(j == 0), stop=False)
                nc.tensor.matmul(acc_ps[:, :], w2_hi[:, e, c, :], lo, start=False, stop=False)
                nc.tensor.matmul(acc_ps[:, :], w2_hi[:, e, c, :], hi, start=False, stop=(j == CHUNKS - 1)).then_inc(w2_done, 1)

            def ternary_sum():
                pe.wait_ge(abs_ready, 2)
                pe.wait_ge(xn2_hi_ready, 3)
                nc.tensor.matmul(side0[:, 0:2], ones[:, :], abs_sum[:, :], start=True, stop=True).then_inc(abs_ps_ready, 1)

            def moe_turn(k):
                h, t0, t1 = PARTS[k]
                pe.wait_ge(moeT_ready, k + 1)
                if k == 0:
                    pe.wait_ge(tern_ready, 1)
                else:
                    pe.wait_ge(gated_ready, B * CHUNKS)
                for t in range(t0, t1):
                    last = nc.tensor.transpose(part_ps[k][:, (t - t0) * P:(t - t0 + 1) * P], moeT[h][:, t * P:(t + 1) * P], ident)
                last.then_inc(moe_ps_ready, 1)

            def scores(k):
                h, t0, t1 = PARTS[k]
                pe.wait_ge(xn3T_ready, k + 1)
                pe.wait_ge(x2_ready, k + 1)
                pe.wait_ge(wqk_ready, 1)
                for t in range(t0, t1):
                    last = nc.tensor.matmul(part_ps[k][:, (t - t0) * CTX:(t - t0 + 1) * CTX], xn3T[h][:, t * P:(t + 1) * P],
                                            wq_k1T[:, h * CTX:(h + 1) * CTX], start=True, stop=True)
                last.then_inc(score_ps_ready, 1)

            def probs_turn(k):
                h, t0, t1 = PARTS[k]
                pe.wait_ge(s_exp_ready, k + 1)
                for t in range(t0, t1):
                    last = nc.tensor.transpose(part_turn_ps[k][0:CTX, (t - t0) * P:(t - t0 + 1) * P], s_exp[h][:, t, :], ident)
                last.then_inc(probsT_ps_ready, 1)

            def att1_products(k):
                h, t0, t1 = PARTS[k]
                pe.wait_ge(probsT_ready, k + 1)
                for t in range(t0, t1):
                    last = nc.tensor.matmul(part_ps[k][:, (t - t0) * C:(t - t0 + 1) * C], probsT[h][:, t * P:(t + 1) * P],
                                            v1[:, h, :], start=True, stop=True)
                last.then_inc(att1_ps_ready, 1)

            def residual_T(h):
                pe.wait_ge(x3_ready, TILES * (h + 1))
                if h == 0:
                    pe.wait_ge(route_b_ready, B * EXPERTS)
                else:
                    pe.wait_ge(xn4_lo_ready, 1)
                for t in range(TILES):
                    nc.tensor.matmul(y_ps[h][:, t * P:(t + 1) * P], x3[h][:, t, :], ident, start=(t == 0), stop=False,
                                     skip_group_check=True)

            def ff_up_hi():
                pe.wait_ge(xn4_hi_ready, 1)
                pe.wait_ge(tern_ready, 2)
                pe.wait_ge(silu_ready, B * CHUNKS)
                pe.wait_ge(moeT_ready, len(PARTS))
                pe.wait_ge(probsT_ready, 1)
                for c in range(FF1_CHUNKS):
                    nc.tensor.matmul(ff_ps[0][c][:, :], tern[:, 0, c * P:(c + 1) * P], xn4_hi[0][:, :],
                                     start=True, stop=False)

            def ff_up_lo():
                pe.wait_ge(xn4_lo_ready, 1)
                for c in range(FF1_CHUNKS):
                    nc.tensor.matmul(ff_ps[0][c][:, :], tern[:, 0, c * P:(c + 1) * P], xn4_lo[0][:, :],
                                     start=False, stop=True).then_inc(ff_ps_ready, 1)

            def ff_up_last():
                pe.wait_ge(xn4_lo_ready, len(PARTS))
                for c in range(FF1_CHUNKS):
                    if c >= 2:
                        pe.wait_ge(gelu_ready, c - 1)
                    w = tern[:, 0, c * P:(c + 1) * P]
                    nc.tensor.matmul(ff_ps[1][c][:, :], w, xn4_hi[1][:, :], start=True, stop=False)
                    nc.tensor.matmul(ff_ps[1][c][:, :], w, xn4_lo[1][:, :], start=False, stop=True).then_inc(ff_ps_ready, 1)

            def ff_down(h, c):
                pe.wait_ge(gelu_lo_ready, FF1_CHUNKS * h + c + 1)
                w = tern[:, 1, c * P:(c + 1) * P]
                nc.tensor.matmul(y_ps[h][:, :], w, gelu_lo[h][c][:, :], start=False, stop=False, skip_group_check=True)
                nc.tensor.matmul(y_ps[h][:, :], w, gelu_hi[h][c][:, :], start=False, stop=(c == FF1_CHUNKS - 1),
                                 skip_group_check=True).then_inc(ff_done, 1)

            pe.wait_ge(ones_set, 1)
            keep_warm(acc_ps, WARM[0])
            bias_rows()
            ctx0_keys_values()
            inverse_row()
            for k in (0, 1):
                ln_T(xn1T_ps[k], ln0(k, 0), *PARTS0[k][1:])
            keep_warm(acc_ps, WARM[1])
            for k in (0, 1):
                q_project(k)
            ctx1_keys_values()
            keep_warm(spread_ps, WARM[2])
            head_sums()
            for k in (0, 1):
                sum_squares(k)
            for k in (0, 1):
                sum_sixths(k)
            for k in (0, 1):
                att0_products(k)
            ln_T(spread_ps, ln0(2, 0))
            pe.wait_ge(v1_ready, 1)
            keep_warm(val_ps[1], WARM[3])
            q_project(2)
            ctx1_wq_keys()
            keep_warm(val_ps[1], WARM[4])
            sum_squares(2)
            att0_products(2)
            for k in (0, 1):
                pe.wait_ge(att0_read, k + 1)
                ln_T(xn2T_ps[k], ln0(k, 1), *PARTS0[k][1:])
            sum_sixths(2)
            keep_warm(val_ps[1], WARM[5])
            router(0)
            for n in range(B * CHUNKS):
                chunk_up(n)
                if n == 1:
                    route_turn(0)
                if n == 2:
                    spread(0)
                if n == 3:
                    spread(1)
                if n == 4:
                    spread(2)
                if n % CHUNKS_PER_EXPERT == 1 and 5 <= n < B * CHUNKS - 1:
                    spread(n // CHUNKS_PER_EXPERT + 1)
                for m in downs(n):
                    chunk_down(m)
                if n == 11:
                    pe.wait_ge(xn2_hi_ready, 2)
                    ln_T(side0, ln0(2, 1))
                if n == 12:
                    router(1)
                if n == 14:
                    route_turn(1)
                if n == 16:
                    ternary_sum()
                if n == 20:
                    moe_turn(0)
                if n == 26:
                    pe.wait_ge(routeT_ready, 2)
                    ln_T(side1, ln1(0, 0))
                if n == 28:
                    scores(0)
            chunk_down(B * CHUNKS - 3)
            chunk_down(B * CHUNKS - 2)
            chunk_down(B * CHUNKS - 1)
            probs_turn(0)
            for k in (1, 2):
                moe_turn(k)
            att1_products(0)
            pe.wait_ge(silu_ready, B * CHUNKS)
            keep_warm(gate_ps[0], TAIL_WARM[0])
            for k in (1, 2):
                ln_T(part_turn_ps[k], ln1(k, 0), *PARTS[k][1:])
            for k in (1, 2):
                scores(k)
            residual_T(0)
            keep_warm(gate_ps[0], TAIL_WARM[1])
            for k in (1, 2):
                probs_turn(k)
            keep_warm(gate_ps[0], TAIL_WARM[2])
            for k in (1, 2):
                att1_products(k)
            keep_warm(gate_ps[0], TAIL_WARM[3])
            ln_T(side0, ln1(0, 1))
            keep_warm(gate_ps[0], TAIL_WARM[4])
            ff_up_hi()
            ff_up_lo()
            for k in (1, 2):
                ln_T(part_ps[k], ln1(k, 1), *PARTS[k][1:])
            residual_T(1)
            ff_up_last()
            for h in range(B):
                for c in range(FF1_CHUNKS):
                    ff_down(h, c)


def kernel(x, ctx_1024, L0_xattn_Wq, L0_xattn_bq, L0_xattn_Wk, L0_xattn_bk, L0_xattn_Wv, L0_xattn_bv,
           L0_xattn_scale, L0_ffn_Wr, L0_ffn_W1, L0_ffn_W2, L1_xattn_Wq, L1_xattn_Wkv, L1_ffn_W1,
           L1_ffn_b1, L1_ffn_W2, L1_ffn_b2):
    import concourse.bacc as bacc
    from concourse.bass_utils import run_bass_kernel_spmd

    f = np.float32
    a = [np.asarray(v) for v in (ctx_1024, L0_xattn_Wq, L0_xattn_bq, L0_xattn_Wk, L0_xattn_bk, L0_xattn_Wv,
                                 L0_xattn_bv, L0_xattn_scale, L0_ffn_Wr, L0_ffn_W1, L0_ffn_W2, L1_xattn_Wq,
                                 L1_xattn_Wkv, L1_ffn_W1, L1_ffn_b1, L1_ffn_W2, L1_ffn_b2)]
    ctx_, wq0, bq, wk0, bk, wv0, bv, scale, wr, w1, w2, wq1, wkv1, tw1, b1, tw2, b2 = a
    head = np.arange(C) // HEAD_DIM
    kv_mask = np.concatenate([head[:, None] == head[None, :], head[:, None] == np.arange(HEADS)[None, :]], 1).astype(f)
    iota = np.tile(np.arange(EXPERTS, dtype=f), (P, 1))
    parts = {
        "ctxT": ctx_.reshape(B * CTX, C).T, "Wkv0": np.concatenate([wk0, wv0], 1), "Wq0": wq0,
        "scale_bq": np.stack([scale.reshape(C), bq], 1), "ident": np.eye(C, dtype=f), "Wkv1": wkv1, "Wq1T": wq1.T,
        "WrT": wr.T, "b1": b1.reshape(FF1_CHUNKS, P).T, "b2": b2.reshape(C, 1), "kv_mask": kv_mask, "iota": iota,
    }
    arrays = {
        "x": np.ascontiguousarray(np.asarray(x)),
        "pack": np.ascontiguousarray(np.concatenate([parts[k] for k in PACK], 1)),
        "rows": np.concatenate([bk, bv, bk, bv]).reshape(1, ROW_COLS),
        "w1": np.ascontiguousarray(w1.transpose(2, 0, 1)),
        "w2": np.ascontiguousarray(w2.reshape(EXPERTS, C, CHUNKS_PER_EXPERT, P).transpose(3, 0, 2, 1)),
        "ternary_w": np.ascontiguousarray(np.stack([tw1.T, tw2.reshape(C, FF1_CHUNKS, P).transpose(2, 1, 0).reshape(P, FF1)], 1)),
    }
    nc = bacc.Bacc("TRN2", target_bir_lowering=False, num_devices=1)
    args = [nc.dram_tensor(n, v.shape, mybir.dt.from_np(v.dtype), kind="ExternalInput").ap() for n, v in arrays.items()]
    out = nc.dram_tensor("out", (P, B, N_TOK), mybir.dt.float32, kind="ExternalOutput").ap()
    build(nc, *args, out)
    r = run_bass_kernel_spmd(nc, [arrays], core_ids=[0])
    got = np.asarray(r.results[0]["out"])
    return np.ascontiguousarray(got.reshape(C, B, TILES, P).transpose(1, 3, 2, 0).reshape(B, N_TOK, C))
```
